# Optimizing a Trainium2 kernel written in Bass

```python
import numpy as np
import jax
import jax.numpy as jnp

def _softmax(x, axis=-1):
    return jax.nn.softmax(x, axis=axis)

def _gelu(x):
    return jax.nn.gelu(x, approximate=True)

def _silu(x):
    return jax.nn.silu(x)

def _sigmoid(x):
    return jax.nn.sigmoid(x)

def _layernorm(x, axis=-1, eps=1e-05):
    m = jnp.mean(x, axis=axis, keepdims=True)
    v = jnp.var(x, axis=axis, keepdims=True)
    return (x - m) / jnp.sqrt(v + eps)

def _scatter_add(tgt, idx, src, axis=0):
    return tgt.at[idx].add(src)

def _segment_sum(src, seg, n):
    return jax.ops.segment_sum(src, seg, n)
kernel_name = 'mk_adj_ffn_d4_adj_r2_86d389'

def setup_inputs(seed: int=0):
    np.random.seed(seed)
    _w = jnp.asarray

    def _rec_inputs():
        import jax
        import jax.numpy as jnp
        _gk = jax.random.key(seed)
        x = -0.0002928 + 1 * jax.random.normal(jax.random.fold_in(_gk, 1), (16, 512, 128), jnp.float32)
        _a = jax.random.bernoulli(jax.random.fold_in(_gk, 2), 0.03125, (16, 512, 512))
        _af = _a.astype(jnp.float32)
        adj = _af
        return (x, adj)
    x, adj = _rec_inputs()

    def _L0_gnn_setup():
        import jax, jax.numpy as jnp
        import numpy as np
        B, N, D_IN, D_OUT = (16, 512, 128, 128)
        NEG_INF = -9000000000000000.0
        LRELU_SLOPE = 0.2
        key = jax.random.key(seed)
        k1, k2, k3, k4 = jax.random.split(key, 4)
        x = jax.random.normal(k1, (B, N, D_IN), dtype=jnp.float32)
        adj_matrix = jax.random.randint(k2, (B, N, N), 0, 2).astype(jnp.float32)
        w_lim = float(np.sqrt(6.0 / (D_IN + D_OUT)))
        a_lim = float(np.sqrt(6.0 / (2 * D_OUT + 1)))
        W = jax.random.uniform(k3, (D_IN, D_OUT), minval=-w_lim, maxval=w_lim, dtype=jnp.float32)
        a = jax.random.uniform(k4, (2 * D_OUT, 1), minval=-a_lim, maxval=a_lim, dtype=jnp.float32)
        return {'x': x, 'adj_matrix': adj_matrix, 'W': W, 'a': a}
    _L0_gnn_all = _L0_gnn_setup()
    _L0_gnn_in = {k: v for k, v in _L0_gnn_all.items() if k in ('W', 'a')}
    del _L0_gnn_all

    def _L0_ffn_setup():
        import jax, jax.numpy as jnp
        import numpy as np
        D_MODEL = 128
        D_STATE = 64
        D_CONV = 4
        EXPAND = 2
        HEADDIM = 64
        D_INNER = EXPAND * D_MODEL
        NHEADS = D_INNER // HEADDIM
        CONV_DIM = D_INNER + 2 * D_STATE
        D_IN_PROJ = 2 * D_INNER + 2 * D_STATE + NHEADS
        CHUNK = 128
        EPS = 1e-05

        def segsum(a):
            T = a.shape[-1]
            cs = jnp.cumsum(a, axis=-1)
            ss = cs[..., :, None] - cs[..., None, :]
            mask = jnp.tril(jnp.ones((T, T), dtype=bool))
            return jnp.where(mask, ss, -jnp.inf)

        def mamba2_block(x, W_in, conv_w, conv_b, dt_bias, A_log, D, norm_w, W_out, W_lin, b_lin):
            Bsz, L, _ = x.shape
            zxbcdt = x @ W_in
            z, xBC, dt = jnp.split(zxbcdt, [D_INNER, D_INNER + CONV_DIM], axis=-1)
            xp = jnp.pad(xBC, ((0, 0), (D_CONV - 1, 0), (0, 0)))
            conv = conv_b + sum((xp[:, k:k + L, :] * conv_w[:, k] for k in range(D_CONV)))
            xBC = jax.nn.silu(conv)
            xh, Bmat, Cmat = jnp.split(xBC, [D_INNER, D_INNER + D_STATE], axis=-1)
            dt = jax.nn.softplus(dt + dt_bias)
            A = -jnp.exp(A_log)
            nc = L // CHUNK
            xh = xh.reshape(Bsz, nc, CHUNK, NHEADS, HEADDIM)
            Bc = Bmat.reshape(Bsz, nc, CHUNK, D_STATE)
            Cc = Cmat.reshape(Bsz, nc, CHUNK, D_STATE)
            dtc = dt.reshape(Bsz, nc, CHUNK, NHEADS)
            dA = jnp.einsum('bclh,h->bhcl', dtc, A)
            A_cum = jnp.cumsum(dA, axis=-1)
            Lmat = jnp.exp(segsum(dA))
            xdt = xh * dtc[..., None]
            Y_diag = jnp.einsum('bcln,bcsn,bhcls,bcshp->bclhp', Cc, Bc, Lmat, xdt)
            decay_states = jnp.exp(A_cum[..., -1:] - A_cum)
            states = jnp.einsum('bcln,bhcl,bclhp->bchpn', Bc, decay_states, xdt)
            chunk_decay = jnp.exp(A_cum[..., -1])

            def step(h, inp):
                s, d = inp
                return (h * d[..., None, None] + s, h)
            _, prevs = jax.lax.scan(step, jnp.zeros_like(states[:, 0]), (jnp.moveaxis(states, 1, 0), jnp.moveaxis(chunk_decay, 2, 0)))
            prevs = jnp.moveaxis(prevs, 0, 1)
            Y_off = jnp.einsum('bcln,bchpn,bhcl->bclhp', Cc, prevs, jnp.exp(A_cum))
            Y = (Y_diag + Y_off + xh * D[:, None]).reshape(Bsz, L, D_INNER)
            Y = Y * jax.nn.silu(z)
            Y = Y * jax.lax.rsqrt(jnp.mean(Y * Y, axis=-1, keepdims=True) + EPS) * norm_w
            out = Y @ W_out
            return out @ W_lin + b_lin
        key = jax.random.key(seed)
        ks = jax.random.split(key, 12)
        B, L = (8, 2048)

        def gauss(k, shape, scale):
            return jax.random.normal(k, shape, dtype=jnp.float32) * scale
        return {'x': gauss(ks[0], (B, L, D_MODEL), 1.0), 'W_in': gauss(ks[1], (D_MODEL, D_IN_PROJ), D_MODEL ** (-0.5)), 'conv_w': gauss(ks[2], (CONV_DIM, D_CONV), 0.3), 'conv_b': gauss(ks[3], (CONV_DIM,), 0.1), 'dt_bias': jax.random.uniform(ks[4], (NHEADS,), minval=-4.0, maxval=-1.0), 'A_log': jnp.log(jax.random.uniform(ks[5], (NHEADS,), minval=1.0, maxval=16.0)), 'D': jnp.ones((NHEADS,), jnp.float32), 'norm_w': jnp.ones((D_INNER,), jnp.float32), 'W_out': gauss(ks[6], (D_INNER, D_MODEL), D_INNER ** (-0.5)), 'W_lin': gauss(ks[7], (D_MODEL, D_MODEL), D_MODEL ** (-0.5)), 'b_lin': jnp.zeros((D_MODEL,), jnp.float32)}
    _L0_ffn_all = _L0_ffn_setup()
    _L0_ffn_in = {k: v for k, v in _L0_ffn_all.items() if k in ('W_in', 'conv_w', 'conv_b', 'dt_bias', 'A_log', 'D', 'norm_w', 'W_out', 'W_lin', 'b_lin')}
    del _L0_ffn_all

    def _L1_gnn_setup():
        import jax, jax.numpy as jnp
        import numpy as np
        key = jax.random.key(seed)
        k1, k2, k3, k4 = jax.random.split(key, 4)
        B, N, F_in, F_out = (8, 1024, 128, 128)
        x = jax.random.normal(k1, (B, N, F_in), dtype=jnp.float32)
        adj = jax.random.uniform(k2, (B, N, N), dtype=jnp.float32)
        stdv = 1.0 / np.sqrt(F_out)
        weight = jax.random.uniform(k3, (F_in, F_out), dtype=jnp.float32, minval=-stdv, maxval=stdv)
        bias = jax.random.uniform(k4, (F_out,), dtype=jnp.float32, minval=-stdv, maxval=stdv)
        return {'x': x, 'adj': adj, 'weight': weight, 'bias': bias}
    _L1_gnn_all = _L1_gnn_setup()
    _L1_gnn_in = {k: v for k, v in _L1_gnn_all.items() if k in ('weight', 'bias')}
    del _L1_gnn_all

    def _L1_ffn_setup():
        import jax, jax.numpy as jnp
        import numpy as np
        B, K, D = (256, 16, 128)
        E = 32
        H = int(D * 0.25)
        key = jax.random.key(seed)
        ks = jax.random.split(key, 7)
        d_rs = D ** (-0.5)
        h_rs = H ** (-0.5)
        x = jax.random.normal(ks[0], (B, K, D), dtype=jnp.float32)
        router_w = jax.random.uniform(ks[1], (E, D), jnp.float32, -d_rs, d_rs)
        router_b = jax.random.uniform(ks[2], (E,), jnp.float32, -d_rs, d_rs)
        W1 = jax.random.uniform(ks[3], (E, D, H), jnp.float32, -h_rs, h_rs)
        b1 = jax.random.uniform(ks[4], (E, H), jnp.float32, -h_rs, h_rs)
        W2 = jax.random.uniform(ks[5], (E, H, D), jnp.float32, -d_rs, d_rs)
        b2 = jax.random.uniform(ks[6], (E, D), jnp.float32, -d_rs, d_rs)
        return {'x': x, 'router_w': router_w, 'router_b': router_b, 'W1': W1, 'b1': b1, 'W2': W2, 'b2': b2}
    _L1_ffn_all = _L1_ffn_setup()
    _L1_ffn_in = {k: v for k, v in _L1_ffn_all.items() if k in ('router_w', 'router_b', 'W1', 'b1', 'W2', 'b2')}
    del _L1_ffn_all

    def _L2_gnn_setup():
        import jax, jax.numpy as jnp
        import numpy as np
        from jax import lax
        DIM = 128
        EPS = 1e-05

        def _bn(h, g, b, m, v):
            scale = g / jnp.sqrt(v + EPS)
            return h * scale[None, :, None] + (b - m * scale)[None, :, None]

        def _conv1d(h, w, pad):
            return lax.conv_general_dilated(h, w, window_strides=(1,), padding=[(pad, pad)], dimension_numbers=('NCH', 'OIH', 'NCH'))
        key = jax.random.key(seed)
        ks = jax.random.split(key, 16)
        bs, n, d = (16, 1024, DIM)
        s = 0.05
        return {'x': jax.random.normal(ks[0], (bs, n, d), jnp.float32), 'mask': jnp.ones((bs, n, n), jnp.float32), 'w_se': jax.random.normal(ks[1], (3, d), jnp.float32) * s, 'b_se': jnp.zeros((3,), jnp.float32), 'conv1_w': jax.random.normal(ks[2], (d, d, 1), jnp.float32) * s, 'bn1_g': jnp.ones((d,), jnp.float32), 'bn1_b': jnp.zeros((d,), jnp.float32), 'bn1_m': jnp.zeros((d,), jnp.float32), 'bn1_v': jnp.ones((d,), jnp.float32), 'conv2_w': jax.random.normal(ks[3], (d, d, 17), jnp.float32) * s, 'bn2_g': jnp.ones((d,), jnp.float32), 'bn2_b': jnp.zeros((d,), jnp.float32), 'bn2_m': jnp.zeros((d,), jnp.float32), 'bn2_v': jnp.ones((d,), jnp.float32), 'w_msg': jax.random.normal(ks[4], (d, d), jnp.float32) * s, 'b_msg': jnp.zeros((d,), jnp.float32), 'w_ih': jax.random.normal(ks[5], (3 * d, 2 * d), jnp.float32) * s, 'b_ih': jnp.zeros((3 * d,), jnp.float32), 'w_hh': jax.random.normal(ks[6], (3 * d, d), jnp.float32) * s, 'b_hh': jnp.zeros((3 * d,), jnp.float32)}
    _L2_gnn_all = _L2_gnn_setup()
    _L2_gnn_in = {k: v for k, v in _L2_gnn_all.items() if k in ('w_se', 'b_se', 'conv1_w', 'bn1_g', 'bn1_b', 'bn1_m', 'bn1_v', 'conv2_w', 'bn2_g', 'bn2_b', 'bn2_m', 'bn2_v', 'w_msg', 'b_msg', 'w_ih', 'b_ih', 'w_hh', 'b_hh')}
    del _L2_gnn_all

    def _L2_ffn_setup():
        import jax, jax.numpy as jnp
        import numpy as np
        B, T, C = (64, 192, 128)
        NH, NKV = (4, 2)
        HD = C // NH
        NREP = NH // NKV
        NE, TOPK = (8, 2)
        HID = int(8 / 3 * C)
        EPS_RMS = 1e-06

        def _rope_tables(t_len):
            inv_freq = 1.0 / 10000.0 ** (np.arange(0, HD, 2, dtype=np.float32) / HD)
            t = np.arange(t_len, dtype=np.float32)
            freqs = np.outer(t, inv_freq)
            emb = np.concatenate([freqs, freqs], axis=-1)
            return (jnp.asarray(np.cos(emb)), jnp.asarray(np.sin(emb)))

        def _rotate_half(x):
            h = x.shape[-1] // 2
            return jnp.concatenate([-x[..., h:], x[..., :h]], axis=-1)

        def _rmsnorm(v, w):
            return v * jax.lax.rsqrt(jnp.mean(v * v, axis=-1, keepdims=True) + EPS_RMS) * w
        key = jax.random.key(seed)
        ks = jax.random.split(key, 10)
        s = lambda k, shape: jax.random.normal(k, shape, jnp.float32) * 0.02
        return {'x': jax.random.normal(ks[0], (B, T, C), jnp.float32), 'ln1_w': jnp.ones((C,), jnp.float32), 'ln2_w': jnp.ones((C,), jnp.float32), 'wq': s(ks[1], (NH * HD, C)), 'wk': s(ks[2], (NKV * HD, C)), 'wv': s(ks[3], (NKV * HD, C)), 'wo': s(ks[4], (C, C)), 'router_w': s(ks[5], (NE, C)), 'w1': s(ks[6], (NE, HID, C)), 'w2': s(ks[7], (NE, C, HID)), 'w3': s(ks[8], (NE, HID, C))}
    _L2_ffn_all = _L2_ffn_setup()
    _L2_ffn_in = {k: v for k, v in _L2_ffn_all.items() if k in ('ln1_w', 'ln2_w', 'wq', 'wk', 'wv', 'wo', 'router_w', 'w1', 'w2', 'w3')}
    del _L2_ffn_all

    def _L3_gnn_setup():
        import jax, jax.numpy as jnp
        import numpy as np
        B, K, H = (32, 512, 128)
        LN_EPS = 1e-05

        def layer_norm(x, gamma, beta):
            mu = jnp.mean(x, axis=-1, keepdims=True)
            var = jnp.mean(jnp.square(x - mu), axis=-1, keepdims=True)
            return (x - mu) * jax.lax.rsqrt(var + LN_EPS) * gamma + beta
        key = jax.random.key(seed)
        k1, k2, k3, k4 = jax.random.split(key, 4)
        x = jax.random.normal(k1, (B, K, H), dtype=jnp.float32)
        adj = jax.random.uniform(k2, (B, K, K), dtype=jnp.float32)
        s = 1.0 / np.sqrt(H)
        W_rel = jax.random.normal(k3, (H, H), dtype=jnp.float32) * s
        b_rel = jnp.zeros((H,), dtype=jnp.float32)
        W_root = jax.random.normal(k4, (H, H), dtype=jnp.float32) * s
        ln_gamma = jnp.ones((H,), dtype=jnp.float32)
        ln_beta = jnp.zeros((H,), dtype=jnp.float32)
        return {'x': x, 'adj': adj, 'W_rel': W_rel, 'b_rel': b_rel, 'W_root': W_root, 'ln_gamma': ln_gamma, 'ln_beta': ln_beta}
    _L3_gnn_all = _L3_gnn_setup()
    _L3_gnn_in = {k: v for k, v in _L3_gnn_all.items() if k in ('W_rel', 'b_rel', 'W_root', 'ln_gamma', 'ln_beta')}
    del _L3_gnn_all

    def _L3_ffn_setup():
        import jax, jax.numpy as jnp
        import numpy as np
        B, S, H, F, E, K = (8, 2048, 128, 256, 16, 2)
        EPS = 1e-05
        key = jax.random.key(seed)
        ks = jax.random.split(key, 9)
        sc = 0.02
        return {'x': jax.random.normal(ks[0], (B, S, H), dtype=jnp.float32), 'gate_w': jax.random.normal(ks[1], (H, E), dtype=jnp.float32) * sc, 'gate_b': jnp.zeros((E,), dtype=jnp.float32), 'w1': jax.random.normal(ks[2], (E, H, F), dtype=jnp.float32) * sc, 'b1': jnp.zeros((E, F), dtype=jnp.float32), 'w2': jax.random.normal(ks[3], (E, F, H), dtype=jnp.float32) * sc, 'b2': jnp.zeros((E, H), dtype=jnp.float32), 'gamma': jnp.ones((H,), dtype=jnp.float32), 'beta': jnp.zeros((H,), dtype=jnp.float32)}
    _L3_ffn_all = _L3_ffn_setup()
    _L3_ffn_in = {k: v for k, v in _L3_ffn_all.items() if k in ('gate_w', 'gate_b', 'w1', 'b1', 'w2', 'b2', 'gamma', 'beta')}
    del _L3_ffn_all
    return {'x': x, 'adj': adj, 'L0_gnn_W': _L0_gnn_in['W'], 'L0_gnn_a': _L0_gnn_in['a'], 'L0_ffn_W_in': _L0_ffn_in['W_in'], 'L0_ffn_conv_w': _L0_ffn_in['conv_w'], 'L0_ffn_conv_b': _L0_ffn_in['conv_b'], 'L0_ffn_dt_bias': _L0_ffn_in['dt_bias'], 'L0_ffn_A_log': _L0_ffn_in['A_log'], 'L0_ffn_D': _L0_ffn_in['D'], 'L0_ffn_norm_w': _L0_ffn_in['norm_w'], 'L0_ffn_W_out': _L0_ffn_in['W_out'], 'L0_ffn_W_lin': _L0_ffn_in['W_lin'], 'L0_ffn_b_lin': _L0_ffn_in['b_lin'], 'L1_gnn_weight': _L1_gnn_in['weight'], 'L1_gnn_bias': _L1_gnn_in['bias'], 'L1_ffn_router_w': _L1_ffn_in['router_w'], 'L1_ffn_router_b': _L1_ffn_in['router_b'], 'L1_ffn_W1': _L1_ffn_in['W1'], 'L1_ffn_b1': _L1_ffn_in['b1'], 'L1_ffn_W2': _L1_ffn_in['W2'], 'L1_ffn_b2': _L1_ffn_in['b2'], 'L2_gnn_w_se': _L2_gnn_in['w_se'], 'L2_gnn_b_se': _L2_gnn_in['b_se'], 'L2_gnn_conv1_w': _L2_gnn_in['conv1_w'], 'L2_gnn_bn1_g': _L2_gnn_in['bn1_g'], 'L2_gnn_bn1_b': _L2_gnn_in['bn1_b'], 'L2_gnn_bn1_m': _L2_gnn_in['bn1_m'], 'L2_gnn_bn1_v': _L2_gnn_in['bn1_v'], 'L2_gnn_conv2_w': _L2_gnn_in['conv2_w'], 'L2_gnn_bn2_g': _L2_gnn_in['bn2_g'], 'L2_gnn_bn2_b': _L2_gnn_in['bn2_b'], 'L2_gnn_bn2_m': _L2_gnn_in['bn2_m'], 'L2_gnn_bn2_v': _L2_gnn_in['bn2_v'], 'L2_gnn_w_msg': _L2_gnn_in['w_msg'], 'L2_gnn_b_msg': _L2_gnn_in['b_msg'], 'L2_gnn_w_ih': _L2_gnn_in['w_ih'], 'L2_gnn_b_ih': _L2_gnn_in['b_ih'], 'L2_gnn_w_hh': _L2_gnn_in['w_hh'], 'L2_gnn_b_hh': _L2_gnn_in['b_hh'], 'L2_ffn_ln1_w': _L2_ffn_in['ln1_w'], 'L2_ffn_ln2_w': _L2_ffn_in['ln2_w'], 'L2_ffn_wq': _L2_ffn_in['wq'], 'L2_ffn_wk': _L2_ffn_in['wk'], 'L2_ffn_wv': _L2_ffn_in['wv'], 'L2_ffn_wo': _L2_ffn_in['wo'], 'L2_ffn_router_w': _L2_ffn_in['router_w'], 'L2_ffn_w1': _L2_ffn_in['w1'], 'L2_ffn_w2': _L2_ffn_in['w2'], 'L2_ffn_w3': _L2_ffn_in['w3'], 'L3_gnn_W_rel': _L3_gnn_in['W_rel'], 'L3_gnn_b_rel': _L3_gnn_in['b_rel'], 'L3_gnn_W_root': _L3_gnn_in['W_root'], 'L3_gnn_ln_gamma': _L3_gnn_in['ln_gamma'], 'L3_gnn_ln_beta': _L3_gnn_in['ln_beta'], 'L3_ffn_gate_w': _L3_ffn_in['gate_w'], 'L3_ffn_gate_b': _L3_ffn_in['gate_b'], 'L3_ffn_w1': _L3_ffn_in['w1'], 'L3_ffn_b1': _L3_ffn_in['b1'], 'L3_ffn_w2': _L3_ffn_in['w2'], 'L3_ffn_b2': _L3_ffn_in['b2'], 'L3_ffn_gamma': _L3_ffn_in['gamma'], 'L3_ffn_beta': _L3_ffn_in['beta']}

def reference(x, adj, L0_gnn_W, L0_gnn_a, L0_ffn_W_in, L0_ffn_conv_w, L0_ffn_conv_b, L0_ffn_dt_bias, L0_ffn_A_log, L0_ffn_D, L0_ffn_norm_w, L0_ffn_W_out, L0_ffn_W_lin, L0_ffn_b_lin, L1_gnn_weight, L1_gnn_bias, L1_ffn_router_w, L1_ffn_router_b, L1_ffn_W1, L1_ffn_b1, L1_ffn_W2, L1_ffn_b2, L2_gnn_w_se, L2_gnn_b_se, L2_gnn_conv1_w, L2_gnn_bn1_g, L2_gnn_bn1_b, L2_gnn_bn1_m, L2_gnn_bn1_v, L2_gnn_conv2_w, L2_gnn_bn2_g, L2_gnn_bn2_b, L2_gnn_bn2_m, L2_gnn_bn2_v, L2_gnn_w_msg, L2_gnn_b_msg, L2_gnn_w_ih, L2_gnn_b_ih, L2_gnn_w_hh, L2_gnn_b_hh, L2_ffn_ln1_w, L2_ffn_ln2_w, L2_ffn_wq, L2_ffn_wk, L2_ffn_wv, L2_ffn_wo, L2_ffn_router_w, L2_ffn_w1, L2_ffn_w2, L2_ffn_w3, L3_gnn_W_rel, L3_gnn_b_rel, L3_gnn_W_root, L3_gnn_ln_gamma, L3_gnn_ln_beta, L3_ffn_gate_w, L3_ffn_gate_b, L3_ffn_w1, L3_ffn_b1, L3_ffn_w2, L3_ffn_b2, L3_ffn_gamma, L3_ffn_beta):
    import jax
    import jax.numpy as jnp

    def _L0_gnn_ref(x, adj_matrix, W, a):
        import jax, jax.numpy as jnp
        import numpy as np
        B, N, D_IN, D_OUT = (16, 512, 128, 128)
        NEG_INF = -9000000000000000.0
        LRELU_SLOPE = 0.2
        h = jnp.einsum('bni,io->bno', x, W)
        d = h.shape[-1]
        a1 = a[:d, 0]
        a2 = a[d:, 0]
        src = h @ a1
        dst = h @ a2
        e = src[:, :, None] + dst[:, None, :]
        e = jnp.where(e >= 0, e, LRELU_SLOPE * e)
        masked_e = jnp.where(adj_matrix > 0, e, NEG_INF)
        attention = jax.nn.softmax(masked_e, axis=2)
        h_out = jnp.einsum('bij,bjd->bid', attention, h)
        return h_out

    def _L0_ffn_ref(x, W_in, conv_w, conv_b, dt_bias, A_log, D, norm_w, W_out, W_lin, b_lin):
        import jax, jax.numpy as jnp
        import numpy as np
        D_MODEL = 128
        D_STATE = 64
        D_CONV = 4
        EXPAND = 2
        HEADDIM = 64
        D_INNER = EXPAND * D_MODEL
        NHEADS = D_INNER // HEADDIM
        CONV_DIM = D_INNER + 2 * D_STATE
        D_IN_PROJ = 2 * D_INNER + 2 * D_STATE + NHEADS
        CHUNK = 128
        EPS = 1e-05

        def segsum(a):
            T = a.shape[-1]
            cs = jnp.cumsum(a, axis=-1)
            ss = cs[..., :, None] - cs[..., None, :]
            mask = jnp.tril(jnp.ones((T, T), dtype=bool))
            return jnp.where(mask, ss, -jnp.inf)

        def mamba2_block(x, W_in, conv_w, conv_b, dt_bias, A_log, D, norm_w, W_out, W_lin, b_lin):
            Bsz, L, _ = x.shape
            zxbcdt = x @ W_in
            z, xBC, dt = jnp.split(zxbcdt, [D_INNER, D_INNER + CONV_DIM], axis=-1)
            xp = jnp.pad(xBC, ((0, 0), (D_CONV - 1, 0), (0, 0)))
            conv = conv_b + sum((xp[:, k:k + L, :] * conv_w[:, k] for k in range(D_CONV)))
            xBC = jax.nn.silu(conv)
            xh, Bmat, Cmat = jnp.split(xBC, [D_INNER, D_INNER + D_STATE], axis=-1)
            dt = jax.nn.softplus(dt + dt_bias)
            A = -jnp.exp(A_log)
            nc = L // CHUNK
            xh = xh.reshape(Bsz, nc, CHUNK, NHEADS, HEADDIM)
            Bc = Bmat.reshape(Bsz, nc, CHUNK, D_STATE)
            Cc = Cmat.reshape(Bsz, nc, CHUNK, D_STATE)
            dtc = dt.reshape(Bsz, nc, CHUNK, NHEADS)
            dA = jnp.einsum('bclh,h->bhcl', dtc, A)
            A_cum = jnp.cumsum(dA, axis=-1)
            Lmat = jnp.exp(segsum(dA))
            xdt = xh * dtc[..., None]
            Y_diag = jnp.einsum('bcln,bcsn,bhcls,bcshp->bclhp', Cc, Bc, Lmat, xdt)
            decay_states = jnp.exp(A_cum[..., -1:] - A_cum)
            states = jnp.einsum('bcln,bhcl,bclhp->bchpn', Bc, decay_states, xdt)
            chunk_decay = jnp.exp(A_cum[..., -1])

            def step(h, inp):
                s, d = inp
                return (h * d[..., None, None] + s, h)
            _, prevs = jax.lax.scan(step, jnp.zeros_like(states[:, 0]), (jnp.moveaxis(states, 1, 0), jnp.moveaxis(chunk_decay, 2, 0)))
            prevs = jnp.moveaxis(prevs, 0, 1)
            Y_off = jnp.einsum('bcln,bchpn,bhcl->bclhp', Cc, prevs, jnp.exp(A_cum))
            Y = (Y_diag + Y_off + xh * D[:, None]).reshape(Bsz, L, D_INNER)
            Y = Y * jax.nn.silu(z)
            Y = Y * jax.lax.rsqrt(jnp.mean(Y * Y, axis=-1, keepdims=True) + EPS) * norm_w
            out = Y @ W_out
            return out @ W_lin + b_lin
        return mamba2_block(x, W_in, conv_w, conv_b, dt_bias, A_log, D, norm_w, W_out, W_lin, b_lin)

    def _L1_gnn_ref(x, adj, weight, bias):
        import jax, jax.numpy as jnp
        import numpy as np
        support = jnp.einsum('bni,io->bno', x, weight)
        out = jnp.einsum('bnm,bmo->bno', adj, support)
        return out + bias

    def _L1_ffn_ref(x, router_w, router_b, W1, b1, W2, b2):
        import jax, jax.numpy as jnp
        import numpy as np
        B, K, D = (256, 16, 128)
        E = 32
        H = int(D * 0.25)
        xf = x.reshape(-1, D)
        logits = xf @ router_w.T + router_b
        idx = jnp.argmax(logits, axis=-1)
        w1t = jnp.take(W1, idx, axis=0)
        h = jnp.einsum('nd,ndh->nh', xf, w1t) + jnp.take(b1, idx, axis=0)
        h = jax.nn.relu(h)
        w2t = jnp.take(W2, idx, axis=0)
        out = jnp.einsum('nh,nhd->nd', h, w2t) + jnp.take(b2, idx, axis=0)
        out = jax.nn.relu(out)
        return out.reshape(x.shape)

    def _L2_gnn_ref(x, mask, w_se, b_se, conv1_w, bn1_g, bn1_b, bn1_m, bn1_v, conv2_w, bn2_g, bn2_b, bn2_m, bn2_v, w_msg, b_msg, w_ih, b_ih, w_hh, b_hh):
        import jax, jax.numpy as jnp
        import numpy as np
        from jax import lax
        DIM = 128
        EPS = 1e-05

        def _bn(h, g, b, m, v):
            scale = g / jnp.sqrt(v + EPS)
            return h * scale[None, :, None] + (b - m * scale)[None, :, None]

        def _conv1d(h, w, pad):
            return lax.conv_general_dilated(h, w, window_strides=(1,), padding=[(pad, pad)], dimension_numbers=('NCH', 'OIH', 'NCH'))
        d = x.shape[-1]
        xc = jnp.transpose(x, (0, 2, 1))
        h = _bn(_conv1d(xc, conv1_w, 0), bn1_g, bn1_b, bn1_m, bn1_v)
        h = jax.nn.relu(h)
        h = _bn(_conv1d(h, conv2_w, 8), bn2_g, bn2_b, bn2_m, bn2_v)
        x_conv = jnp.transpose(jax.nn.relu(h + xc), (0, 2, 1))
        s = x @ w_se.T + b_se
        sq = jnp.sum(s * s, axis=-1)
        dist = sq[:, :, None] + sq[:, None, :] - 2.0 * jnp.einsum('bnd,bmd->bnm', s, s)
        A = jnp.exp(-dist) * mask
        msg = jax.nn.relu(x @ w_msg.T + b_msg)
        x_nmp = jnp.einsum('bnm,bmd->bnd', A, msg)
        x_in = jnp.concatenate([x_conv, x_nmp], axis=-1)
        gi = x_in @ w_ih.T + b_ih
        gh = x @ w_hh.T + b_hh
        gi_r, gi_z, gi_n = (gi[..., :d], gi[..., d:2 * d], gi[..., 2 * d:])
        gh_r, gh_z, gh_n = (gh[..., :d], gh[..., d:2 * d], gh[..., 2 * d:])
        r = jax.nn.sigmoid(gi_r + gh_r)
        z = jax.nn.sigmoid(gi_z + gh_z)
        nn_ = jnp.tanh(gi_n + r * gh_n)
        return (1.0 - z) * nn_ + z * x

    def _L2_ffn_ref(x, ln1_w, ln2_w, wq, wk, wv, wo, router_w, w1, w2, w3):
        import jax, jax.numpy as jnp
        import numpy as np
        B, T, C = (64, 192, 128)
        NH, NKV = (4, 2)
        HD = C // NH
        NREP = NH // NKV
        NE, TOPK = (8, 2)
        HID = int(8 / 3 * C)
        EPS_RMS = 1e-06

        def _rope_tables(t_len):
            inv_freq = 1.0 / 10000.0 ** (np.arange(0, HD, 2, dtype=np.float32) / HD)
            t = np.arange(t_len, dtype=np.float32)
            freqs = np.outer(t, inv_freq)
            emb = np.concatenate([freqs, freqs], axis=-1)
            return (jnp.asarray(np.cos(emb)), jnp.asarray(np.sin(emb)))

        def _rotate_half(x):
            h = x.shape[-1] // 2
            return jnp.concatenate([-x[..., h:], x[..., :h]], axis=-1)

        def _rmsnorm(v, w):
            return v * jax.lax.rsqrt(jnp.mean(v * v, axis=-1, keepdims=True) + EPS_RMS) * w
        Bx, Tx, Cx = x.shape
        h = _rmsnorm(x, ln1_w)
        q = (h @ wq.T).reshape(Bx, Tx, NH, HD).transpose(0, 2, 1, 3)
        k = (h @ wk.T).reshape(Bx, Tx, NKV, HD).transpose(0, 2, 1, 3)
        v = (h @ wv.T).reshape(Bx, Tx, NKV, HD).transpose(0, 2, 1, 3)
        cos, sin = _rope_tables(Tx)
        cos, sin = (cos[None, None], sin[None, None])
        q = q * cos + _rotate_half(q) * sin
        k = k * cos + _rotate_half(k) * sin
        k = jnp.repeat(k, NREP, axis=1)
        v = jnp.repeat(v, NREP, axis=1)
        scores = jnp.einsum('bhtd,bhsd->bhts', q, k) / jnp.sqrt(jnp.float32(HD))
        causal = jnp.tril(jnp.ones((Tx, Tx), dtype=bool))
        scores = jnp.where(causal[None, None], scores, jnp.float32(-1e+30))
        att = jax.nn.softmax(scores, axis=-1)
        y = jnp.einsum('bhts,bhsd->bhtd', att, v).transpose(0, 2, 1, 3).reshape(Bx, Tx, Cx)
        x = x + y @ wo.T
        flat = _rmsnorm(x, ln2_w).reshape(-1, Cx)
        probs = jax.nn.softmax(flat @ router_w.T, axis=-1)
        tp, ti = jax.lax.top_k(probs, TOPK)
        tp = tp / (jnp.sum(tp, axis=-1, keepdims=True) + 1e-09)
        weights = jnp.sum(tp[..., None] * jax.nn.one_hot(ti, NE, dtype=flat.dtype), axis=1)
        out = jnp.zeros_like(flat)
        for e in range(NE):
            hh = jax.nn.silu(flat @ w1[e].T) * (flat @ w3[e].T)
            out = out + weights[:, e:e + 1] * (hh @ w2[e].T)
        return x + out.reshape(Bx, Tx, Cx)

    def _L3_gnn_ref(x, adj, W_rel, b_rel, W_root, ln_gamma, ln_beta):
        import jax, jax.numpy as jnp
        import numpy as np
        B, K, H = (32, 512, 128)
        LN_EPS = 1e-05

        def layer_norm(x, gamma, beta):
            mu = jnp.mean(x, axis=-1, keepdims=True)
            var = jnp.mean(jnp.square(x - mu), axis=-1, keepdims=True)
            return (x - mu) * jax.lax.rsqrt(var + LN_EPS) * gamma + beta
        h = layer_norm(x, ln_gamma, ln_beta)
        agg = jnp.einsum('bij,bjh->bih', adj, h)
        conv = jnp.einsum('bkh,ho->bko', agg, W_rel) + b_rel + jnp.einsum('bkh,ho->bko', h, W_root)
        return x + jax.nn.relu(conv)

    def _L3_ffn_ref(x, gate_w, gate_b, w1, b1, w2, b2, gamma, beta):
        import jax, jax.numpy as jnp
        import numpy as np
        B, S, H, F, E, K = (8, 2048, 128, 256, 16, 2)
        EPS = 1e-05
        gate_logits = x @ gate_w + gate_b
        topk_vals, topk_idx = jax.lax.top_k(gate_logits, K)
        topk_w = jax.nn.softmax(topk_vals, axis=-1)
        h = jax.nn.relu(jnp.einsum('bsh,ehf->bsef', x, w1) + b1)
        expert_out = jnp.einsum('bsef,efh->bseh', h, w2) + b2
        sel = jnp.take_along_axis(expert_out, topk_idx[:, :, :, None], axis=2)
        moe = jnp.sum(topk_w[..., None] * sel, axis=2)
        y = x + moe
        mu = jnp.mean(y, axis=-1, keepdims=True)
        var = jnp.var(y, axis=-1, keepdims=True)
        return (y - mu) / jnp.sqrt(var + EPS) * gamma + beta
    x = x + _L0_gnn_ref(_layernorm(x, axis=-1), adj, L0_gnn_W, L0_gnn_a)
    x = x + _L0_ffn_ref(_layernorm(x, axis=-1), L0_ffn_W_in, L0_ffn_conv_w, L0_ffn_conv_b, L0_ffn_dt_bias, L0_ffn_A_log, L0_ffn_D, L0_ffn_norm_w, L0_ffn_W_out, L0_ffn_W_lin, L0_ffn_b_lin)
    x = x + _L1_gnn_ref(_layernorm(x, axis=-1), adj, L1_gnn_weight, L1_gnn_bias)
    x = x + _L1_ffn_ref(_layernorm(x, axis=-1), L1_ffn_router_w, L1_ffn_router_b, L1_ffn_W1, L1_ffn_b1, L1_ffn_W2, L1_ffn_b2)
    x = x + _L2_gnn_ref(_layernorm(x, axis=-1), adj, L2_gnn_w_se, L2_gnn_b_se, L2_gnn_conv1_w, L2_gnn_bn1_g, L2_gnn_bn1_b, L2_gnn_bn1_m, L2_gnn_bn1_v, L2_gnn_conv2_w, L2_gnn_bn2_g, L2_gnn_bn2_b, L2_gnn_bn2_m, L2_gnn_bn2_v, L2_gnn_w_msg, L2_gnn_b_msg, L2_gnn_w_ih, L2_gnn_b_ih, L2_gnn_w_hh, L2_gnn_b_hh)
    x = x + _L2_ffn_ref(_layernorm(x, axis=-1), L2_ffn_ln1_w, L2_ffn_ln2_w, L2_ffn_wq, L2_ffn_wk, L2_ffn_wv, L2_ffn_wo, L2_ffn_router_w, L2_ffn_w1, L2_ffn_w2, L2_ffn_w3)
    x = x + _L3_gnn_ref(_layernorm(x, axis=-1), adj, L3_gnn_W_rel, L3_gnn_b_rel, L3_gnn_W_root, L3_gnn_ln_gamma, L3_gnn_ln_beta)
    x = x + _L3_ffn_ref(_layernorm(x, axis=-1), L3_ffn_gate_w, L3_ffn_gate_b, L3_ffn_w1, L3_ffn_b1, L3_ffn_w2, L3_ffn_b2, L3_ffn_gamma, L3_ffn_beta)
    return x

_drawn_inputs = setup_inputs


def setup_inputs(seed=0):
    import zlib

    import numpy as np

    out = dict(_drawn_inputs(seed))
    spreads = {'L0_ffn_D': (1.0, 0.2),
     'L0_ffn_norm_w': (1.0, 0.2),
     'L0_ffn_b_lin': (0.0, 0.1),
     'L2_gnn_b_se': (0.0, 2.0),
     'L2_gnn_bn1_g': (1.0, 0.6),
     'L2_gnn_bn1_b': (0.0, 0.8),
     'L2_gnn_bn1_m': (0.0, 0.8),
     'L2_gnn_bn1_v': (1.0, 0.6),
     'L2_gnn_bn2_g': (1.0, 0.6),
     'L2_gnn_bn2_b': (0.0, 0.8),
     'L2_gnn_bn2_m': (0.0, 0.8),
     'L2_gnn_bn2_v': (1.0, 0.6),
     'L2_gnn_b_msg': (0.0, 0.333),
     'L2_gnn_b_ih': (0.0, 0.481),
     'L2_gnn_b_hh': (0.0, 0.8),
     'L2_ffn_ln1_w': (1.0, 0.6),
     'L2_ffn_ln2_w': (1.0, 0.6),
     'L3_gnn_b_rel': (0.0, 0.8),
     'L3_gnn_ln_gamma': (1.0, 0.2),
     'L3_gnn_ln_beta': (0.0, 0.1),
     'L3_ffn_gate_b': (0.0, 0.8),
     'L3_ffn_b1': (0.0, 0.8),
     'L3_ffn_b2': (0.0, 2.0),
     'L3_ffn_gamma': (1.0, 0.6),
     'L3_ffn_beta': (0.0, 0.8)}
    factors = {'L0_ffn_A_log': 6.83,
     'L1_ffn_router_b': 4.003,
     'L1_ffn_b1': 8.0,
     'L1_ffn_b2': 6.185,
     'L2_ffn_wq': 8.0,
     'L2_ffn_wk': 8.0,
     'L2_ffn_wv': 7.1,
     'L2_ffn_wo': 7.769,
     'L2_ffn_router_w': 8.0,
     'L2_ffn_w1': 8.0,
     'L2_ffn_w2': 8.0,
     'L2_ffn_w3': 8.0,
     'L3_ffn_gate_w': 7.048,
     'L3_ffn_w1': 8.0,
     'L3_ffn_w2': 8.0}
    for name, (base, spread) in spreads.items():
        noise = np.random.default_rng([zlib.crc32(name.encode()), seed]).standard_normal(out[name].shape)
        drawn = base * np.exp(spread * noise) if base else spread * noise
        out[name] = jnp.asarray(drawn.astype(out[name].dtype))
    for name, factor in factors.items():
        out[name] = (out[name] * factor).astype(out[name].dtype)
    return out
```

```python
from contextlib import ExitStack

import concourse.bass as bass
from concourse import mybir
from concourse.alu_op_type import AluOpType as ALU

ACT = mybir.ActivationFunctionType
AX = mybir.AxisListType
F32 = mybir.dt.float32
BF16 = mybir.dt.bfloat16
U32 = mybir.dt.uint32

N_LAYERS = 8
P = 128
N = 512
T = N // P
U = 2
NEG = -9.0e15
LN_EPS = 1e-5
RMS_EPS = 1e-6
HID, FCH = 341, 3
FW = [min(P, HID - P * f) for f in range(FCH)]
E1, E2, E3 = 32, 8, 16
TAPS, PAD = 17, 8
NHM, HDM, DST = 4, 64, 64
NHA, HDA = 4, 32
SLOTS = 15


def nth(k, u):
    return U * k + u + 1


class Semaphores:

    def __init__(self, ctx, nc):
        self.ctx, self.nc, self.of = ctx, nc, {}

    def __getitem__(self, name):
        if name not in self.of:
            self.of[name] = self.ctx.enter_context(self.nc.semaphore(name))
        return self.of[name]


class Chain:

    def __init__(self, engine, sem):
        self.engine, self.sem, self.n = engine, sem, 0

    def mark(self, ins):
        ins.then_inc(self.sem, 1)
        self.n += 1
        return self.n

    def wait(self, n):
        self.engine.wait_ge(self.sem, n)

    def link(self, ins):
        self.wait(self.mark(ins))


def build_network(nc, d, out):
    B = d["x"].shape[0]
    with ExitStack() as ctx:
        def sb(name, shape, dt=F32):
            return ctx.enter_context(nc.sbuf_tensor(name, shape, dt))

        S = Semaphores(ctx, nc)

        ident = sb("ident", [P, P])
        ident_h = sb("ident_h", [P, P], BF16)
        upper = sb("upper", [P, P])
        causal = sb("causal", [P, P], BF16)
        ones_row = sb("ones_row", [1, P])
        minus_half = sb("minus_half", [P, T])
        iota32 = sb("iota32", [P, E1])
        pick = sb("pick", [E1, E1 // 4, P], BF16)

        gat_w = sb("gat_w", [P, P])
        gat_wt = sb("gat_wt", [P, P])
        gat_a = sb("gat_a", [P, 2])
        gat_wa = sb("gat_wa", [P, 2])
        gat_wdst = sb("gat_wdst", [P, P])

        m_in = sb("m_in", [P, 644])
        m_taps = sb("m_taps", [P, 3, 4])
        m_convb = sb("m_convb", [P, 3])
        m_dtb = sb("m_dtb", [P, NHM])
        m_a = sb("m_a", [P, NHM])
        m_d = sb("m_d", [P, NHM])
        m_norm = sb("m_norm", [P, 2])
        m_wol = sb("m_wol", [P, 2, P])
        m_blin = sb("m_blin", [P, P])

        gcn_w = sb("gcn_w", [P, P])
        gcn_b = sb("gcn_b", [1, P])

        e1_router = sb("e1_router", [P, E1])
        e1_rb = sb("e1_rb", [P, E1])
        e1_w1 = sb("e1_w1", [P, 8, P])
        e1_b1 = sb("e1_b1", [P, 8])
        e1_w2 = sb("e1_w2", [P, 8, P])
        e1_b2 = sb("e1_b2", [E1, P])

        g_se = sb("g_se", [P, 96])
        g_seb = sb("g_seb", [96, 1])
        g_seb2 = sb("g_seb2", [32, 1])
        g_c1 = sb("g_c1", [P, P])
        g_c2 = sb("g_c2", [P, TAPS, P])
        g_bn = sb("g_bn", [P, 8])
        g_s = sb("g_s", [P, 2])
        g_c = sb("g_c", [P, 2])
        g_msg = sb("g_msg", [P, P])
        g_msgb = sb("g_msgb", [1, P])
        g_ih = sb("g_ih", [P, 2, 3 * P])
        g_hh = sb("g_hh", [P, 3 * P])
        g_bi = sb("g_bi", [P, 3])
        g_bh = sb("g_bh", [P, 3])
        g_half = sb("g_half", [P, 3])

        a_ln1 = sb("a_ln1", [P, 1])
        a_ln2 = sb("a_ln2", [P, 1])
        a_qk = sb("a_qk", [P, 4, P])
        a_v = sb("a_v", [P, 2 * HDA])
        a_o = sb("a_o", [P, P])
        a_cos = sb("a_cos", [P, N])
        a_sin = sb("a_sin", [P, N])
        e2_router = sb("e2_router", [P, E2])
        e2_w1 = sb("e2_w1", [P, E2, HID])
        e2_w3 = sb("e2_w3", [P, E2, HID])
        e2_w2 = sb("e2_w2", [P, E2, FCH, P])

        r_rel = sb("r_rel", [P, P])
        r_root = sb("r_root", [P, P])
        r_b = sb("r_b", [1, P])
        r_gamma = sb("r_gamma", [P, P])
        r_beta = sb("r_beta", [P, P])

        e3_gate = sb("e3_gate", [P, E3])
        e3_gb = sb("e3_gb", [P, E3])
        e3_w1 = sb("e3_w1", [P, E3, 2, P])
        e3_b1 = sb("e3_b1", [P, E3, 2])
        e3_w2 = sb("e3_w2", [P, E3, 2, P])
        e3_b2 = sb("e3_b2", [E3, P])
        e3_gamma = sb("e3_gamma", [P, P])
        e3_beta = sb("e3_beta", [P, P])

        def per(name, shape, dt=F32):
            return [sb(f"{name}{u}", shape, dt) for u in range(U)]

        x = per("x", [P, T, P])
        xh = per("xh", [P, T, P])
        xT = per("xT", [P, N])
        adjT = per("adjT", [P, T, N])
        work = per("work", [P, SLOTS, N])
        stats = per("stats", [P, T, 6])
        mv = per("mv", [P, T, 2])
        var = per("var", [P, T])
        rstd = per("rstd", [P, T])
        lg = per("lg", [P, T, E1])
        top = per("top", [P, T, 8])
        idx = per("idx", [P, T, 8], U32)
        idxf = per("idxf", [P, T, 2])
        oh = per("oh", [P, T, E1])
        oh2 = per("oh2", [P, T, E1])
        wts = per("wts", [P, T, E3])
        den = per("den", [P, T])
        den2 = per("den2", [P, T])
        sm = per("sm", [P, 8, 16])
        PS = [ctx.enter_context(nc.psum_tensor(f"PS{u}", [P, 4, N], F32)) for u in range(U)]

        def slot(u, a, n=1):
            return work[u][:, a:a + n, :].rearrange("p s n -> p (s n)")

        def tok(ap):
            return ap.rearrange("p (t c) -> p t c", t=T)

        def cols(t):
            return slice(P * t, P * (t + 1))

        with nc.Block() as block:
            loads = []

            def load(dst, src):
                loads.append((dst, src))

            def bcast(ap, n=P):
                return ap.partition_broadcast(n)

            load(gat_w[:], d["gat_w"]); load(gat_wt[:], d["gat_wt"]); load(gat_a[:], d["gat_a"])
            load(m_in[:], d["m_in"])
            load(m_taps[:], d["m_conv_w"])
            load(m_convb[:], d["m_conv_b"])
            load(m_dtb[:], bcast(d["m_dt_bias"]))
            load(m_a[:], bcast(d["m_a_log"]))
            load(m_d[:], bcast(d["m_d"]))
            load(m_norm[:], d["m_norm_w"])
            load(m_blin[:], bcast(d["m_b_lin"]))
            load(work[0][:, 0, 0:256], d["m_out_t"])
            load(work[0][:, 1, 0:P], d["m_lin"])
            load(gcn_w[:], d["gcn_w"]); load(gcn_b[:], d["gcn_b"].unsqueeze(0))
            load(e1_router[:], d["e1_router_t"]); load(e1_rb[:], bcast(d["e1_rb"]))
            load(e1_w1[:], d["e1_w1"])
            load(e1_b1[:], d["e1_b1"])
            load(e1_w2[:], d["e1_w2"])
            load(e1_b2[:], d["e1_b2"])
            load(g_c1[:], d["g_c1_t"]); load(g_c2[:], d["g_c2_t"])
            load(g_bn[:], d["g_bn"])
            load(g_msg[:], d["g_msg_t"]); load(g_msgb[:], d["g_msg_b"].unsqueeze(0))
            load(g_ih[:], d["g_ih_t"]); load(g_hh[:], d["g_hh_t"])
            load(g_bi[:], d["g_b_ih"])
            load(g_bh[:], d["g_b_hh"])
            load(a_ln1[:], d["a_ln1"]); load(a_ln2[:], d["a_ln2"])
            load(a_qk[:], d["a_qk"])
            load(a_v[:], d["a_v_t"]); load(a_o[:], d["a_o_t"])
            load(a_cos[:], d["a_cos"]); load(a_sin[:], d["a_sin"])
            load(e2_router[:], d["e2_router_t"])
            load(e2_w1[:], d["e2_w1_t"]); load(e2_w3[:], d["e2_w3_t"])
            for f in range(FCH):
                load(e2_w2[0:FW[f], :, f, :], d["e2_w2_t"][P * f:P * f + FW[f]])
            load(r_rel[:], d["r_rel"]); load(r_root[:], d["r_root"]); load(r_b[:], d["r_b"].unsqueeze(0))
            load(r_gamma[:], bcast(d["r_gamma"])); load(r_beta[:], bcast(d["r_beta"]))
            load(e3_gate[:], d["e3_gate"]); load(e3_gb[:], bcast(d["e3_gb"]))
            load(e3_w1[:], d["e3_w1"])
            load(e3_b1[:], d["e3_b1"])
            load(e3_w2[:], d["e3_w2"])
            load(e3_b2[:], d["e3_b2"])
            load(e3_gamma[:], bcast(d["e3_gamma"])); load(e3_beta[:], bcast(d["e3_beta"]))
            late = []
            for k in range(3):
                late.append((g_se[:, 32 * k:32 * k + 3], d["g_se_t"]))
                late.append((g_seb[32 * k:32 * k + 3, :], d["g_se_b"]))
            late.append((g_seb2[0:3, :], d["g_se_b"]))
            all_loads = 16 * (len(loads) + len(late))

            @block.sync
            def _(sp):
                for dst, src in loads:
                    sp.dma_start(dst, src).then_inc(S["weights_in"], 16)
                sp.wait_ge(S["se_zeroed"], 1)
                for dst, src in late:
                    sp.dma_start(dst, src).then_inc(S["weights_in"], 16)
                sp.wait_ge(S["weights_in"], all_loads)

            @block.gpsimd
            def _(pool):
                ch = Chain(pool, S["pool_own"])
                nc.gpsimd.memset(g_se[:], 0.0)
                nc.gpsimd.memset(g_seb2[:], 0.0)
                nc.gpsimd.memset(g_seb[:], 0.0).then_inc(S["se_zeroed"], 1)
                nc.gpsimd.memset(ident[:], 0.0)
                nc.gpsimd.memset(upper[:], 1.0)
                nc.gpsimd.memset(causal[:], 0.0)
                nc.gpsimd.memset(pick[:], 1.0e30)
                nc.gpsimd.memset(ones_row[:], 1.0)
                ch.link(nc.gpsimd.memset(minus_half[:], -0.5))
                nc.gpsimd.iota(iota32[:], [[1, E1]], base=0, channel_multiplier=0, allow_small_or_imprecise_dtypes=True)
                nc.gpsimd.affine_select(out=upper[:], in_=upper[:], compare_op=ALU.is_ge, fill=0.0,
                                        base=0, pattern=[[1, P]], channel_multiplier=-1)
                nc.gpsimd.affine_select(out=causal[:], in_=causal[:], compare_op=ALU.is_ge, fill=-1.0e30,
                                        base=0, pattern=[[-1, P]], channel_multiplier=1)
                ch.link(nc.gpsimd.affine_select(out=pick[:], in_=pick[:], compare_op=ALU.is_ge, fill=0.0, base=0,
                                                pattern=[[128, 8], [1, P]], channel_multiplier=-32))
                ch.link(nc.gpsimd.affine_select(out=pick[:], in_=pick[:], compare_op=ALU.is_ge, fill=0.0, base=31,
                                                pattern=[[-128, 8], [-1, P]], channel_multiplier=32))
                ch.link(nc.gpsimd.affine_select(out=ident[:], in_=ident[:], compare_op=ALU.not_equal, fill=1.0,
                                                base=0, pattern=[[-1, P]], channel_multiplier=1))
                nc.gpsimd.tensor_copy(ident_h[:], ident[:])
                pool.wait_ge(S["bn_var"], 1)
                nc.gpsimd.tensor_tensor(g_s[:], sm[0][:, 0, 0:2], minus_half[:, 0:2], ALU.pow).then_inc(S["bn_pow"], 1)

            @block.tensor
            def _(pe):
                pe.wait_ge(S["weights_in"], all_loads)
                nc.tensor.matmul(PS[0][:, 0, 0:2], gat_wt[:], gat_a[:], start=True, stop=True)
                for i in range(2):
                    mm = nc.tensor.matmul(PS[0][:, 1 + i, 0:P], work[0][:, 0, cols(i)], work[0][:, 1, 0:P],
                                          start=True, stop=True)
                mm.then_inc(S["folded"], 1)

            @block.scalar
            def _(act):
                act.wait_ge(S["weights_in"], all_loads)
                nc.scalar.activation(m_a[:], m_a[:], ACT.Exp).then_inc(S["a_exp"], 1)

            @block.vector
            def _(dve):
                ch = Chain(dve, S["dve_own"])
                dve.wait_ge(S["weights_in"], all_loads)
                bn = g_bn[:, :].rearrange("p (n k) -> p k n", k=4)
                nc.vector.tensor_scalar(sm[0][:, 0, 0:2], bn[:, 3, :], LN_EPS, None, ALU.add).then_inc(S["bn_var"], 1)
                nc.vector.tensor_scalar(m_taps[:], m_taps[:], 0.5, None, ALU.mult)
                nc.vector.tensor_scalar(m_convb[:], m_convb[:], 0.5, None, ALU.mult)
                nc.vector.tensor_scalar(g_seb2[:], g_seb2[:], 2.0, None, ALU.mult)
                nc.vector.tensor_scalar(g_half[:, 2:3], g_bh[:, 2:3], 0.5, None, ALU.mult)
                ch.link(nc.vector.tensor_tensor(g_half[:, 0:2], g_bi[:, 0:2], g_bh[:, 0:2], ALU.add))
                nc.vector.tensor_scalar(g_half[:, 0:2], g_half[:, 0:2], 0.5, None, ALU.mult)
                dve.wait_ge(S["a_exp"], 1)
                nc.vector.tensor_scalar(m_a[:], m_a[:], -1.0, None, ALU.mult)
                dve.wait_ge(S["bn_pow"], 1)
                ch.link(nc.vector.tensor_tensor(g_s[:], g_s[:], bn[:, 0, :], ALU.mult))
                ch.link(nc.vector.tensor_tensor(sm[0][:, 0, 2:4], bn[:, 2, :], g_s[:], ALU.mult))
                nc.vector.tensor_tensor(g_c[:], bn[:, 1, :], sm[0][:, 0, 2:4], ALU.subtract)
                dve.wait_ge(S["folded"], 1)
                ch.link(nc.vector.tensor_copy(gat_wa[:], PS[0][:, 0, 0:2]))
                nc.vector.tensor_copy(gat_wdst[:], gat_wa[:, 1:2].to_broadcast([P, P]))
                for i in range(2):
                    nc.vector.tensor_scalar(m_wol[:, i, :], PS[0][:, 1 + i, 0:P], m_norm[:, i:i + 1], None, ALU.mult)

        def norm_vector(dve, ch, k, src, dst, ready=None):
            for u in range(U):
                if ready:
                    ready(u)
                for t in range(T):
                    n = ch.mark(nc.vector.bn_stats(stats[u][:, t, :], src[u][:, t, :]))
                ch.wait(n)
                for t in range(T):
                    n = ch.mark(nc.vector.bn_aggr(mv[u][:, t, :], stats[u][:, t, :]))
                ch.wait(n)
                nc.vector.tensor_scalar(var[u][:], mv[u][:, :, 1], LN_EPS, None, ALU.add).then_inc(S["var"], 1)
            for u in range(U):
                dve.wait_ge(S["rstd"], nth(k, u))
                for t in range(T):
                    ins = nc.vector.tensor_scalar(dst[u][:, t, :], src[u][:, t, :], mv[u][:, t, 0:1],
                                                  rstd[u][:, t:t + 1], ALU.subtract, ALU.mult)
                ins.then_inc(S["normed"], 1)

        def rstd_gpsimd(pool, k):
            for u in range(U):
                pool.wait_ge(S["var"], nth(k, u))
                nc.gpsimd.tensor_tensor(rstd[u][:], var[u][:], minus_half[:], ALU.pow).then_inc(S["rstd"], 1)

        def turn_tensor(pe, k, src, ready):
            for u in range(U):
                ready(u)
                for t in range(T):
                    mm = nc.tensor.transpose(PS[u][:, 0, cols(t)], src(u)[:, t, :], ident[:])
                mm.then_inc(S["turned"], 1)

        def turn_scalar(act, k, dst, scale=None):
            for u in range(U):
                act.wait_ge(S["turned"], nth(k, u))
                if scale is None:
                    ins = nc.scalar.activation(dst(u), PS[u][:, 0, :], ACT.Copy)
                else:
                    ins = nc.scalar.activation(dst(u), PS[u][:, 0, :], ACT.Copy, scale=scale)
                ins.then_inc(S["chan"], 1)

        def top_index(dve, ch, u, n):
            for t in range(T):
                m = ch.mark(nc.vector.max(top[u][:, t, :], lg[u][:, t, 0:n]))
            ch.wait(m)
            for t in range(T):
                m = ch.mark(nc.vector.max_index(idx[u][:, t, :], top[u][:, t, :], lg[u][:, t, 0:n]))
            ch.wait(m)
            ch.link(nc.vector.tensor_copy(idxf[u][:], idx[u][:, :, 0:2]))

        def one_hot(dst, u, k, n):
            return nc.vector.tensor_tensor(dst[:, :, 0:n], iota32[:, 0:n].unsqueeze(1).to_broadcast([P, T, n]),
                                           idxf[u][:, :, k:k + 1].to_broadcast([P, T, n]), ALU.is_equal)

        def gat_sync(sp, turn):
            for u in range(U):
                sp.dma_start(x[u][:], d["x"][bass.ds(U * turn + u, 1)].rearrange("o (t p) c -> p (o t) c", p=P))\
                    .then_inc(S[f"x_in{u}"], 16)
                sp.dma_start(work[u][:, 9:13, :], d["adj"][bass.ds(U * turn + u, 1)].rearrange("o (t p) j -> p (o t) j", p=P))\
                    .then_inc(S[f"adj_in{u}"], 16)
            for u in range(U):
                sp.dma_start(adjT[u][:], d["adj_t"][bass.ds(U * turn + u, 1)].rearrange("o (t p) j -> p (o t) j", p=P))\
                    .then_inc(S[f"adjT_in{u}"], 16)

        def gat_tensor(pe):
            turn_tensor(pe, 0, lambda u: xh[u], lambda u: pe.wait_ge(S["normed"], nth(0, u)))
            for u in range(U):
                pe.wait_ge(S["chan"], nth(0, u))
                for t in range(T):
                    nc.tensor.matmul(PS[u][:, 1, cols(t)], xT[u][:, cols(t)], gat_w[:], start=True, stop=True)
                for t in range(T):
                    nc.tensor.matmul(PS[u][:, 2, t:t + 1], xT[u][:, cols(t)], gat_wa[:, 0:1], start=True, stop=True)
                nc.tensor.matmul(PS[u][:, 3, :], gat_wdst[:], xT[u][:], start=True, stop=True)\
                    .then_inc(S["gat_products"], 1)
            for it in range(T):
                for u in range(U):
                    pe.wait_ge(S["gat_p"], nth(it, u))
                    if it == 0:
                        pe.wait_ge(S["gat_h"], nth(0, u))
                    if it == 1:
                        pe.wait_ge(S["gat_src"], nth(0, u))
                    if it >= 2:
                        pe.wait_ge(S["gat_pT"], nth(it - 2, u))
                    for jt in range(T):
                        mm = nc.tensor.transpose(PS[u][:, 1 + it % 2, cols(jt)], work[u][:, it, cols(jt)], ident[:])
                    mm.then_inc(S["gat_p_turned"], 1)
            for it in range(T):
                for u in range(U):
                    pe.wait_ge(S["gat_pT"], nth(it, u))
                    for jt in range(T):
                        mm = nc.tensor.matmul(PS[u][:, 0, cols(it)], work[u][:, 4 + it, cols(jt)],
                                              work[u][:, 8, cols(jt)], start=(jt == 0), stop=(jt == T - 1))
                    mm.then_inc(S["gat_out"], 1)

        def gat_scalar(act):
            turn_scalar(act, 0, lambda u: xT[u][:])
            for u in range(U):
                act.wait_ge(S["gat_products"], nth(0, u))
                nc.scalar.activation(work[u][:, 8, :], PS[u][:, 1, :], ACT.Copy).then_inc(S["gat_h"], 1)
            for it in range(T):
                for u in range(U):
                    if it == 0:
                        act.wait_ge(S["gat_src"], nth(0, u))
                    nc.scalar.activation(work[u][:, it, :], PS[u][:, 3, :], ACT.Identity,
                                         bias=sm[u][:, 0, it:it + 1]).then_inc(S["gat_sum"], 1)
            for it in range(T):
                for u in range(U):
                    act.wait_ge(S["gat_max"], nth(it, u))
                    nc.scalar.activation(work[u][:, it, :], work[u][:, it, :], ACT.Exp,
                                         bias=sm[u][:, 1, it:it + 1], accum_out=sm[u][:, 2, it:it + 1])\
                        .then_inc(S["gat_p"], 1)

        def gat_vector(dve, ch):
            norm_vector(dve, ch, 0, x, xh, lambda u: dve.wait_ge(S[f"x_in{u}"], 16))
            for u in range(U):
                dve.wait_ge(S["gat_products"], nth(0, u))
                nc.vector.tensor_copy(sm[u][:, 0, 0:T], PS[u][:, 2, 0:T]).then_inc(S["gat_src"], 1)
            for it in range(T):
                for u in range(U):
                    e = work[u][:, it, :]
                    dve.wait_ge(S["gat_sum"], nth(it, u))
                    ch.link(nc.vector.scalar_tensor_tensor(out=e, in0=e, scalar=0.2, in1=e, op0=ALU.mult, op1=ALU.max))
                    dve.wait_ge(S["gat_penalty"], nth(0, u))
                    ch.link(nc.vector.tensor_tensor(e, e, work[u][:, 9 + it, :], ALU.add))
                    ch.link(nc.vector.tensor_reduce(sm[u][:, 3, it:it + 1], e, AX.X, ALU.max))
                    nc.vector.tensor_scalar(sm[u][:, 1, it:it + 1], sm[u][:, 3, it:it + 1], -1.0, None, ALU.mult)\
                        .then_inc(S["gat_max"], 1)
            for it in range(T):
                for u in range(U):
                    dve.wait_ge(S["gat_p_turned"], nth(it, u))
                    nc.vector.tensor_copy(work[u][:, 4 + it, :], PS[u][:, 1 + it % 2, :]).then_inc(S["gat_pT"], 1)
            for u in range(U):
                dve.wait_ge(S["gat_p"], nth(T - 1, u))
                ch.link(nc.vector.reciprocal(den[u][:], sm[u][:, 2, 0:T]))
                dve.wait_ge(S["gat_out"], nth(T - 1, u))
                for t in range(T):
                    ins = nc.vector.scalar_tensor_tensor(out=x[u][:, t, :], in0=PS[u][:, 0, cols(t)],
                                                         scalar=den[u][:, t:t + 1], in1=x[u][:, t, :],
                                                         op0=ALU.mult, op1=ALU.add)
                ins.then_inc(S["x"], 1)

        def gat_gpsimd(pool, ch):
            rstd_gpsimd(pool, 0)
            for u in range(U):
                pool.wait_ge(S[f"adj_in{u}"], 16)
                a = work[u][:, 9:13, :]
                nc.gpsimd.tensor_scalar(a, a, 0.0, NEG, ALU.is_le, ALU.mult).then_inc(S["gat_penalty"], 1)

        def states_of(u):
            return slot(u, 4, 2)[0:DST, :].rearrange("n (c m) -> n c m", c=T)

        def heads(ap):
            return ap.rearrange("p (k w) -> p k w", k=T * NHM)

        def mamba_tensor(pe):
            turn_tensor(pe, 1, lambda u: xh[u], lambda u: pe.wait_ge(S["normed"], nth(1, u)))
            for u in range(U):
                pe.wait_ge(S["chan"], nth(1, u))
                for i in range(3):
                    nc.tensor.matmul(PS[u][:, i, :], m_in[:, 256 + P * i:256 + P * (i + 1)], xT[u][:], start=True, stop=True)
                for c in range(T):
                    mm = nc.tensor.matmul(PS[u][:, 3, 4 * c:4 * c + 4], xT[u][:, cols(c)], m_in[:, 640:644],
                                          start=True, stop=True)
                mm.then_inc(S["m_projected"], 1)
            for u in range(U):
                pe.wait_ge(S["m_silu"], nth(0, u))
                for c in range(T):
                    for i in range(2):
                        nc.tensor.transpose(PS[u][:, c // 2, cols(2 * (c % 2) + i)], work[u][:, 6 + i, cols(c)], ident[:])
                for c in range(T):
                    nc.tensor.transpose(PS[u][:, 2, DST * c:DST * (c + 1)], work[u][0:DST, 8, cols(c)],
                                        ident[0:DST, 0:DST])
                pe.wait_ge(S["m_da"], nth(0, u))
                nc.tensor.matmul(PS[u][:, 3, 0:16], upper[:], sm[u][:, 1, :], start=True, stop=True)\
                    .then_inc(S["m_turned"], 1)
            for u in range(U):
                pe.wait_ge(S["m_x_tok"], nth(0, u))
                for c in range(T):
                    mm = nc.tensor.matmul(PS[u][:, 0, cols(c)], work[u][0:DST, 8, cols(c)], work[u][0:DST, 9, cols(c)],
                                          start=True, stop=True)
                mm.then_inc(S["m_cb"], 1)
            for c in range(T):
                for u in range(U):
                    if c == 0:
                        pe.wait_ge(S["m_cum"], nth(0, u))
                        pe.wait_ge(S["m_b_tok"], nth(0, u))
                    if c >= 2:
                        pe.wait_ge(S["m_diff"], nth(c - 2, u))
                    for h in range(NHM):
                        k = NHM * c + h
                        mm = nc.tensor.matmul(PS[u][:, 2 + c % 2, cols(h)], sm[u][:, 2, k:k + 1].to_broadcast([P, P]), ident[:],
                                              start=True, stop=True)
                    mm.then_inc(S["m_rows"], 1)
            for u in range(U):
                pe.wait_ge(S["m_xdd"], nth(0, u))
                for c in range(T - 1):
                    mm = nc.tensor.matmul(PS[u][0:DST, 2 + c // 2, 256 * (c % 2):256 * (c % 2 + 1)],
                                          work[u][:, 12, DST * c:DST * (c + 1)],
                                          slot(u, 6, 2)[:, 256 * c:256 * (c + 1)], start=True, stop=True)
                mm.then_inc(S["m_states"], 1)
            for u in range(U):
                pe.wait_ge(S["m_decays"], nth(0, u))
                for c in range(T):
                    for h in range(NHM):
                        k = NHM * c + h
                        mm = nc.tensor.matmul(PS[u][:, c // 2, 256 * (c % 2) + HDM * h:256 * (c % 2) + HDM * (h + 1)],
                                              slot(u, 0, 4)[:, P * k:P * (k + 1)],
                                              slot(u, 13, 2)[:, HDM * k:HDM * (k + 1)], start=True, stop=True)
                mm.then_inc(S["m_y_in"], 1)
                pe.wait_ge(S["m_scanned"], nth(0, u))
                for c in range(T):
                    mm = nc.tensor.matmul(PS[u][:, 2 + c // 2, 256 * (c % 2):256 * (c % 2 + 1)],
                                          work[u][0:DST, 9, cols(c)], states_of(u)[:, c, :], start=True, stop=True)
                mm.then_inc(S["m_y_off"], 1)
            for u in range(U):
                pe.wait_ge(S["m_y"], nth(0, u))
                for t in range(T):
                    mm = nc.tensor.matmul(PS[u][:, t // 2, 256 * (t % 2):256 * (t % 2 + 1)], xT[u][:, cols(t)],
                                          m_in[:, 0:256], start=True, stop=True)
                mm.then_inc(S["m_z"], 1)
            for u in range(U):
                pe.wait_ge(S["m_gated"], nth(0, u))
                for i in range(2):
                    for t in range(T):
                        mm = nc.tensor.transpose(PS[u][:, 2 + i, cols(t)], slot(u, 6, 2)[:, 256 * t + P * i:256 * t + P * (i + 1)],
                                                 ident[:])
                mm.then_inc(S["m_y_turned"], 1)
            for u in range(U):
                pe.wait_ge(S["m_y_chan"], nth(0, u))
                for t in range(T):
                    for i in range(2):
                        mm = nc.tensor.matmul(PS[u][:, 0, cols(t)], work[u][:, i, cols(t)], m_wol[:, i, :],
                                              start=(i == 0), stop=(i == 1))
                mm.then_inc(S["m_out"], 1)

        def mamba_scalar(act):
            turn_scalar(act, 1, lambda u: xT[u][:])
            for u in range(U):
                act.wait_ge(S["m_dt_abs"], nth(0, u))
                nc.scalar.activation(sm[u][:, 3, :], sm[u][:, 2, :], ACT.Exp).then_inc(S["m_dt_exp"], 1)
            for u in range(U):
                act.wait_ge(S["m_dt_exp"], nth(0, u))
                nc.scalar.activation(sm[u][:, 4, :], sm[u][:, 3, :], ACT.Ln, bias=1.0).then_inc(S["m_dt_ln"], 1)
            for u in range(U):
                act.wait_ge(S["m_conv"], nth(0, u))
                nc.scalar.activation(work[u][:, 3:6, :], work[u][:, 0:3, :], ACT.Tanh).then_inc(S["m_tanh"], 1)
            for u in range(U):
                act.wait_ge(S["m_turned"], nth(0, u))
                nc.scalar.activation(work[u][:, 10:12, :], PS[u][:, 0:2, :], ACT.Copy).then_inc(S["m_x_tok"], 1)
                nc.scalar.activation(work[u][:, 12, 0:256], PS[u][:, 2, 0:256], ACT.Copy).then_inc(S["m_b_tok"], 1)
            for u in range(U):
                act.wait_ge(S["m_ends"], nth(0, u))
                nc.scalar.activation(sm[u][:, 5:8, :], sm[u][:, 5:8, :], ACT.Exp).then_inc(S["m_ends_exp"], 1)
            for u in range(U):
                act.wait_ge(S["m_clamped"], nth(0, u))
                nc.scalar.activation(work[u][:, 0:4, :], work[u][:, 0:4, :], ACT.Exp).then_inc(S["m_exp"], 1)
            for u in range(U):
                act.wait_ge(S["m_z"], nth(0, u))
                nc.scalar.activation(work[u][:, 13:15, :], PS[u][:, 0:2, :], ACT.Tanh, scale=0.5).then_inc(S["m_z_tanh"], 1)
            for u in range(U):
                act.wait_ge(S["m_gated"], nth(0, u))
                for t in range(T):
                    y_t = slot(u, 6, 2)[:, 256 * t:256 * (t + 1)]
                    ins = nc.scalar.activation(slot(u, 10, 2)[:, 256 * t:256 * (t + 1)], y_t, ACT.Square,
                                               accum_out=sm[u][:, 0, t:t + 1])
                ins.then_inc(S["m_square"], 1)
                act.wait_ge(S["m_y_turned"], nth(0, u))
                nc.scalar.activation(work[u][:, 0:2, :], PS[u][:, 2:4, :], ACT.Copy).then_inc(S["m_y_chan"], 1)

        def mamba_vector(dve, ch):
            norm_vector(dve, ch, 1, x, xh, lambda u: dve.wait_ge(S["x"], nth(0, u)))
            for u in range(U):
                dve.wait_ge(S["m_projected"], nth(0, u))
                ch.link(nc.vector.tensor_tensor(sm[u][:, 0, :].rearrange("p (c h) -> p c h", c=T),
                                                PS[u][:, 3, 0:16].rearrange("p (c h) -> p c h", c=T),
                                                m_dtb[:].unsqueeze(1).to_broadcast([P, T, NHM]), ALU.add))
                nc.vector.scalar_tensor_tensor(out=sm[u][:, 2, :], in0=sm[u][:, 0, :], scalar=-1.0, in1=sm[u][:, 0, :],
                                               op0=ALU.mult, op1=ALU.min).then_inc(S["m_dt_abs"], 1)
            for u in range(U):
                for i in range(3):
                    m = ch.mark(nc.vector.tensor_scalar(work[u][:, i, :], PS[u][:, i, :], m_taps[:, i, 3:4], m_convb[:, i:i + 1],
                                                        ALU.mult, ALU.add))
                for k in (2, 1, 0):
                    ch.wait(m)
                    for i in range(3):
                        s = 3 - k
                        ins = nc.vector.scalar_tensor_tensor(
                            out=work[u][:, i, s:N], in0=PS[u][:, i, 0:N - s], scalar=m_taps[:, i, k:k + 1],
                            in1=work[u][:, i, s:N], op0=ALU.mult, op1=ALU.add)
                        if k > 0 or i < 2:
                            m = ch.mark(ins)
                ins.then_inc(S["m_conv"], 1)
            for u in range(U):
                dve.wait_ge(S["m_dt_ln"], nth(0, u))
                ch.link(nc.vector.scalar_tensor_tensor(out=sm[u][:, 0, :], in0=sm[u][:, 0, :], scalar=0.0,
                                                       in1=sm[u][:, 4, :], op0=ALU.max, op1=ALU.add))
                nc.vector.tensor_tensor(sm[u][:, 1, :].rearrange("p (c h) -> p c h", c=T),
                                        sm[u][:, 0, :].rearrange("p (c h) -> p c h", c=T),
                                        m_a[:].unsqueeze(1).to_broadcast([P, T, NHM]), ALU.mult).then_inc(S["m_da"], 1)
            for u in range(U):
                dve.wait_ge(S["m_tanh"], nth(0, u))
                for tanh, conv, dst in ((work[u][:, 3:5, :], work[u][:, 0:2, :], work[u][:, 6:8, :]),
                                        (work[u][0:64, 5, :], work[u][0:64, 2, :], work[u][0:64, 8, :]),
                                        (work[u][64:P, 5, :], work[u][64:P, 2, :], work[u][0:64, 9, :])):
                    ins = nc.vector.scalar_tensor_tensor(out=dst, in0=tanh, scalar=1.0, in1=conv, op0=ALU.add, op1=ALU.mult)
                ins.then_inc(S["m_silu"], 1)
            for u in range(U):
                dve.wait_ge(S["m_turned"], nth(0, u))
                nc.vector.tensor_copy(sm[u][:, 2, :], PS[u][:, 3, 0:16]).then_inc(S["m_cum"], 1)
                dve.wait_ge(S["m_x_tok"], nth(0, u))
                m = ch.mark(nc.vector.tensor_tensor(heads(slot(u, 13, 2)), heads(slot(u, 10, 2)),
                                                    sm[u][:, 0, :].unsqueeze(2).to_broadcast([P, 16, HDM]), ALU.mult))
            for c in range(T):
                for u in range(U):
                    dve.wait_ge(S["m_rows"], nth(c, u))
                    rows_ps = PS[u][:, 2 + c % 2, :].rearrange("p (h l) -> p h l", h=NHM)
                    if c == 0:
                        dve.wait_ge(S["m_cum"], nth(0, u))
                    m = ch.mark(nc.vector.tensor_copy(sm[u][:, 7, NHM * c:NHM * (c + 1)], rows_ps[:, :, P - 1]))
                    nc.vector.tensor_tensor(work[u][:, c, :].rearrange("p (h l) -> p h l", h=NHM), rows_ps,
                                            sm[u][:, 2, NHM * c:NHM * (c + 1)].unsqueeze(2).to_broadcast([P, NHM, P]),
                                            ALU.subtract).then_inc(S["m_diff"], 1)
            for u in range(U):
                dve.wait_ge(S["m_diff"], nth(T - 1, u))
                nc.vector.tensor_copy(sm[u][:, 6, :], sm[u][:, 2, :])
                ch.link(nc.vector.tensor_tensor(sm[u][:, 5, :], sm[u][:, 7, :], sm[u][:, 2, :], ALU.subtract))
                nc.vector.tensor_scalar(sm[u][:, 5, :], sm[u][:, 5, :], 0.0, None, ALU.min).then_inc(S["m_ends"], 1)
                nc.vector.tensor_scalar(work[u][:, 0:4, :], work[u][:, 0:4, :], 0.0, None, ALU.min).then_inc(S["m_clamped"], 1)
            for u in range(U):
                dve.wait_ge(S["m_cb"], nth(0, u))
                nc.vector.tensor_tensor(tok(work[u][:, 4, :]), PS[u][:, 0, :].rearrange("p (c l) -> p c l", c=T),
                                        upper[:].unsqueeze(1).to_broadcast([P, T, P]), ALU.mult).then_inc(S["m_cb_masked"], 1)
                dve.wait_ge(S["m_ends_exp"], nth(0, u))
                nc.vector.tensor_tensor(heads(slot(u, 6, 2)), heads(slot(u, 13, 2)),
                                        sm[u][:, 5, :].unsqueeze(2).to_broadcast([P, 16, HDM]), ALU.mult)\
                    .then_inc(S["m_xdd"], 1)
            for u in range(U):
                dve.wait_ge(S["m_exp"], nth(0, u))
                dve.wait_ge(S["m_cb_masked"], nth(0, u))
                decays = slot(u, 0, 4).rearrange("p (c h l) -> p c h l", c=T, h=NHM)
                nc.vector.tensor_tensor(decays, decays, tok(work[u][:, 4, :]).unsqueeze(2).to_broadcast([P, T, NHM, P]),
                                        ALU.mult).then_inc(S["m_decays"], 1)
            for u in range(U):
                dve.wait_ge(S["m_decays"], nth(0, u))
                st = states_of(u)
                m = ch.mark(nc.vector.memset(st[:, 0, :], 0.0))
                dve.wait_ge(S["m_states"], nth(0, u))
                ch.link(nc.vector.tensor_copy(st[:, 1, :], PS[u][0:DST, 2, 0:256]))
                for c in (1, 2):
                    ch.link(nc.vector.tensor_tensor(st[:, c + 1, :].rearrange("n (h w) -> n h w", h=NHM),
                                                    st[:, c, :].rearrange("n (h w) -> n h w", h=NHM),
                                                    sm[u][0:DST, 7, NHM * c:NHM * (c + 1)].unsqueeze(2).to_broadcast([DST, NHM, HDM]),
                                                    ALU.mult))
                    ins = nc.vector.tensor_tensor(st[:, c + 1, :], st[:, c + 1, :],
                                                  PS[u][0:DST, 2 + c // 2, 256 * (c % 2):256 * (c % 2 + 1)], ALU.add)
                    if c == 1:
                        ch.link(ins)
                ins.then_inc(S["m_scanned"], 1)
            for u in range(U):
                y = slot(u, 6, 2)
                dve.wait_ge(S["m_y_off"], nth(0, u))
                ch.link(nc.vector.tensor_tensor(heads(y), PS[u][:, 2:4, :].rearrange("p b (k w) -> p (b k) w", w=HDM),
                                                sm[u][:, 6, :].unsqueeze(2).to_broadcast([P, 16, HDM]), ALU.mult))
                ch.link(nc.vector.tensor_tensor(work[u][:, 6:8, :], work[u][:, 6:8, :], PS[u][:, 0:2, :], ALU.add))
                dve.wait_ge(S["m_skip"], nth(0, u))
                nc.vector.tensor_tensor(y, y, slot(u, 10, 2), ALU.add).then_inc(S["m_y"], 1)
            for u in range(U):
                dve.wait_ge(S["m_z_tanh"], nth(0, u))
                gate = work[u][:, 13:15, :]
                ch.link(nc.vector.scalar_tensor_tensor(out=gate, in0=gate, scalar=1.0, in1=PS[u][:, 0:2, :],
                                                       op0=ALU.add, op1=ALU.mult))
                nc.vector.scalar_tensor_tensor(out=work[u][:, 6:8, :], in0=work[u][:, 6:8, :], scalar=0.5, in1=gate,
                                               op0=ALU.mult, op1=ALU.mult).then_inc(S["m_gated"], 1)
            for u in range(U):
                dve.wait_ge(S["m_square"], nth(0, u))
                nc.vector.tensor_scalar(den[u][:], sm[u][:, 0, 0:T], 1.0 / 256, LN_EPS, ALU.mult, ALU.add)\
                    .then_inc(S["m_mean_sq"], 1)
            for u in range(U):
                dve.wait_ge(S["m_rstd"], nth(0, u))
                dve.wait_ge(S["m_out"], nth(0, u))
                for t in range(T):
                    ins = nc.vector.scalar_tensor_tensor(out=x[u][:, t, :], in0=PS[u][:, 0, cols(t)], scalar=den2[u][:, t:t + 1],
                                                         in1=x[u][:, t, :], op0=ALU.mult, op1=ALU.add)
                ins.then_inc(S["x"], 1)

        def mamba_gpsimd(pool, ch):
            rstd_gpsimd(pool, 1)
            for u in range(U):
                pool.wait_ge(S["normed"], nth(1, u))
                nc.gpsimd.tensor_tensor(x[u][:], x[u][:], m_blin[:].unsqueeze(1).to_broadcast([P, T, P]), ALU.add)
            for u in range(U):
                pool.wait_ge(S["m_xdd"], nth(0, u))
                v = slot(u, 10, 2).rearrange("p (c h w) -> p c h w", c=T, h=NHM)
                nc.gpsimd.tensor_tensor(v, v, m_d[:].unsqueeze(1).unsqueeze(3).to_broadcast([P, T, NHM, HDM]), ALU.mult)\
                    .then_inc(S["m_skip"], 1)
            for u in range(U):
                pool.wait_ge(S["m_mean_sq"], nth(0, u))
                nc.gpsimd.tensor_tensor(den2[u][:], den[u][:], minus_half[:], ALU.pow).then_inc(S["m_rstd"], 1)


        def gcn_tensor(pe):
            for u in range(U):
                pe.wait_ge(S["normed"], nth(2, u))
                pe.wait_ge(S[f"adjT_in{u}"], 16)
                for t in range(T):
                    mm = nc.tensor.matmul(PS[u][:, 0, :], xh[u][:, t, :], adjT[u][:, t, :], start=(t == 0), stop=(t == T - 1))
                mm.then_inc(S["gcn_sum"], 1)
            for u in range(U):
                pe.wait_ge(S["gcn_chan"], nth(0, u))
                for t in range(T):
                    nc.tensor.matmul(PS[u][:, 1, cols(t)], ones_row[:], gcn_b[:], start=True, stop=False)
                    mm = nc.tensor.matmul(PS[u][:, 1, cols(t)], work[u][:, 0, cols(t)], gcn_w[:], start=False, stop=True)
                mm.then_inc(S["gcn_out"], 1)

        def gcn_scalar(act):
            for u in range(U):
                act.wait_ge(S["gcn_sum"], nth(0, u))
                nc.scalar.activation(work[u][:, 0, :], PS[u][:, 0, :], ACT.Copy).then_inc(S["gcn_chan"], 1)

        def gcn_vector(dve, ch):
            norm_vector(dve, ch, 2, x, xh, lambda u: dve.wait_ge(S["x"], nth(1, u)))
            for u in range(U):
                dve.wait_ge(S["gcn_out"], nth(0, u))
                nc.vector.tensor_tensor(x[u][:], x[u][:], tok(PS[u][:, 1, :]), ALU.add).then_inc(S["x"], 1)

        def gcn_gpsimd(pool, ch):
            rstd_gpsimd(pool, 2)

        G1 = E1 // 4

        def not_chosen(u):
            return work[u][0:E1, 9, 0:N // 2].bitcast(BF16)

        def top1_tensor(pe):
            turn_tensor(pe, 2, lambda u: xh[u], lambda u: pe.wait_ge(S["normed"], nth(3, u)))
            for u in range(U):
                pe.wait_ge(S["chan"], nth(2, u))
                for t in range(T):
                    mm = nc.tensor.matmul(PS[u][:, 1, E1 * t:E1 * (t + 1)], xT[u][:, cols(t)], e1_router[:], start=True, stop=True)
                mm.then_inc(S["e1_logits"], 1)
            for u in range(U):
                pe.wait_ge(S["e1_hot"], nth(0, u))
                for t in range(T):
                    mm = nc.tensor.transpose(PS[u][0:E1, 2, cols(t)], oh[u][:, t, :], ident[:])
                mm.then_inc(S["e1_hot_turned"], 1)
            for g in range(G1):
                for u in range(U):
                    if g == 0:
                        pe.wait_ge(S["e1_not_chosen"], nth(0, u))
                    else:
                        if g >= 2:
                            pe.wait_ge(S["e1_hidden"], nth(g - 2, u))
                    b = 3 * (g % 2)
                    nc.tensor.matmul(PS[u][:, b, :], e1_w1[:, g, :], xT[u][:], start=True, stop=False)
                    nc.tensor.matmul(PS[u][:, b, :], pick[:, g, :], not_chosen(u), start=False, stop=True)\
                        .then_inc(S["e1_up"], 1)
            for u in range(U):
                pe.wait_ge(S["e1_hidden"], nth(G1 - 1, u))
                for t in range(T):
                    nc.tensor.matmul(PS[u][:, 1, cols(t)], work[u][0:E1, 8, cols(t)], e1_b2[:], start=True, stop=False)
                    for g in range(G1):
                        mm = nc.tensor.matmul(PS[u][:, 1, cols(t)], work[u][:, g, cols(t)], e1_w2[:, g, :],
                                              start=False, stop=(g == G1 - 1))
                mm.then_inc(S["e1_out"], 1)

        def top1_scalar(act):
            turn_scalar(act, 2, lambda u: xT[u][:])
            for g in range(G1):
                for u in range(U):
                    act.wait_ge(S["e1_up"], nth(g, u))
                    nc.scalar.activation(work[u][:, g, :], PS[u][:, 3 * (g % 2), :], ACT.Relu, bias=e1_b1[:, g:g + 1])\
                        .then_inc(S["e1_hidden"], 1)

        def top1_vector(dve, ch):
            norm_vector(dve, ch, 3, x, xh, lambda u: dve.wait_ge(S["x"], nth(2, u)))
            for u in range(U):
                dve.wait_ge(S["e1_logits"], nth(0, u))
                ch.link(nc.vector.tensor_tensor(lg[u][:], PS[u][:, 1, 0:T * E1].rearrange("p (t e) -> p t e", t=T),
                                                e1_rb[:].unsqueeze(1).to_broadcast([P, T, E1]), ALU.add))
                top_index(dve, ch, u, E1)
                one_hot(oh[u], u, 0, E1).then_inc(S["e1_hot"], 1)
            for u in range(U):
                dve.wait_ge(S["e1_hot_turned"], nth(0, u))
                nc.vector.tensor_copy(work[u][0:E1, 8, :], PS[u][0:E1, 2, :])
                nc.vector.tensor_scalar(not_chosen(u), PS[u][0:E1, 2, :], 1.0, None, ALU.subtract)\
                    .then_inc(S["e1_not_chosen"], 1)
            for u in range(U):
                dve.wait_ge(S["e1_out"], nth(0, u))
                nc.vector.scalar_tensor_tensor(out=x[u][:], in0=tok(PS[u][:, 1, :]), scalar=0.0, in1=x[u][:],
                                               op0=ALU.max, op1=ALU.add).then_inc(S["x"], 1)

        def top1_gpsimd(pool, ch):
            rstd_gpsimd(pool, 3)

        SE = 96

        def gru_tensor(pe):
            turn_tensor(pe, 3, lambda u: xh[u], lambda u: pe.wait_ge(S["normed"], nth(4, u)))
            for u in range(U):
                pe.wait_ge(S["chan"], nth(3, u))
                nc.tensor.matmul(PS[u][:, 1, :], g_c1[:], xT[u][:], start=True, stop=True).then_inc(S["g_conv1"], 1)
                nc.tensor.matmul(PS[u][0:SE, 2, :], g_se[:], xT[u][:], start=True, stop=True).then_inc(S["g_struct"], 1)
                for t in range(T):
                    nc.tensor.matmul(PS[u][:, 3, cols(t)], ones_row[:], g_msgb[:], start=True, stop=False)
                    mm = nc.tensor.matmul(PS[u][:, 3, cols(t)], xT[u][:, cols(t)], g_msg[:], start=False, stop=True)
                mm.then_inc(S["g_msg"], 1)
            for u in range(U):
                pe.wait_ge(S["g_padded"], nth(0, u))
                pe.wait_ge(S["g_hidden"], nth(0, u))
                for k in range(TAPS):
                    mm = nc.tensor.matmul(PS[u][:, 0, :], g_c2[:, k, :], slot(u, 0, 2)[:, k:k + N],
                                          start=(k == 0), stop=(k == TAPS - 1))
                mm.then_inc(S["g_conv2"], 1)
            for t in range(T):
                for u in range(U):
                    if t == 0:
                        pe.wait_ge(S["g_factors"], nth(0, u))
                    if t >= 2:
                        pe.wait_ge(S["g_near"], nth(t - 2, u))
                    nc.tensor.matmul(PS[u][:, 1 + t % 2, :], work[u][0:SE, 2, cols(t)], work[u][0:SE, 3, :],
                                     start=True, stop=True).then_inc(S["g_dist"], 1)
            for u in range(U):
                pe.wait_ge(S["g_affinity"], nth(T - 1, u))
                pe.wait_ge(S["g_msg_tok"], nth(0, u))
                for t in range(T):
                    mm = nc.tensor.matmul(PS[u][:, 3, :], work[u][:, 4, cols(t)], work[u][:, 6 + t, :],
                                          start=(t == 0), stop=(t == T - 1))
                mm.then_inc(S["g_received"], 1)
            for u in range(U):
                pe.wait_ge(S["g_conv_out"], nth(0, u))
                pe.wait_ge(S["g_received_sb"], nth(0, u))
                for g in range(3):
                    w = slice(P * g, P * (g + 1))
                    nc.tensor.matmul(PS[u][:, g, :], g_ih[:, 0, w], work[u][:, 5, :], start=True, stop=False)
                    nc.tensor.matmul(PS[u][:, g, :], g_ih[:, 1, w], work[u][:, 10, :], start=False, stop=(g == 2))
                    mm = nc.tensor.matmul(PS[u][:, g if g < 2 else 3, :], g_hh[:, w], xT[u][:], start=(g == 2), stop=True)
                mm.then_inc(S["g_gates"], 1)
            for u in range(U):
                pe.wait_ge(S["g_new"], nth(0, u))
                for t in range(T):
                    mm = nc.tensor.transpose(PS[u][:, 0, cols(t)], work[u][:, 1, cols(t)], ident[:])
                mm.then_inc(S["g_new_tok"], 1)

        def gru_scalar(act):
            turn_scalar(act, 3, lambda u: xT[u][:])
            for u in range(U):
                act.wait_ge(S["g_conv1"], nth(0, u))
                nc.scalar.activation(slot(u, 0, 2)[:, PAD:PAD + N], PS[u][:, 1, :], ACT.Relu, bias=g_c[:, 0:1],
                                     scale=g_s[:, 0:1]).then_inc(S["g_hidden"], 1)
                act.wait_ge(S["g_struct"], nth(0, u))
                act.wait_ge(S["g_padded"], nth(0, u))
                nc.scalar.activation(work[u][0:32, 2, :], PS[u][0:32, 2, :], ACT.Identity, bias=g_seb[0:32, :])
                nc.scalar.activation(work[u][32:64, 2, :], PS[u][32:64, 2, :], ACT.Square, bias=g_seb[32:64, :])
                nc.scalar.activation(work[u][0:32, 3, :], PS[u][0:32, 2, :], ACT.Identity, bias=g_seb2[:], scale=2.0)
                nc.scalar.activation(work[u][64:SE, 3, :], PS[u][64:SE, 2, :], ACT.Square, bias=g_seb[64:SE, :])\
                    .then_inc(S["g_factors"], 1)
            for u in range(U):
                act.wait_ge(S["g_msg"], nth(0, u))
                nc.scalar.activation(work[u][:, 4, :], PS[u][:, 3, :], ACT.Relu).then_inc(S["g_msg_tok"], 1)
            for t in range(T):
                for u in range(U):
                    act.wait_ge(S["g_dist"], nth(t, u))
                    nc.scalar.activation(work[u][:, 6 + t, :], PS[u][:, 1 + t % 2, :], ACT.Exp).then_inc(S["g_near"], 1)
            for u in range(U):
                act.wait_ge(S["g_conv_sum"], nth(0, u))
                nc.scalar.activation(work[u][:, 5, :], work[u][:, 5, :], ACT.Relu, bias=g_c[:, 1:2]).then_inc(S["g_conv_out"], 1)
                act.wait_ge(S["g_received"], nth(0, u))
                nc.scalar.activation(work[u][:, 10, :], PS[u][:, 3, :], ACT.Copy).then_inc(S["g_received_sb"], 1)
            for u in range(U):
                act.wait_ge(S["g_gates"], nth(0, u))
                nc.scalar.activation(work[u][:, 13, :], PS[u][:, 3, :], ACT.Identity, bias=g_half[:, 2:3], scale=0.5)
                nc.scalar.activation(work[u][:, 11, :], PS[u][:, 0, :], ACT.Tanh, bias=g_half[:, 0:1], scale=0.5)\
                    .then_inc(S["g_r"], 1)
                nc.scalar.activation(work[u][:, 12, :], PS[u][:, 1, :], ACT.Tanh, bias=g_half[:, 1:2], scale=0.5)\
                    .then_inc(S["g_z"], 1)
            for u in range(U):
                act.wait_ge(S["g_n_sum"], nth(0, u))
                nc.scalar.activation(work[u][:, 14, :], work[u][:, 13, :], ACT.Tanh, bias=g_bi[:, 2:3]).then_inc(S["g_n"], 1)

        def gru_vector(dve, ch):
            norm_vector(dve, ch, 4, x, xh, lambda u: dve.wait_ge(S["x"], nth(3, u)))
            for t in range(T):
                for u in range(U):
                    dve.wait_ge(S["g_near"], nth(t, u))
                    nc.vector.tensor_tensor(work[u][:, 6 + t, :], work[u][:, 6 + t, :], adjT[u][:, t, :], ALU.mult)\
                        .then_inc(S["g_affinity"], 1)
            for u in range(U):
                dve.wait_ge(S["g_conv2"], nth(0, u))
                nc.vector.scalar_tensor_tensor(out=work[u][:, 5, :], in0=PS[u][:, 0, :], scalar=g_s[:, 1:2], in1=xT[u][:],
                                               op0=ALU.mult, op1=ALU.add).then_inc(S["g_conv_sum"], 1)
            for u in range(U):
                h_n = work[u][:, 13, :]
                dve.wait_ge(S["g_r"], nth(0, u))
                ch.link(nc.vector.scalar_tensor_tensor(out=h_n, in0=work[u][:, 11, :], scalar=1.0, in1=h_n,
                                                       op0=ALU.add, op1=ALU.mult))
                nc.vector.tensor_tensor(h_n, h_n, PS[u][:, 2, :], ALU.add).then_inc(S["g_n_sum"], 1)
            for u in range(U):
                diff = work[u][:, 0, :]
                dve.wait_ge(S["g_n"], nth(0, u))
                ch.link(nc.vector.tensor_tensor(diff, xT[u][:], work[u][:, 14, :], ALU.subtract))
                dve.wait_ge(S["g_z"], nth(0, u))
                ch.link(nc.vector.scalar_tensor_tensor(out=diff, in0=work[u][:, 12, :], scalar=1.0, in1=diff,
                                                       op0=ALU.add, op1=ALU.mult))
                nc.vector.scalar_tensor_tensor(out=work[u][:, 1, :], in0=diff, scalar=0.5, in1=work[u][:, 14, :],
                                               op0=ALU.mult, op1=ALU.add).then_inc(S["g_new"], 1)
            for u in range(U):
                dve.wait_ge(S["g_new_tok"], nth(0, u))
                nc.vector.tensor_tensor(x[u][:], x[u][:], tok(PS[u][:, 0, :]), ALU.add).then_inc(S["x"], 1)

        def gru_gpsimd(pool, ch):
            rstd_gpsimd(pool, 4)
            for u in range(U):
                pool.wait_ge(S["normed"], nth(4, u))
                nc.gpsimd.memset(slot(u, 0, 2)[:, 0:PAD], 0.0)
                ch.link(nc.gpsimd.memset(slot(u, 0, 2)[:, PAD + N:PAD + N + PAD], 0.0))
                ch.link(nc.gpsimd.memset(work[u][64:SE, 2, :], -1.0))
                nc.gpsimd.memset(work[u][32:64, 3, :], -1.0).then_inc(S["g_padded"], 1)
                pool.wait_ge(S["g_padded"], nth(0, u))

        def route_vector(dve, ch, r, n, logits, extra):
            for u in range(U):
                logits(u)
                top_index(dve, ch, u, n)
                nc.vector.tensor_tensor(wts[u][:, :, 0:n], lg[u][:, :, 0:n], top[u][:, :, 0:1].to_broadcast([P, T, n]),
                                        ALU.subtract).then_inc(S["route_diff"], 1)
            for u in range(U):
                one_hot(oh[u], u, 0, n)
                ch.link(one_hot(oh2[u], u, 1, n))
                ch.link(nc.vector.tensor_tensor(oh[u][:, :, 0:n], oh[u][:, :, 0:n], oh2[u][:, :, 0:n], ALU.add))
                w = wts[u][:, :, 0:n]
                dve.wait_ge(S["route_exp"], nth(r, u))
                nc.vector.tensor_reduce(den2[u][:], w, AX.X, ALU.add)
                ch.link(nc.vector.tensor_tensor(oh[u][:, :, 0:n], w, oh[u][:, :, 0:n], ALU.mult))
                ch.link(nc.vector.tensor_reduce(den[u][:], oh[u][:, :, 0:n], AX.X, ALU.add))
                if extra:
                    ch.link(nc.vector.scalar_tensor_tensor(out=den[u][:], in0=den2[u][:], scalar=extra, in1=den[u][:],
                                                           op0=ALU.mult, op1=ALU.add))
                ch.link(nc.vector.reciprocal(den[u][:], den[u][:]))
                nc.vector.tensor_tensor(w, oh[u][:, :, 0:n], den[u][:].unsqueeze(2).to_broadcast([P, T, n]), ALU.mult)\
                    .then_inc(S["routed"], 1)

        def route_scalar(act, r, n):
            for u in range(U):
                act.wait_ge(S["route_diff"], nth(r, u))
                nc.scalar.activation(wts[u][:, :, 0:n], wts[u][:, :, 0:n], ACT.Exp).then_inc(S["route_exp"], 1)

        def rms_scalar(act, k, src_ready):
            for u in range(U):
                src_ready(u)
                for t in range(T):
                    ins = nc.scalar.activation(work[u][:, 3, cols(t)], xh[u][:, t, :], ACT.Square,
                                               accum_out=sm[u][:, 0, t:t + 1])
                ins.then_inc(S["a_squares"], 1)

        def rms_vector(dve, k):
            for u in range(U):
                dve.wait_ge(S["a_squares"], nth(k, u))
                nc.vector.tensor_scalar(den[u][:], sm[u][:, 0, 0:T], 1.0 / P, RMS_EPS, ALU.mult, ALU.add)\
                    .then_inc(S["a_mean_sq"], 1)
            for u in range(U):
                dve.wait_ge(S["a_rms"], nth(k, u))
                nc.vector.tensor_tensor(tok(work[u][:, 0, :]), xh[u][:], den2[u][:].unsqueeze(2).to_broadcast([P, T, P]),
                                        ALU.mult).then_inc(S["a_normed"], 1)

        def rms_gpsimd(pool, k):
            for u in range(U):
                pool.wait_ge(S["a_mean_sq"], nth(k, u))
                nc.gpsimd.tensor_tensor(den2[u][:], den[u][:], minus_half[:], ALU.pow).then_inc(S["a_rms"], 1)

        def attn_tensor(pe):
            turn_tensor(pe, 4, lambda u: tok(work[u][:, 0, :]), lambda u: pe.wait_ge(S["a_normed"], nth(0, u)))
            for u in range(U):
                pe.wait_ge(S["chan"], nth(4, u))
                for i in range(4):
                    mm = nc.tensor.matmul(PS[u][:, i, :], a_qk[:, i, :], work[u][:, 1, :], start=True, stop=True)
                mm.then_inc(S["a_qk"], 1)
            for u in range(U):
                pe.wait_ge(S["a_parts"], nth(0, u))
                for t in range(T):
                    mm = nc.tensor.matmul(PS[u][:, 0, 64 * t:64 * (t + 1)], work[u][:, 1, cols(t)], a_v[:],
                                          start=True, stop=True)
                mm.then_inc(S["a_v_ps"], 1)
            for t in range(T):
                w = P * (t + 1)
                for u in range(U):
                    if t == 0:
                        pe.wait_ge(S["a_rotated"], nth(0, u))
                        pe.wait_ge(S["a_v"], nth(0, u))
                    else:
                        pe.wait_ge(S["a_y"], nth(t - 1, u))
                    for h in range(NHA):
                        r = slice(HDA * h, HDA * (h + 1))
                        nc.tensor.matmul(PS[u][:, h, 0:w], work[u][r, 2, cols(t)], work[u][r, 4, 0:w], start=True, stop=False)
                        mm = nc.tensor.matmul(PS[u][:, h, w - P:w], ident_h[:], causal[:], start=False, stop=True)
                    mm.then_inc(S["a_scores"], 1)
                for u in range(U):
                    pe.wait_ge(S["a_p"], nth(t, u))
                    for s in range(t + 1):
                        for h in range(NHA):
                            mm = nc.tensor.transpose(PS[u][:, s, cols(h)], work[u][:, 7 + h, cols(s)], ident[:])
                    mm.then_inc(S["a_p_turned"], 1)
                for u in range(U):
                    pe.wait_ge(S["a_pT"], nth(t, u))
                    for h in range(NHA):
                        for s in range(t + 1):
                            kv = 64 * s + HDA * (h // 2)
                            mm = nc.tensor.matmul(PS[u][:, 0, HDA * h:HDA * (h + 1)], work[u][:, 11 + s, cols(h)],
                                                  work[u][:, 6, kv:kv + HDA], start=(s == 0), stop=(s == t))
                    mm.then_inc(S["a_pv"], 1)
            turn_tensor(pe, 5, lambda u: tok(work[u][:, 5, :]), lambda u: pe.wait_ge(S["a_y"], nth(T - 1, u)))
            for u in range(U):
                pe.wait_ge(S["chan"], nth(5, u))
                for t in range(T):
                    mm = nc.tensor.matmul(PS[u][:, 1, cols(t)], work[u][:, 1, cols(t)], a_o[:], start=True, stop=True)
                mm.then_inc(S["a_out"], 1)
            turn_tensor(pe, 6, lambda u: tok(work[u][:, 0, :]), lambda u: pe.wait_ge(S["a_normed"], nth(1, u)))
            for u in range(U):
                pe.wait_ge(S["chan"], nth(6, u))
                for t in range(T):
                    mm = nc.tensor.matmul(PS[u][:, 1, E2 * t:E2 * (t + 1)], work[u][:, 1, cols(t)], e2_router[:],
                                          start=True, stop=True)
                mm.then_inc(S["e2_logits"], 1)
            for e in range(E2 + 1):
                for f in range(FCH):
                    for u in range(U):
                        i = FCH * e + f
                        if e < E2:
                            pe.wait_ge(*((S["e2_hidden"], nth(i - 1, u)) if i else (S["e2_lg"], nth(0, u))))
                            w = slice(P * f, P * f + FW[f])
                            nc.tensor.matmul(PS[u][0:FW[f], 0, :], e2_w1[:, e, w], work[u][:, 1, :], start=True, stop=True)
                            nc.tensor.matmul(PS[u][0:FW[f], 1, :], e2_w3[:, e, w], work[u][:, 1, :], start=True, stop=True)\
                                .then_inc(S["e2_up"], 1)
                        if e > 0 and f == 1:
                            pe.wait_ge(S["e2_hidden"], nth(FCH * e - 1, u))
                            if e > 2:
                                pe.wait_ge(S["e2_added"], nth(e - 3, u))
                            o = e - 1
                            for t in range(T):
                                for g in range(FCH):
                                    mm = nc.tensor.matmul(PS[u][:, 2 + o % 2, cols(t)],
                                                          work[u][0:FW[g], 6 + FCH * (o % 2) + g, cols(t)],
                                                          e2_w2[0:FW[g], o, g, :], start=(g == 0), stop=(g == FCH - 1))
                            mm.then_inc(S["e2_down"], 1)

        def attn_scalar(act):
            rms_scalar(act, 0, lambda u: act.wait_ge(S["normed"], nth(5, u)))
            turn_scalar(act, 4, lambda u: work[u][:, 1, :], a_ln1[:])
            for u in range(U):
                act.wait_ge(S["a_v_ps"], nth(0, u))
                nc.scalar.activation(work[u][:, 6, 0:256], PS[u][:, 0, 0:256], ACT.Copy).then_inc(S["a_v"], 1)
            for t in range(T):
                w = P * (t + 1)
                for u in range(U):
                    act.wait_ge(S["a_max"], nth(t, u))
                    for h in range(NHA):
                        ins = nc.scalar.activation(work[u][:, 7 + h, 0:w], PS[u][:, h, 0:w], ACT.Exp, scale=HDA ** -0.5,
                                                   bias=sm[u][:, 1 + t, h:h + 1], accum_out=sm[u][:, 1 + t, 4 + h:5 + h])
                    ins.then_inc(S["a_p"], 1)
            turn_scalar(act, 5, lambda u: work[u][:, 1, :])
            rms_scalar(act, 1, lambda u: act.wait_ge(S["a_x"], nth(0, u)))
            turn_scalar(act, 6, lambda u: work[u][:, 1, :], a_ln2[:])
            route_scalar(act, 0, E2)
            for i in range(FCH * E2):
                for u in range(U):
                    act.wait_ge(S["e2_up"], nth(i, u))
                    if i >= 2:
                        act.wait_ge(S["e2_hidden"], nth(i - 2, u))
                    w = FW[i % FCH]
                    nc.scalar.activation(work[u][0:w, 2 + i % 2, :], PS[u][0:w, 0, :], ACT.Tanh, scale=0.5)\
                        .then_inc(S["e2_tanh"], 1)

        def attn_vector(dve, ch):
            norm_vector(dve, ch, 5, x, xh, lambda u: dve.wait_ge(S["x"], nth(4, u)))
            rms_vector(dve, 0)
            for u in range(U):
                dve.wait_ge(S["a_qk"], nth(0, u))
                for i in range(4):
                    ins = nc.vector.tensor_tensor(work[u][:, 2 + i, :], PS[u][:, i, :], (a_cos, a_sin)[i % 2][:], ALU.mult)
                ins.then_inc(S["a_parts"], 1)
            for t in range(T):
                w = P * (t + 1)
                for u in range(U):
                    dve.wait_ge(S["a_scores"], nth(t, u))
                    ch.link(nc.vector.tensor_reduce(sm[u][:, 5, 0:NHA], PS[u][:, :, 0:w], AX.X, ALU.max))
                    nc.vector.tensor_scalar(sm[u][:, 1 + t, 0:NHA], sm[u][:, 5, 0:NHA], -HDA ** -0.5, None, ALU.mult)\
                        .then_inc(S["a_max"], 1)
                for u in range(U):
                    dve.wait_ge(S["a_p_turned"], nth(t, u))
                    for s in range(t + 1):
                        ins = nc.vector.tensor_copy(work[u][:, 11 + s, :], PS[u][:, s, :])
                    ins.then_inc(S["a_pT"], 1)
                for u in range(U):
                    ch.link(nc.vector.reciprocal(sm[u][:, 6, 0:NHA], sm[u][:, 1 + t, 4:8]))
                    dve.wait_ge(S["a_pv"], nth(t, u))
                    nc.vector.tensor_tensor(work[u][:, 5, cols(t)].rearrange("p (h w) -> p h w", h=NHA),
                                            PS[u][:, 0, 0:P].rearrange("p (h w) -> p h w", h=NHA),
                                            sm[u][:, 6, 0:NHA].unsqueeze(2).to_broadcast([P, NHA, HDA]), ALU.mult)\
                        .then_inc(S["a_y"], 1)
            for u in range(U):
                dve.wait_ge(S["a_out"], nth(0, u))
                nc.vector.tensor_tensor(xh[u][:], xh[u][:], tok(PS[u][:, 1, :]), ALU.add).then_inc(S["a_x"], 1)
            rms_vector(dve, 1)

            def e2_logits(u):
                dve.wait_ge(S["e2_logits"], nth(0, u))
                nc.vector.tensor_copy(lg[u][:, :, 0:E2], PS[u][:, 1, 0:T * E2].rearrange("p (t e) -> p t e", t=T))\
                    .then_inc(S["e2_lg"], 1)
                dve.wait_ge(S["e2_lg"], nth(0, u))

            route_vector(dve, ch, 0, E2, e2_logits, 1e-9)
            for e in range(E2 + 1):
                for f in range(FCH):
                    for u in range(U):
                        i, w = FCH * e + f, FW[f]
                        if e < E2:
                            dve.wait_ge(S["e2_tanh"], nth(i, u))
                            gate = work[u][0:w, 4 + i % 2, :]
                            ch.link(nc.vector.scalar_tensor_tensor(out=gate, in0=work[u][0:w, 2 + i % 2, :], scalar=1.0,
                                                                   in1=PS[u][0:w, 0, :], op0=ALU.add, op1=ALU.mult))
                            if e > 1 and f == 0:
                                dve.wait_ge(S["e2_down"], nth(e - 2, u))
                            nc.vector.scalar_tensor_tensor(out=work[u][0:w, 6 + FCH * (e % 2) + f, :], in0=gate, scalar=0.5,
                                                           in1=PS[u][0:w, 1, :], op0=ALU.mult, op1=ALU.mult)\
                                .then_inc(S["e2_hidden"], 1)
                        if e > 0 and f == 2:
                            o = e - 1
                            dve.wait_ge(S["e2_down"], nth(o, u))
                            if o == 0:
                                dve.wait_ge(S["e2_base"], nth(0, u))
                                dve.wait_ge(S["routed"], nth(0, u))
                            else:
                                dve.wait_ge(S["e2_added"], nth(o - 1, u))
                            for t in range(T):
                                ins = nc.vector.scalar_tensor_tensor(out=x[u][:, t, :], in0=PS[u][:, 2 + o % 2, cols(t)],
                                                                     scalar=wts[u][:, t, o:o + 1], in1=x[u][:, t, :],
                                                                     op0=ALU.mult, op1=ALU.add)
                            ins.then_inc(S["e2_added"] if o < E2 - 1 else S["x"], 1)

        def attn_gpsimd(pool, ch):
            rstd_gpsimd(pool, 5)
            rms_gpsimd(pool, 0)
            for u in range(U):
                pool.wait_ge(S["a_parts"], nth(0, u))
                nc.gpsimd.tensor_tensor(work[u][:, 2, :], work[u][:, 2, :], work[u][:, 3, :], ALU.add)
                nc.gpsimd.tensor_tensor(work[u][:, 4, :], work[u][:, 4, :], work[u][:, 5, :], ALU.add)\
                    .then_inc(S["a_rotated"], 1)
            for u in range(U):
                pool.wait_ge(S["a_x"], nth(0, u))
                nc.gpsimd.tensor_tensor(x[u][:], x[u][:], xh[u][:], ALU.add).then_inc(S["e2_base"], 1)
            rms_gpsimd(pool, 1)

        def root_tensor(pe):
            turn_tensor(pe, 7, lambda u: tok(work[u][:, 0, :]), lambda u: pe.wait_ge(S["r_h"], nth(0, u)))
            for u in range(U):
                for t in range(T):
                    mm = nc.tensor.matmul(PS[u][:, 1, :], work[u][:, 0, cols(t)], adjT[u][:, t, :], start=(t == 0), stop=(t == T - 1))
                mm.then_inc(S["r_sum"], 1)
            for u in range(U):
                pe.wait_ge(S["chan"], nth(7, u))
                pe.wait_ge(S["r_sum_sb"], nth(0, u))
                for t in range(T):
                    nc.tensor.matmul(PS[u][:, 2, cols(t)], ones_row[:], r_b[:], start=True, stop=False)
                    nc.tensor.matmul(PS[u][:, 2, cols(t)], work[u][:, 2, cols(t)], r_rel[:], start=False, stop=False)
                    mm = nc.tensor.matmul(PS[u][:, 2, cols(t)], work[u][:, 1, cols(t)], r_root[:], start=False, stop=True)
                mm.then_inc(S["r_out"], 1)

        def root_scalar(act):
            turn_scalar(act, 7, lambda u: work[u][:, 1, :])
            for u in range(U):
                act.wait_ge(S["r_sum"], nth(0, u))
                nc.scalar.activation(work[u][:, 2, :], PS[u][:, 1, :], ACT.Copy).then_inc(S["r_sum_sb"], 1)

        def root_vector(dve, ch):
            norm_vector(dve, ch, 6, x, xh, lambda u: dve.wait_ge(S["x"], nth(5, u)))
            h = [tok(work[u][:, 0, :]) for u in range(U)]
            norm_vector(dve, ch, 7, xh, h, lambda u: dve.wait_ge(S["normed"], nth(6, u)))
            for u in range(U):
                dve.wait_ge(S["normed"], nth(7, u))
                ch.link(nc.vector.tensor_tensor(h[u], h[u], r_gamma[:].unsqueeze(1).to_broadcast([P, T, P]), ALU.mult))
                nc.vector.tensor_tensor(h[u], h[u], r_beta[:].unsqueeze(1).to_broadcast([P, T, P]), ALU.add)\
                    .then_inc(S["r_h"], 1)
            for u in range(U):
                dve.wait_ge(S["r_out"], nth(0, u))
                dve.wait_ge(S["r_base"], nth(0, u))
                nc.vector.scalar_tensor_tensor(out=x[u][:], in0=tok(PS[u][:, 2, :]), scalar=0.0, in1=x[u][:],
                                               op0=ALU.max, op1=ALU.add).then_inc(S["x"], 1)

        def root_gpsimd(pool, ch):
            rstd_gpsimd(pool, 6)
            rstd_gpsimd(pool, 7)
            for u in range(U):
                nc.gpsimd.tensor_tensor(x[u][:], x[u][:], xh[u][:], ALU.add).then_inc(S["r_base"], 1)

        def top2_tensor(pe):
            turn_tensor(pe, 8, lambda u: xh[u], lambda u: pe.wait_ge(S["normed"], nth(8, u)))
            for u in range(U):
                pe.wait_ge(S["chan"], nth(8, u))
                for t in range(T):
                    mm = nc.tensor.matmul(PS[u][:, 1, E3 * t:E3 * (t + 1)], xT[u][:, cols(t)], e3_gate[:], start=True, stop=True)
                mm.then_inc(S["e3_logits"], 1)
            for u in range(U):
                pe.wait_ge(S["routed"], nth(1, u))
                for t in range(T):
                    mm = nc.tensor.transpose(PS[u][0:E3, 2, cols(t)], wts[u][:, t, :], ident[:])
                mm.then_inc(S["e3_w_turned"], 1)
            for u in range(U):
                pe.wait_ge(S["e3_w_chan"], nth(0, u))
                for t in range(T):
                    mm = nc.tensor.matmul(PS[u][:, 3, cols(t)], work[u][0:E3, 0, cols(t)], e3_b2[:], start=True, stop=True)
                mm.then_inc(S["e3_biases"], 1)
            for e in range(E3 + 1):
                for u in range(U):
                    if e < E3:
                        for f in range(2):
                            if e > 0:
                                pe.wait_ge(S["e3_hidden"], 2 * nth(e - 1, u) - 1 + f)
                            nc.tensor.matmul(PS[u][:, f, :], e3_w1[:, e, f, :], xT[u][:], start=True, stop=True)\
                                .then_inc(S["e3_up"], 1)
                    if e > 0:
                        o = e - 1
                        pe.wait_ge(S["e3_hidden"], 2 * nth(o, u))
                        if o == 1:
                            pe.wait_ge(S["e3_base"], nth(0, u))
                        if o > 1:
                            pe.wait_ge(S["e3_added"], nth(o - 2, u))
                        for t in range(T):
                            for f in range(2):
                                mm = nc.tensor.matmul(PS[u][:, 2 + o % 2, cols(t)], work[u][:, 1 + 2 * (o % 2) + f, cols(t)],
                                                      e3_w2[:, o, f, :], start=(f == 0), stop=(f == 1))
                        mm.then_inc(S["e3_down"], 1)

        def top2_scalar(act):
            turn_scalar(act, 8, lambda u: xT[u][:])
            route_scalar(act, 1, E3)
            for e in range(E3):
                for u in range(U):
                    for f in range(2):
                        act.wait_ge(S["e3_up"], 2 * nth(e, u) - 1 + f)
                        if e > 1 and f == 0:
                            act.wait_ge(S["e3_down"], nth(e - 2, u))
                        nc.scalar.activation(work[u][:, 1 + 2 * (e % 2) + f, :], PS[u][:, f, :], ACT.Relu,
                                             bias=e3_b1[:, e, f:f + 1]).then_inc(S["e3_hidden"], 1)

        def top2_vector(dve, ch):
            norm_vector(dve, ch, 8, x, xh, lambda u: dve.wait_ge(S["x"], nth(6, u)))

            def e3_logits(u):
                dve.wait_ge(S["e3_logits"], nth(0, u))
                ch.link(nc.vector.tensor_tensor(lg[u][:, :, 0:E3], PS[u][:, 1, 0:T * E3].rearrange("p (t e) -> p t e", t=T),
                                                e3_gb[:].unsqueeze(1).to_broadcast([P, T, E3]), ALU.add))

            route_vector(dve, ch, 1, E3, e3_logits, None)
            for u in range(U):
                dve.wait_ge(S["e3_w_turned"], nth(0, u))
                nc.vector.tensor_copy(work[u][0:E3, 0, :], PS[u][0:E3, 2, :]).then_inc(S["e3_w_chan"], 1)
            y = [tok(work[u][:, 5, :]) for u in range(U)]
            for u in range(U):
                dve.wait_ge(S["e3_biases"], nth(0, u))
                nc.vector.tensor_tensor(y[u], xh[u][:], tok(PS[u][:, 3, :]), ALU.add).then_inc(S["e3_base"], 1)
            for e in range(E3):
                for u in range(U):
                    dve.wait_ge(S["e3_down"], nth(e, u))
                    dve.wait_ge(*((S["e3_added"], nth(e - 1, u)) if e else (S["e3_base"], nth(0, u))))
                    for t in range(T):
                        ins = nc.vector.scalar_tensor_tensor(out=y[u][:, t, :], in0=PS[u][:, 2 + e % 2, cols(t)],
                                                             scalar=wts[u][:, t, e:e + 1], in1=y[u][:, t, :],
                                                             op0=ALU.mult, op1=ALU.add)
                    ins.then_inc(S["e3_added"], 1)
            norm_vector(dve, ch, 9, y, xh, lambda u: dve.wait_ge(S["e3_added"], nth(E3 - 1, u)))
            for u in range(U):
                dve.wait_ge(S["normed"], nth(9, u))
                nc.vector.tensor_tensor(x[u][:], x[u][:], e3_beta[:].unsqueeze(1).to_broadcast([P, T, P]), ALU.add)
                ch.link(nc.vector.tensor_tensor(xh[u][:], xh[u][:], e3_gamma[:].unsqueeze(1).to_broadcast([P, T, P]), ALU.mult))
                nc.vector.tensor_tensor(x[u][:], x[u][:], xh[u][:], ALU.add).then_inc(S["x"], 1)

        def top2_gpsimd(pool, ch):
            rstd_gpsimd(pool, 8)
            rstd_gpsimd(pool, 9)

        layers = [(gat_tensor, gat_scalar, gat_vector, gat_gpsimd),
                  (mamba_tensor, mamba_scalar, mamba_vector, mamba_gpsimd),
                  (gcn_tensor, gcn_scalar, gcn_vector, gcn_gpsimd),
                  (top1_tensor, top1_scalar, top1_vector, top1_gpsimd),
                  (gru_tensor, gru_scalar, gru_vector, gru_gpsimd),
                  (attn_tensor, attn_scalar, attn_vector, attn_gpsimd),
                  (root_tensor, root_scalar, root_vector, root_gpsimd),
                  (top2_tensor, top2_scalar, top2_vector, top2_gpsimd)]

        engines = {e.engine for e in (nc.tensor, nc.vector, nc.scalar, nc.gpsimd, nc.sync)}
        own = list(S.of.values())
        nc.multi_engine_barrier(engines, sems_to_clear=range(own[0].num, own[-1].num + 1))
        with nc.Fori(0, B // U) as turn:
            with nc.Block() as block:
                @block.sync
                def _(sp):
                    gat_sync(sp, turn)
                    for u in range(U):
                        sp.wait_ge(S["x"], nth(N_LAYERS - 1, u))
                        sp.dma_start(out[bass.ds(U * turn + u, 1)].rearrange("o (t p) c -> p (o t) c", p=P), x[u][:])\
                            .then_inc(S["out_written"], 16)
                    for u in range(U):
                        sp.wait_ge(S[f"adjT_in{u}"], 16)
                    sp.wait_ge(S["out_written"], 16 * U)

                @block.tensor
                def _(pe):
                    for layer in layers[:N_LAYERS]:
                        layer[0](pe)

                @block.scalar
                def _(act):
                    for layer in layers[:N_LAYERS]:
                        layer[1](act)

                @block.vector
                def _(dve):
                    ch = Chain(dve, S["dve_own"])
                    for layer in layers[:N_LAYERS]:
                        layer[2](dve, ch)

                @block.gpsimd
                def _(pool):
                    ch = Chain(pool, S["pool_own"])
                    for layer in layers[:N_LAYERS]:
                        layer[3](pool, ch)

            own = list(S.of.values())
            nc.multi_engine_barrier(engines, sems_to_clear=range(own[0].num, own[-1].num + 1))


def kernel(**inputs):
    import numpy as np
    import concourse.bacc as bacc
    from concourse.bass_utils import run_bass_kernel_spmd

    g = {k: np.asarray(v) for k, v in inputs.items()}

    def experts_out(w):
        return w.transpose(2, 0, 1)

    def rows(w):
        return w.reshape(-1, P, *w.shape[1:]).swapaxes(0, 1)

    head = np.arange(HDA)
    swap = (head + HDA // 2) % HDA
    q_cols = np.arange(NHA * HDA)
    q_swap = (q_cols // HDA) * HDA + swap[q_cols % HDA]
    k_cols = (q_cols // HDA // 2) * HDA + q_cols % HDA
    k_swap = (q_cols // HDA // 2) * HDA + swap[q_cols % HDA]
    wq, wk = g["L2_ffn_wq"], g["L2_ffn_wk"]
    a_qk = np.concatenate([wq[q_cols].T, wq[q_swap].T, wk[k_cols].T, wk[k_swap].T], axis=1).reshape(P, 4, P)

    inv_freq = 1.0 / 10000.0 ** (np.arange(0, HDA, 2, dtype=np.float32) / HDA)
    freqs = np.outer(np.arange(N, dtype=np.float32), inv_freq)
    emb = np.concatenate([freqs, freqs], axis=-1)
    sign = np.where(head < HDA // 2, -1.0, 1.0).astype(np.float32)
    a_cos = np.tile(np.cos(emb).T, (NHA, 1)).astype(np.float32)
    a_sin = np.tile((np.sin(emb) * sign).T, (NHA, 1)).astype(np.float32)

    arrays = {
        "x": g["x"], "adj": g["adj"], "adj_t": g["adj"].transpose(0, 2, 1),
        "gat_w": g["L0_gnn_W"], "gat_wt": g["L0_gnn_W"].T, "gat_a": g["L0_gnn_a"].reshape(2, P).T,
        "m_in": g["L0_ffn_W_in"], "m_conv_w": rows(g["L0_ffn_conv_w"]), "m_conv_b": rows(g["L0_ffn_conv_b"]),
        "m_dt_bias": g["L0_ffn_dt_bias"], "m_a_log": g["L0_ffn_A_log"], "m_d": g["L0_ffn_D"],
        "m_norm_w": rows(g["L0_ffn_norm_w"]), "m_out_t": g["L0_ffn_W_out"].T, "m_lin": g["L0_ffn_W_lin"],
        "m_b_lin": g["L0_ffn_b_lin"],
        "gcn_w": g["L1_gnn_weight"], "gcn_b": g["L1_gnn_bias"],
        "e1_router_t": g["L1_ffn_router_w"].T, "e1_rb": g["L1_ffn_router_b"],
        "e1_w1": g["L1_ffn_W1"].transpose(1, 0, 2).reshape(P, 8, P), "e1_b1": rows(g["L1_ffn_b1"].reshape(-1)),
        "e1_w2": rows(g["L1_ffn_W2"].reshape(-1, P)), "e1_b2": g["L1_ffn_b2"],
        "g_se_t": g["L2_gnn_w_se"].T, "g_se_b": g["L2_gnn_b_se"][:, None],
        "g_c1_t": g["L2_gnn_conv1_w"][:, :, 0].T, "g_c2_t": g["L2_gnn_conv2_w"].transpose(1, 2, 0),
        "g_msg_t": g["L2_gnn_w_msg"].T, "g_msg_b": g["L2_gnn_b_msg"],
        "g_ih_t": rows(g["L2_gnn_w_ih"].T), "g_hh_t": g["L2_gnn_w_hh"].T,
        "g_b_ih": rows(g["L2_gnn_b_ih"]), "g_b_hh": rows(g["L2_gnn_b_hh"]),
        "a_ln1": g["L2_ffn_ln1_w"][:, None], "a_ln2": g["L2_ffn_ln2_w"][:, None], "a_qk": a_qk,
        "a_v_t": g["L2_ffn_wv"].T, "a_o_t": g["L2_ffn_wo"].T, "a_cos": a_cos, "a_sin": a_sin,
        "e2_router_t": g["L2_ffn_router_w"].T, "e2_w1_t": experts_out(g["L2_ffn_w1"]),
        "e2_w3_t": experts_out(g["L2_ffn_w3"]), "e2_w2_t": experts_out(g["L2_ffn_w2"]),
        "r_rel": g["L3_gnn_W_rel"], "r_root": g["L3_gnn_W_root"], "r_b": g["L3_gnn_b_rel"],
        "r_gamma": g["L3_gnn_ln_gamma"], "r_beta": g["L3_gnn_ln_beta"],
        "e3_gate": g["L3_ffn_gate_w"], "e3_gb": g["L3_ffn_gate_b"], "e3_w1": g["L3_ffn_w1"].transpose(1, 0, 2).reshape(P, E3, 2, P),
        "e3_b1": g["L3_ffn_b1"].reshape(E3, 2, P).transpose(2, 0, 1),
        "e3_w2": g["L3_ffn_w2"].reshape(E3, 2, P, P).transpose(2, 0, 1, 3), "e3_b2": g["L3_ffn_b2"],
        "e3_gamma": g["L3_ffn_gamma"], "e3_beta": g["L3_ffn_beta"],
    }
    arrays["g_bn"] = np.stack([g[f"L2_gnn_bn{n}_{k}"] for n in (1, 2) for k in "gbmv"], axis=1)

    nc = bacc.Bacc("TRN2", target_bir_lowering=False, num_devices=1)
    feed, d = {}, {}
    for name, a in arrays.items():
        a = np.ascontiguousarray(a)
        feed[f"in_{name}_dram"] = a
        d[name] = nc.dram_tensor(f"in_{name}_dram", a.shape, mybir.dt.from_np(a.dtype), kind="ExternalInput").ap()
    out = nc.dram_tensor("out_0_dram", g["x"].shape, F32, kind="ExternalOutput").ap()
    build_network(nc, d, out)
    return run_bass_kernel_spmd(nc, [feed], core_ids=[0]).results[0]["out_0_dram"]
```

```python
from contextlib import ExitStack

import concourse.bass as bass
from concourse import mybir
from concourse.alu_op_type import AluOpType as ALU

ACT = mybir.ActivationFunctionType
AX = mybir.AxisListType
F32 = mybir.dt.float32
BF16 = mybir.dt.bfloat16
U32 = mybir.dt.uint32
I32 = mybir.dt.int32

P = 128
N = 512
T = N // P
U = 2
NEG = -9.0e15
LN_EPS = 1e-5
RMS_EPS = 1e-6
HID, FCH = 341, 3
FW = [min(P, HID - P * f) for f in range(FCH)]
E1, E2, E3 = 32, 8, 16
TAPS, PAD = 17, 8
NHM, HDM, DST = 4, 64, 64
NHA, HDA = 4, 32
SLOTS = 15


def nth(k, u):
    return U * k + u + 1


class Semaphores:

    def __init__(self, ctx, nc):
        self.ctx, self.nc, self.all, self.of = ctx, nc, [], {}

    def __getitem__(self, name):
        if name not in self.of:
            if len(self.of) == len(self.all):
                self.all.append(self.ctx.enter_context(self.nc.semaphore(f"signal_{len(self.all)}")))
            self.of[name] = self.all[len(self.of)]
        return self.of[name]

    def numbers(self):
        used = [self.all[k].num for k in range(len(self.of))]
        assert used == list(range(used[0], used[0] + len(used)))
        return range(used[0], used[0] + len(used))

    def release(self):
        self.of = {}


class Chain:

    def __init__(self, engine, sem):
        self.engine, self.sem, self.n = engine, sem, 0

    def mark(self, ins):
        ins.then_inc(self.sem, 1)
        self.n += 1
        return self.n

    def wait(self, n):
        self.engine.wait_ge(self.sem, n)

    def link(self, ins):
        self.wait(self.mark(ins))


def build_network(nc, d, out):
    B = d["x"].shape[0]
    REGION = B * N + P

    def TILES(n):
        return 2 * B * T + n

    with ExitStack() as ctx:
        def sb(name, shape, dt=F32):
            return ctx.enter_context(nc.sbuf_tensor(name, shape, dt))

        S = Semaphores(ctx, nc)

        ident = sb("ident", [P, P])
        ident_h = sb("ident_h", [P, P], BF16)
        upper = sb("upper", [P, P])
        causal = sb("causal", [P, P], BF16)
        ones_row = sb("ones_row", [1, P])
        minus_half = sb("minus_half", [P, T])
        iota32 = sb("iota32", [P, E1])
        pick = sb("pick", [E1, E1 // 4, P], BF16)

        gat_w = sb("gat_w", [P, P])
        gat_a = sb("gat_a", [P, 2])
        gat_wa = sb("gat_wa", [P, 2])
        gat_wdst = sb("gat_wdst", [P, P])

        m_in = sb("m_in", [P, 644])
        m_taps = sb("m_taps", [P, 3, 4])
        m_convb = sb("m_convb", [P, 3])
        m_dtb = sb("m_dtb", [P, NHM])
        m_a = sb("m_a", [P, NHM])
        m_d = sb("m_d", [P, NHM])
        m_norm = sb("m_norm", [P, 2])
        m_wol = sb("m_wol", [P, 2, P])
        m_blin = sb("m_blin", [P, P])

        gcn_w = sb("gcn_w", [P, P])
        gcn_b = sb("gcn_b", [1, P])

        e1_router = sb("e1_router", [P, E1])
        e1_rb = sb("e1_rb", [P, E1])
        e1_w1 = sb("e1_w1", [P, 8, P])
        e1_b1 = sb("e1_b1", [P, 8])
        e1_w2 = sb("e1_w2", [P, 8, P])
        e1_b2 = sb("e1_b2", [E1, P])

        g_se = sb("g_se", [P, 96])
        g_seb = sb("g_seb", [96, 1])
        g_seb2 = sb("g_seb2", [32, 1])
        g_c1 = sb("g_c1", [P, P])
        g_c2 = sb("g_c2", [P, TAPS, P])
        g_bn = sb("g_bn", [P, 8])
        g_s = sb("g_s", [P, 2])
        g_c = sb("g_c", [P, 2])
        g_msg = sb("g_msg", [P, P])
        g_msgb = sb("g_msgb", [1, P])
        g_ih = sb("g_ih", [P, 2, 3 * P])
        g_hh = sb("g_hh", [P, 3 * P])
        g_bi = sb("g_bi", [P, 3])
        g_bh = sb("g_bh", [P, 3])
        g_half = sb("g_half", [P, 3])

        a_ln1 = sb("a_ln1", [P, 1])
        a_ln2 = sb("a_ln2", [P, 1])
        a_qk = sb("a_qk", [P, 4, P])
        a_v = sb("a_v", [P, 2 * HDA])
        a_o = sb("a_o", [P, P])
        a_cos = sb("a_cos", [P, N])
        a_sin = sb("a_sin", [P, N])
        e2_router = sb("e2_router", [P, E2])
        e2_w1 = sb("e2_w1", [P, E2, HID])
        e2_w3 = sb("e2_w3", [P, E2, HID])
        e2_w2 = sb("e2_w2", [P, E2, FCH, P])

        r_rel = sb("r_rel", [P, P])
        r_root = sb("r_root", [P, P])
        r_b = sb("r_b", [1, P])

        e3_gate = sb("e3_gate", [P, E3])
        e3_gb = sb("e3_gb", [P, E3])
        e3_w1 = sb("e3_w1", [P, E3, 2, P])
        e3_b1 = sb("e3_b1", [P, E3, 2])
        e3_w2 = sb("e3_w2", [P, E3, 2, P])

        strict = sb("strict", [P, P], BF16)
        ones_h = sb("ones_h", [P, P], BF16)
        region_of = sb("region_of", [P, E3])
        place = sb("place", [P, E3])
        row_of = sb("row_of", [P, (B + U) * T, 2], I32)
        weight_of = sb("weight_of", [P, B * T, 2])
        moe_in = nc.dram_tensor("moe_in", (E3 * REGION + 2 * T * U * P, P), F32, kind="Internal").ap()
        moe_out = nc.dram_tensor("moe_out", (P * TILES(E3), P), F32, kind="Internal").ap()
        carry_x = nc.dram_tensor("carry_x", (B, N, P), F32, kind="Internal").ap()
        carry_h = nc.dram_tensor("carry_h", (B, N, P), F32, kind="Internal").ap()

        def per(name, shape, dt=F32):
            return [sb(f"{name}{u}", shape, dt) for u in range(U)]

        x = per("x", [P, T, P])
        xh = per("xh", [P, T, P])
        xT = per("xT", [P, N])
        adjT = per("adjT", [P, T, N])
        work = per("work", [P, SLOTS, N])
        stats = per("stats", [P, T, 6])
        mv = per("mv", [P, T, 2])
        var = per("var", [P, T])
        rstd = per("rstd", [P, T])
        lg = per("lg", [P, T, E1])
        top = per("top", [P, T, 8])
        idx = per("idx", [P, T, 8], U32)
        idxf = per("idxf", [P, T, 2])
        oh = per("oh", [P, T, E1])
        oh2 = per("oh2", [P, T, E3])
        wts = per("wts", [P, T, E3 + 2])
        rows = per("rows", [P, T, 2], I32)
        sent = per("sent", [P, T, P])
        sent_to = per("sent_to", [P, T, 2], I32)
        chosen = per("chosen", [P, T, E3], BF16)
        den = per("den", [P, T])
        den2 = per("den2", [P, T])
        sm = per("sm", [P, 8, 16])
        PS = [ctx.enter_context(nc.psum_tensor(f"PS{u}", [P, 4, N], F32)) for u in range(U)]

        def slot(u, a, n=1):
            return work[u][:, a:a + n, :].rearrange("p s n -> p (s n)")

        r_gamma, r_beta = work[0][:, 5, 0:P], work[0][:, 5, P:2 * P]
        e3_gamma, e3_beta = work[0][:, 5, 0:P], work[0][:, 5, P:2 * P]
        job = x[0][0:1, :, :].rearrange("p t c -> p (t c)")[:, 0:2 * TILES(E3)].bitcast(I32)\
            .rearrange("p (k j) -> p k j", k=2)

        def tok(ap):
            return ap.rearrange("p (t c) -> p t c", t=T)

        def cols(t):
            return slice(P * t, P * (t + 1))

        with nc.Block() as block:
            loads = []

            def load(dst, src):
                loads.append((dst, src))

            def bcast(ap, n=P):
                return ap.partition_broadcast(n)

            load(gat_w[:], d["gat_w"]); load(work[0][:, 2, 0:P], d["gat_wt"]); load(gat_a[:], d["gat_a"])
            load(m_in[:], d["m_in"])
            load(m_taps[:], d["m_conv_w"])
            load(m_convb[:], d["m_conv_b"])
            load(m_dtb[:], bcast(d["m_dt_bias"]))
            load(m_a[:], bcast(d["m_a_log"]))
            load(m_d[:], bcast(d["m_d"]))
            load(m_norm[:], d["m_norm_w"])
            load(m_blin[:], bcast(d["m_b_lin"]))
            load(work[0][:, 0, 0:256], d["m_out_t"])
            load(work[0][:, 1, 0:P], d["m_lin"])
            load(gcn_w[:], d["gcn_w"]); load(gcn_b[:], d["gcn_b"].unsqueeze(0))
            load(e1_router[:], d["e1_router_t"]); load(e1_rb[:], bcast(d["e1_rb"]))
            load(e1_w1[:], d["e1_w1"])
            load(e1_b1[:], d["e1_b1"])
            load(e1_w2[:], d["e1_w2"])
            load(e1_b2[:], d["e1_b2"])
            load(g_c1[:], d["g_c1_t"]); load(g_c2[:], d["g_c2_t"])
            load(g_bn[:], d["g_bn"])
            load(g_msg[:], d["g_msg_t"]); load(g_msgb[:], d["g_msg_b"].unsqueeze(0))
            load(g_ih[:], d["g_ih_t"]); load(g_hh[:], d["g_hh_t"])
            load(g_bi[:], d["g_b_ih"])
            load(g_bh[:], d["g_b_hh"])
            load(a_ln1[:], d["a_ln1"]); load(a_ln2[:], d["a_ln2"])
            load(a_qk[:], d["a_qk"])
            load(a_v[:], d["a_v_t"]); load(a_o[:], d["a_o_t"])
            load(a_cos[:], d["a_cos"]); load(a_sin[:], d["a_sin"])
            load(e2_router[:], d["e2_router_t"])
            load(e2_w1[:], d["e2_w1_t"]); load(e2_w3[:], d["e2_w3_t"])
            for f in range(FCH):
                load(e2_w2[0:FW[f], :, f, :], d["e2_w2_t"][P * f:P * f + FW[f]])
            load(r_rel[:], d["r_rel"]); load(r_root[:], d["r_root"]); load(r_b[:], d["r_b"].unsqueeze(0))
            load(e3_gate[:], d["e3_gate"]); load(e3_gb[:], bcast(d["e3_gb"]))
            load(e3_w1[:], d["e3_w1"])
            load(e3_b1[:], d["e3_b1"])
            load(e3_w2[:], d["e3_w2"])
            late = []
            for k in range(3):
                late.append((g_se[:, 32 * k:32 * k + 3], d["g_se_t"]))
                late.append((g_seb[32 * k:32 * k + 3, :], d["g_se_b"]))
            late.append((g_seb2[0:3, :], d["g_se_b"]))
            all_loads = 16 * (len(loads) + len(late))

            @block.sync
            def _(sp):
                for dst, src in loads:
                    sp.dma_start(dst, src).then_inc(S["weights_in"], 16)
                sp.wait_ge(S["se_zeroed"], 1)
                for dst, src in late:
                    sp.dma_start(dst, src).then_inc(S["weights_in"], 16)
                sp.wait_ge(S["weights_in"], all_loads)

            @block.gpsimd
            def _(pool):
                ch = Chain(pool, S["pool_own"])
                nc.gpsimd.memset(g_se[:], 0.0)
                nc.gpsimd.memset(g_seb2[:], 0.0)
                nc.gpsimd.memset(g_seb[:], 0.0).then_inc(S["se_zeroed"], 1)
                nc.gpsimd.memset(ident[:], 0.0)
                nc.gpsimd.memset(upper[:], 1.0)
                nc.gpsimd.memset(causal[:], 0.0)
                nc.gpsimd.memset(pick[:], 1.0e30)
                nc.gpsimd.memset(ones_row[:], 1.0)
                nc.gpsimd.memset(strict[:], 1.0)
                nc.gpsimd.memset(ones_h[:], 1.0)
                nc.gpsimd.memset(row_of[:], 0)
                for u in range(U):
                    nc.gpsimd.memset(sent[u][:], 0.0)
                    nc.gpsimd.iota(sent_to[u][:], [[2 * P, T], [P, 2]], base=E3 * REGION + 2 * T * P * u, channel_multiplier=1)
                nc.gpsimd.iota(region_of[:], [[REGION, E3]], base=0, channel_multiplier=0,
                               allow_small_or_imprecise_dtypes=True)
                nc.gpsimd.iota(place[:], [[REGION, E3]], base=0, channel_multiplier=0,
                               allow_small_or_imprecise_dtypes=True)
                ch.link(nc.gpsimd.memset(minus_half[:], -0.5))
                nc.gpsimd.affine_select(out=strict[:], in_=strict[:], compare_op=ALU.is_gt, fill=0.0,
                                        base=0, pattern=[[1, P]], channel_multiplier=-1)
                nc.gpsimd.iota(iota32[:], [[1, E1]], base=0, channel_multiplier=0, allow_small_or_imprecise_dtypes=True)
                nc.gpsimd.affine_select(out=upper[:], in_=upper[:], compare_op=ALU.is_ge, fill=0.0,
                                        base=0, pattern=[[1, P]], channel_multiplier=-1)
                nc.gpsimd.affine_select(out=causal[:], in_=causal[:], compare_op=ALU.is_ge, fill=-1.0e30,
                                        base=0, pattern=[[-1, P]], channel_multiplier=1)
                ch.link(nc.gpsimd.affine_select(out=pick[:], in_=pick[:], compare_op=ALU.is_ge, fill=0.0, base=0,
                                                pattern=[[128, 8], [1, P]], channel_multiplier=-32))
                ch.link(nc.gpsimd.affine_select(out=pick[:], in_=pick[:], compare_op=ALU.is_ge, fill=0.0, base=31,
                                                pattern=[[-128, 8], [-1, P]], channel_multiplier=32))
                ch.link(nc.gpsimd.affine_select(out=ident[:], in_=ident[:], compare_op=ALU.not_equal, fill=1.0,
                                                base=0, pattern=[[-1, P]], channel_multiplier=1))
                nc.gpsimd.tensor_copy(ident_h[:], ident[:])
                pool.wait_ge(S["bn_var"], 1)
                nc.gpsimd.tensor_tensor(g_s[:], sm[0][:, 0, 0:2], minus_half[:, 0:2], ALU.pow).then_inc(S["bn_pow"], 1)

            @block.tensor
            def _(pe):
                pe.wait_ge(S["weights_in"], all_loads)
                nc.tensor.matmul(PS[0][:, 0, 0:2], work[0][:, 2, 0:P], gat_a[:], start=True, stop=True)
                for i in range(2):
                    mm = nc.tensor.matmul(PS[0][:, 1 + i, 0:P], work[0][:, 0, cols(i)], work[0][:, 1, 0:P],
                                          start=True, stop=True)
                mm.then_inc(S["folded"], 1)

            @block.scalar
            def _(act):
                act.wait_ge(S["weights_in"], all_loads)
                nc.scalar.activation(m_a[:], m_a[:], ACT.Exp).then_inc(S["a_exp"], 1)

            @block.vector
            def _(dve):
                ch = Chain(dve, S["dve_own"])
                dve.wait_ge(S["weights_in"], all_loads)
                bn = g_bn[:, :].rearrange("p (n k) -> p k n", k=4)
                nc.vector.tensor_scalar(sm[0][:, 0, 0:2], bn[:, 3, :], LN_EPS, None, ALU.add).then_inc(S["bn_var"], 1)
                nc.vector.tensor_scalar(m_taps[:], m_taps[:], 0.5, None, ALU.mult)
                nc.vector.tensor_scalar(m_convb[:], m_convb[:], 0.5, None, ALU.mult)
                nc.vector.tensor_scalar(g_seb2[:], g_seb2[:], 2.0, None, ALU.mult)
                nc.vector.tensor_scalar(g_half[:, 2:3], g_bh[:, 2:3], 0.5, None, ALU.mult)
                ch.link(nc.vector.tensor_tensor(g_half[:, 0:2], g_bi[:, 0:2], g_bh[:, 0:2], ALU.add))
                nc.vector.tensor_scalar(g_half[:, 0:2], g_half[:, 0:2], 0.5, None, ALU.mult)
                dve.wait_ge(S["a_exp"], 1)
                nc.vector.tensor_scalar(m_a[:], m_a[:], -1.0, None, ALU.mult)
                dve.wait_ge(S["bn_pow"], 1)
                ch.link(nc.vector.tensor_tensor(g_s[:], g_s[:], bn[:, 0, :], ALU.mult))
                ch.link(nc.vector.tensor_tensor(sm[0][:, 0, 2:4], bn[:, 2, :], g_s[:], ALU.mult))
                nc.vector.tensor_tensor(g_c[:], bn[:, 1, :], sm[0][:, 0, 2:4], ALU.subtract)
                dve.wait_ge(S["folded"], 1)
                ch.link(nc.vector.tensor_copy(gat_wa[:], PS[0][:, 0, 0:2]))
                nc.vector.tensor_copy(gat_wdst[:], gat_wa[:, 1:2].to_broadcast([P, P]))
                for i in range(2):
                    nc.vector.tensor_scalar(m_wol[:, i, :], PS[0][:, 1 + i, 0:P], m_norm[:, i:i + 1], None, ALU.mult)

        def updated(dve, k, update):
            def ready(u):
                update(u)
                dve.wait_ge(S["x"], nth(k, u))
            return ready

        def norm_vector(dve, ch, k, src, dst, ready, together=False):
            def apply(u):
                dve.wait_ge(S["rstd"], nth(k, u))
                for t in range(T):
                    ins = nc.vector.tensor_scalar(dst[u][:, t, :], src[u][:, t, :], mv[u][:, t, 0:1],
                                                  rstd[u][:, t:t + 1], ALU.subtract, ALU.mult)
                ins.then_inc(S["normed"], 1)

            for u in range(U):
                ready(u)
                for t in range(T):
                    n = ch.mark(nc.vector.bn_stats(stats[u][:, t, :], src[u][:, t, :]))
                ch.wait(n)
                for t in range(T):
                    n = ch.mark(nc.vector.bn_aggr(mv[u][:, t, :], stats[u][:, t, :]))
                ch.wait(n)
                nc.vector.tensor_scalar(var[u][:], mv[u][:, :, 1], LN_EPS, None, ALU.add).then_inc(S["var"], 1)
                if not together:
                    apply(u)
            if together:
                for u in range(U):
                    apply(u)

        def rstd_gpsimd(pool, k):
            for u in range(U):
                pool.wait_ge(S["var"], nth(k, u))
                nc.gpsimd.tensor_tensor(rstd[u][:], var[u][:], minus_half[:], ALU.pow).then_inc(S["rstd"], 1)

        def turn_tensor(pe, k, src, ready, products):
            for u in range(U):
                ready(u)
                for t in range(T):
                    mm = nc.tensor.transpose(PS[u][:, 0, cols(t)], src(u)[:, t, :], ident[:])
                mm.then_inc(S["turned"], 1)
                products(u)

        def turn_scalar(act, k, dst, scale=None):
            for u in range(U):
                act.wait_ge(S["turned"], nth(k, u))
                if scale is None:
                    ins = nc.scalar.activation(dst(u), PS[u][:, 0, :], ACT.Copy)
                else:
                    ins = nc.scalar.activation(dst(u), PS[u][:, 0, :], ACT.Copy, scale=scale)
                ins.then_inc(S["chan"], 1)

        def top_index(dve, ch, u, n):
            for t in range(T):
                m = ch.mark(nc.vector.max(top[u][:, t, :], lg[u][:, t, 0:n]))
            ch.wait(m)
            for t in range(T):
                m = ch.mark(nc.vector.max_index(idx[u][:, t, :], top[u][:, t, :], lg[u][:, t, 0:n]))
            ch.wait(m)
            ch.link(nc.vector.tensor_copy(idxf[u][:], idx[u][:, :, 0:2]))

        def one_hot(dst, u, k, n):
            return nc.vector.tensor_tensor(dst[:, :, 0:n], iota32[:, 0:n].unsqueeze(1).to_broadcast([P, T, n]),
                                           idxf[u][:, :, k:k + 1].to_broadcast([P, T, n]), ALU.is_equal)

        def gat_tensor(pe):

            def products(u):
                pe.wait_ge(S["chan"], nth(0, u))
                for t in range(T):
                    nc.tensor.matmul(PS[u][:, 1, cols(t)], xT[u][:, cols(t)], gat_w[:], start=True, stop=True)
                for t in range(T):
                    nc.tensor.matmul(PS[u][:, 2, t:t + 1], xT[u][:, cols(t)], gat_wa[:, 0:1], start=True, stop=True)
                nc.tensor.matmul(PS[u][:, 3, :], gat_wdst[:], xT[u][:], start=True, stop=True)\
                    .then_inc(S["gat_products"], 1)

            turn_tensor(pe, 0, lambda u: xh[u], lambda u: pe.wait_ge(S["normed"], nth(0, u)), products)
            for it in range(T):
                for u in range(U):
                    pe.wait_ge(S["gat_p"], nth(it, u))
                    if it == 0:
                        pe.wait_ge(S["gat_h"], nth(0, u))
                    if it == 1:
                        pe.wait_ge(S["gat_src"], nth(0, u))
                    if it >= 2:
                        pe.wait_ge(S["gat_pT"], nth(it - 2, u))
                    for jt in range(T):
                        mm = nc.tensor.transpose(PS[u][:, 1 + it % 2, cols(jt)], work[u][:, it, cols(jt)], ident[:])
                    mm.then_inc(S["gat_p_turned"], 1)
            for u in range(U):
                for it in range(T):
                    pe.wait_ge(S["gat_pT"], nth(it, u))
                    for jt in range(T):
                        mm = nc.tensor.matmul(PS[u][:, 0, cols(it)], work[u][:, 4 + it, cols(jt)],
                                              work[u][:, 8, cols(jt)], start=(jt == 0), stop=(jt == T - 1))
                mm.then_inc(S["gat_out"], 1)

        def gat_scalar(act):
            turn_scalar(act, 0, lambda u: xT[u][:])
            for u in range(U):
                act.wait_ge(S["gat_products"], nth(0, u))
                nc.scalar.activation(work[u][:, 8, :], PS[u][:, 1, :], ACT.Copy).then_inc(S["gat_h"], 1)
            for it in range(T):
                for u in range(U):
                    if it == 0:
                        act.wait_ge(S["gat_src"], nth(0, u))
                    nc.scalar.activation(work[u][:, it, :], PS[u][:, 3, :], ACT.Identity,
                                         bias=sm[u][:, 0, it:it + 1]).then_inc(S["gat_sum"], 1)
            for it in range(T):
                for u in range(U):
                    act.wait_ge(S["gat_max"], nth(it, u))
                    nc.scalar.activation(work[u][:, it, :], work[u][:, it, :], ACT.Exp,
                                         bias=sm[u][:, 1, it:it + 1], accum_out=sm[u][:, 2, it:it + 1])\
                        .then_inc(S["gat_p"], 1)

        def gat_vector(dve, ch):
            norm_vector(dve, ch, 0, x, xh, lambda u: dve.wait_ge(S[f"x_in{u}"], 16), True)
            for u in range(1, U):
                dve.wait_ge(S[f"adj_in{u}"], 16)
                a = work[u][:, 9:13, :]
                ch.link(nc.vector.tensor_scalar(a, a, 0.0, NEG, ALU.is_le, ALU.mult))
            for u in range(U):
                dve.wait_ge(S["gat_products"], nth(0, u))
                nc.vector.tensor_copy(sm[u][:, 0, 0:T], PS[u][:, 2, 0:T]).then_inc(S["gat_src"], 1)
            for it in range(T):
                for u in range(U):
                    e = work[u][:, it, :]
                    dve.wait_ge(S["gat_sum"], nth(it, u))
                    ch.link(nc.vector.scalar_tensor_tensor(out=e, in0=e, scalar=0.2, in1=e, op0=ALU.mult, op1=ALU.max))
                    if u == 0:
                        dve.wait_ge(S["gat_penalty"], 1)
                    ch.link(nc.vector.tensor_tensor(e, e, work[u][:, 9 + it, :], ALU.add))
                    ch.link(nc.vector.tensor_reduce(sm[u][:, 3, it:it + 1], e, AX.X, ALU.max))
                    nc.vector.tensor_scalar(sm[u][:, 1, it:it + 1], sm[u][:, 3, it:it + 1], -1.0, None, ALU.mult)\
                        .then_inc(S["gat_max"], 1)
            for it in range(T):
                for u in range(U):
                    dve.wait_ge(S["gat_p_turned"], nth(it, u))
                    nc.vector.tensor_copy(work[u][:, 4 + it, :], PS[u][:, 1 + it % 2, :]).then_inc(S["gat_pT"], 1)

            def update(u):
                dve.wait_ge(S["gat_p"], nth(T - 1, u))
                ch.link(nc.vector.reciprocal(den[u][:], sm[u][:, 2, 0:T]))
                dve.wait_ge(S["gat_out"], nth(0, u))
                for t in range(T):
                    ins = nc.vector.scalar_tensor_tensor(out=x[u][:, t, :], in0=PS[u][:, 0, cols(t)],
                                                         scalar=den[u][:, t:t + 1], in1=x[u][:, t, :],
                                                         op0=ALU.mult, op1=ALU.add)
                ins.then_inc(S["x"], 1)
            return update

        def gat_gpsimd(pool, ch):
            rstd_gpsimd(pool, 0)
            pool.wait_ge(S["adj_in0"], 16)
            a = work[0][:, 9:13, :]
            nc.gpsimd.tensor_scalar(a, a, 0.0, NEG, ALU.is_le, ALU.mult).then_inc(S["gat_penalty"], 1)

        def states_of(u):
            return slot(u, 4, 2)[0:DST, :].rearrange("n (c m) -> n c m", c=T)

        def heads(ap):
            return ap.rearrange("p (k w) -> p k w", k=T * NHM)

        def mamba_tensor(pe):

            def products(u):
                pe.wait_ge(S["chan"], nth(1, u))
                for i in range(3):
                    nc.tensor.matmul(PS[u][:, i, :], m_in[:, 256 + P * i:256 + P * (i + 1)], xT[u][:], start=True, stop=True)
                for c in range(T):
                    mm = nc.tensor.matmul(PS[u][:, 3, 4 * c:4 * c + 4], xT[u][:, cols(c)], m_in[:, 640:644],
                                          start=True, stop=True)
                mm.then_inc(S["m_projected"], 1)

            turn_tensor(pe, 1, lambda u: xh[u], lambda u: pe.wait_ge(S["normed"], nth(1, u)), products)
            for u in range(U):
                pe.wait_ge(S["m_silu"], nth(0, u))
                for c in range(T):
                    for i in range(2):
                        nc.tensor.transpose(PS[u][:, c // 2, cols(2 * (c % 2) + i)], work[u][:, 6 + i, cols(c)], ident[:])
                for c in range(T):
                    nc.tensor.transpose(PS[u][:, 2, DST * c:DST * (c + 1)], work[u][0:DST, 8, cols(c)],
                                        ident[0:DST, 0:DST])
                pe.wait_ge(S["m_da"], nth(0, u))
                nc.tensor.matmul(PS[u][:, 3, 0:16], upper[:], sm[u][:, 1, :], start=True, stop=True)\
                    .then_inc(S["m_turned"], 1)
            for u in range(U):
                pe.wait_ge(S["m_x_tok"], nth(0, u))
                for c in range(T):
                    mm = nc.tensor.matmul(PS[u][:, 0, cols(c)], work[u][0:DST, 8, cols(c)], work[u][0:DST, 9, cols(c)],
                                          start=True, stop=True)
                mm.then_inc(S["m_cb"], 1)
            for c in range(T):
                for u in range(U):
                    if c == 0:
                        pe.wait_ge(S["m_cum"], nth(0, u))
                        pe.wait_ge(S["m_b_tok"], nth(0, u))
                    if c >= 2:
                        pe.wait_ge(S["m_diff"], nth(c - 2, u))
                    for h in range(NHM):
                        k = NHM * c + h
                        mm = nc.tensor.matmul(PS[u][:, 2 + c % 2, cols(h)], sm[u][:, 2, k:k + 1].to_broadcast([P, P]), ident[:],
                                              start=True, stop=True)
                    mm.then_inc(S["m_rows"], 1)
            for u in range(U):
                pe.wait_ge(S["m_xdd"], nth(0, u))
                for c in range(T - 1):
                    mm = nc.tensor.matmul(PS[u][0:DST, 2 + c // 2, 256 * (c % 2):256 * (c % 2 + 1)],
                                          work[u][:, 12, DST * c:DST * (c + 1)],
                                          slot(u, 6, 2)[:, 256 * c:256 * (c + 1)], start=True, stop=True)
                mm.then_inc(S["m_states"], 1)
            for u in range(U):
                pe.wait_ge(S["m_decays"], nth(0, u))
                for c in range(T):
                    for h in range(NHM):
                        k = NHM * c + h
                        mm = nc.tensor.matmul(PS[u][:, c // 2, 256 * (c % 2) + HDM * h:256 * (c % 2) + HDM * (h + 1)],
                                              slot(u, 0, 4)[:, P * k:P * (k + 1)],
                                              slot(u, 13, 2)[:, HDM * k:HDM * (k + 1)], start=True, stop=True)
                mm.then_inc(S["m_y_in"], 1)
                pe.wait_ge(S["m_scanned"], nth(0, u))
                for c in range(T):
                    mm = nc.tensor.matmul(PS[u][:, 2 + c // 2, 256 * (c % 2):256 * (c % 2 + 1)],
                                          work[u][0:DST, 9, cols(c)], states_of(u)[:, c, :], start=True, stop=True)
                mm.then_inc(S["m_y_off"], 1)
            for u in range(U):
                pe.wait_ge(S["m_y"], nth(0, u))
                for t in range(T):
                    mm = nc.tensor.matmul(PS[u][:, t // 2, 256 * (t % 2):256 * (t % 2 + 1)], xT[u][:, cols(t)],
                                          m_in[:, 0:256], start=True, stop=True)
                mm.then_inc(S["m_z"], 1)
            for u in range(U):
                pe.wait_ge(S["m_gated"], nth(0, u))
                for i in range(2):
                    for t in range(T):
                        mm = nc.tensor.transpose(PS[u][:, 2 + i, cols(t)], slot(u, 6, 2)[:, 256 * t + P * i:256 * t + P * (i + 1)],
                                                 ident[:])
                mm.then_inc(S["m_y_turned"], 1)
            for u in range(U):
                pe.wait_ge(S["m_y_chan"], nth(0, u))
                for t in range(T):
                    for i in range(2):
                        mm = nc.tensor.matmul(PS[u][:, 0, cols(t)], work[u][:, i, cols(t)], m_wol[:, i, :],
                                              start=(i == 0), stop=(i == 1))
                mm.then_inc(S["m_out"], 1)

        def mamba_scalar(act):
            turn_scalar(act, 1, lambda u: xT[u][:])
            for u in range(U):
                act.wait_ge(S["m_dt_abs"], nth(0, u))
                nc.scalar.activation(sm[u][:, 3, :], sm[u][:, 2, :], ACT.Exp).then_inc(S["m_dt_exp"], 1)
            for u in range(U):
                act.wait_ge(S["m_dt_exp"], nth(0, u))
                nc.scalar.activation(sm[u][:, 4, :], sm[u][:, 3, :], ACT.Ln, bias=1.0).then_inc(S["m_dt_ln"], 1)
            for u in range(U):
                act.wait_ge(S["m_conv"], nth(0, u))
                nc.scalar.activation(work[u][:, 3:6, :], work[u][:, 0:3, :], ACT.Tanh).then_inc(S["m_tanh"], 1)
            for u in range(U):
                act.wait_ge(S["m_turned"], nth(0, u))
                nc.scalar.activation(work[u][:, 10:12, :], PS[u][:, 0:2, :], ACT.Copy).then_inc(S["m_x_tok"], 1)
                nc.scalar.activation(work[u][:, 12, 0:256], PS[u][:, 2, 0:256], ACT.Copy).then_inc(S["m_b_tok"], 1)
            for u in range(U):
                act.wait_ge(S["m_ends"], nth(0, u))
                nc.scalar.activation(sm[u][:, 5:8, :], sm[u][:, 5:8, :], ACT.Exp).then_inc(S["m_ends_exp"], 1)
            for u in range(U):
                act.wait_ge(S["m_clamped"], nth(0, u))
                nc.scalar.activation(work[u][:, 0:4, :], work[u][:, 0:4, :], ACT.Exp).then_inc(S["m_exp"], 1)
            for u in range(U):
                act.wait_ge(S["m_z"], nth(0, u))
                nc.scalar.activation(work[u][:, 13:15, :], PS[u][:, 0:2, :], ACT.Tanh, scale=0.5).then_inc(S["m_z_tanh"], 1)
            for u in range(U):
                act.wait_ge(S["m_gated"], nth(0, u))
                for t in range(T):
                    y_t = slot(u, 6, 2)[:, 256 * t:256 * (t + 1)]
                    ins = nc.scalar.activation(slot(u, 10, 2)[:, 256 * t:256 * (t + 1)], y_t, ACT.Square,
                                               accum_out=sm[u][:, 0, t:t + 1])
                ins.then_inc(S["m_square"], 1)
                act.wait_ge(S["m_y_turned"], nth(0, u))
                nc.scalar.activation(work[u][:, 0:2, :], PS[u][:, 2:4, :], ACT.Copy).then_inc(S["m_y_chan"], 1)

        def mamba_vector(dve, ch, ready):
            norm_vector(dve, ch, 1, x, xh, ready)
            for u in range(U):
                dve.wait_ge(S["m_projected"], nth(0, u))
                ch.link(nc.vector.tensor_tensor(sm[u][:, 0, :].rearrange("p (c h) -> p c h", c=T),
                                                PS[u][:, 3, 0:16].rearrange("p (c h) -> p c h", c=T),
                                                m_dtb[:].unsqueeze(1).to_broadcast([P, T, NHM]), ALU.add))
                nc.vector.scalar_tensor_tensor(out=sm[u][:, 2, :], in0=sm[u][:, 0, :], scalar=-1.0, in1=sm[u][:, 0, :],
                                               op0=ALU.mult, op1=ALU.min).then_inc(S["m_dt_abs"], 1)
            for u in range(U):
                for i in range(3):
                    m = ch.mark(nc.vector.tensor_scalar(work[u][:, i, :], PS[u][:, i, :], m_taps[:, i, 3:4], m_convb[:, i:i + 1],
                                                        ALU.mult, ALU.add))
                for k in (2, 1, 0):
                    ch.wait(m)
                    for i in range(3):
                        s = 3 - k
                        ins = nc.vector.scalar_tensor_tensor(
                            out=work[u][:, i, s:N], in0=PS[u][:, i, 0:N - s], scalar=m_taps[:, i, k:k + 1],
                            in1=work[u][:, i, s:N], op0=ALU.mult, op1=ALU.add)
                        if k > 0 or i < 2:
                            m = ch.mark(ins)
                ins.then_inc(S["m_conv"], 1)
            for u in range(U):
                dve.wait_ge(S["m_dt_ln"], nth(0, u))
                ch.link(nc.vector.scalar_tensor_tensor(out=sm[u][:, 0, :], in0=sm[u][:, 0, :], scalar=0.0,
                                                       in1=sm[u][:, 4, :], op0=ALU.max, op1=ALU.add))
                nc.vector.tensor_tensor(sm[u][:, 1, :].rearrange("p (c h) -> p c h", c=T),
                                        sm[u][:, 0, :].rearrange("p (c h) -> p c h", c=T),
                                        m_a[:].unsqueeze(1).to_broadcast([P, T, NHM]), ALU.mult).then_inc(S["m_da"], 1)
            for u in range(U):
                dve.wait_ge(S["m_tanh"], nth(0, u))
                for tanh, conv, dst in ((work[u][:, 3:5, :], work[u][:, 0:2, :], work[u][:, 6:8, :]),
                                        (work[u][0:64, 5, :], work[u][0:64, 2, :], work[u][0:64, 8, :]),
                                        (work[u][64:P, 5, :], work[u][64:P, 2, :], work[u][0:64, 9, :])):
                    ins = nc.vector.scalar_tensor_tensor(out=dst, in0=tanh, scalar=1.0, in1=conv, op0=ALU.add, op1=ALU.mult)
                ins.then_inc(S["m_silu"], 1)
            for u in range(U):
                dve.wait_ge(S["m_turned"], nth(0, u))
                nc.vector.tensor_copy(sm[u][:, 2, :], PS[u][:, 3, 0:16]).then_inc(S["m_cum"], 1)
                dve.wait_ge(S["m_x_tok"], nth(0, u))
                m = ch.mark(nc.vector.tensor_tensor(heads(slot(u, 13, 2)), heads(slot(u, 10, 2)),
                                                    sm[u][:, 0, :].unsqueeze(2).to_broadcast([P, 16, HDM]), ALU.mult))
            for c in range(T):
                for u in range(U):
                    dve.wait_ge(S["m_rows"], nth(c, u))
                    rows_ps = PS[u][:, 2 + c % 2, :].rearrange("p (h l) -> p h l", h=NHM)
                    if c == 0:
                        dve.wait_ge(S["m_cum"], nth(0, u))
                    m = ch.mark(nc.vector.tensor_copy(sm[u][:, 7, NHM * c:NHM * (c + 1)], rows_ps[:, :, P - 1]))
                    nc.vector.tensor_tensor(work[u][:, c, :].rearrange("p (h l) -> p h l", h=NHM), rows_ps,
                                            sm[u][:, 2, NHM * c:NHM * (c + 1)].unsqueeze(2).to_broadcast([P, NHM, P]),
                                            ALU.subtract).then_inc(S["m_diff"], 1)
            for u in range(U):
                dve.wait_ge(S["m_diff"], nth(T - 1, u))
                nc.vector.tensor_copy(sm[u][:, 6, :], sm[u][:, 2, :])
                ch.link(nc.vector.tensor_tensor(sm[u][:, 5, :], sm[u][:, 7, :], sm[u][:, 2, :], ALU.subtract))
                nc.vector.tensor_scalar(sm[u][:, 5, :], sm[u][:, 5, :], 0.0, None, ALU.min).then_inc(S["m_ends"], 1)
                nc.vector.tensor_scalar(work[u][:, 0:4, :], work[u][:, 0:4, :], 0.0, None, ALU.min).then_inc(S["m_clamped"], 1)
            for u in range(U):
                dve.wait_ge(S["m_cb"], nth(0, u))
                nc.vector.tensor_tensor(tok(work[u][:, 4, :]), PS[u][:, 0, :].rearrange("p (c l) -> p c l", c=T),
                                        upper[:].unsqueeze(1).to_broadcast([P, T, P]), ALU.mult).then_inc(S["m_cb_masked"], 1)
                dve.wait_ge(S["m_ends_exp"], nth(0, u))
                nc.vector.tensor_tensor(heads(slot(u, 6, 2)), heads(slot(u, 13, 2)),
                                        sm[u][:, 5, :].unsqueeze(2).to_broadcast([P, 16, HDM]), ALU.mult)\
                    .then_inc(S["m_xdd"], 1)
            for u in range(U):
                dve.wait_ge(S["m_exp"], nth(0, u))
                dve.wait_ge(S["m_cb_masked"], nth(0, u))
                decays = slot(u, 0, 4).rearrange("p (c h l) -> p c h l", c=T, h=NHM)
                nc.vector.tensor_tensor(decays, decays, tok(work[u][:, 4, :]).unsqueeze(2).to_broadcast([P, T, NHM, P]),
                                        ALU.mult).then_inc(S["m_decays"], 1)
            for u in range(U):
                dve.wait_ge(S["m_decays"], nth(0, u))
                st = states_of(u)
                m = ch.mark(nc.vector.memset(st[:, 0, :], 0.0))
                dve.wait_ge(S["m_states"], nth(0, u))
                ch.link(nc.vector.tensor_copy(st[:, 1, :], PS[u][0:DST, 2, 0:256]))
                for c in (1, 2):
                    ch.link(nc.vector.tensor_tensor(st[:, c + 1, :].rearrange("n (h w) -> n h w", h=NHM),
                                                    st[:, c, :].rearrange("n (h w) -> n h w", h=NHM),
                                                    sm[u][0:DST, 7, NHM * c:NHM * (c + 1)].unsqueeze(2).to_broadcast([DST, NHM, HDM]),
                                                    ALU.mult))
                    ins = nc.vector.tensor_tensor(st[:, c + 1, :], st[:, c + 1, :],
                                                  PS[u][0:DST, 2 + c // 2, 256 * (c % 2):256 * (c % 2 + 1)], ALU.add)
                    if c == 1:
                        ch.link(ins)
                ins.then_inc(S["m_scanned"], 1)
            for u in range(U):
                y = slot(u, 6, 2)
                dve.wait_ge(S["m_y_off"], nth(0, u))
                ch.link(nc.vector.tensor_tensor(heads(y), PS[u][:, 2:4, :].rearrange("p b (k w) -> p (b k) w", w=HDM),
                                                sm[u][:, 6, :].unsqueeze(2).to_broadcast([P, 16, HDM]), ALU.mult))
                ch.link(nc.vector.tensor_tensor(work[u][:, 6:8, :], work[u][:, 6:8, :], PS[u][:, 0:2, :], ALU.add))
                dve.wait_ge(S["m_skip"], nth(0, u))
                nc.vector.tensor_tensor(y, y, slot(u, 10, 2), ALU.add).then_inc(S["m_y"], 1)
            for u in range(U):
                dve.wait_ge(S["m_z_tanh"], nth(0, u))
                gate = work[u][:, 13:15, :]
                ch.link(nc.vector.scalar_tensor_tensor(out=gate, in0=gate, scalar=1.0, in1=PS[u][:, 0:2, :],
                                                       op0=ALU.add, op1=ALU.mult))
                nc.vector.scalar_tensor_tensor(out=work[u][:, 6:8, :], in0=work[u][:, 6:8, :], scalar=0.5, in1=gate,
                                               op0=ALU.mult, op1=ALU.mult).then_inc(S["m_gated"], 1)
            for u in range(U):
                dve.wait_ge(S["m_square"], nth(0, u))
                nc.vector.tensor_scalar(den[u][:], sm[u][:, 0, 0:T], 1.0 / 256, LN_EPS, ALU.mult, ALU.add)\
                    .then_inc(S["m_mean_sq"], 1)

            def update(u):
                dve.wait_ge(S["m_rstd"], nth(0, u))
                dve.wait_ge(S["m_out"], nth(0, u))
                for t in range(T):
                    ins = nc.vector.scalar_tensor_tensor(out=x[u][:, t, :], in0=PS[u][:, 0, cols(t)], scalar=den2[u][:, t:t + 1],
                                                         in1=x[u][:, t, :], op0=ALU.mult, op1=ALU.add)
                ins.then_inc(S["x"], 1)
            return update

        def mamba_gpsimd(pool, ch):
            rstd_gpsimd(pool, 1)
            for u in range(U):
                pool.wait_ge(S["normed"], nth(1, u))
                nc.gpsimd.tensor_tensor(x[u][:], x[u][:], m_blin[:].unsqueeze(1).to_broadcast([P, T, P]), ALU.add)
            for u in range(U):
                pool.wait_ge(S["m_xdd"], nth(0, u))
                v = slot(u, 10, 2).rearrange("p (c h w) -> p c h w", c=T, h=NHM)
                nc.gpsimd.tensor_tensor(v, v, m_d[:].unsqueeze(1).unsqueeze(3).to_broadcast([P, T, NHM, HDM]), ALU.mult)\
                    .then_inc(S["m_skip"], 1)
            for u in range(U):
                pool.wait_ge(S["m_mean_sq"], nth(0, u))
                nc.gpsimd.tensor_tensor(den2[u][:], den[u][:], minus_half[:], ALU.pow).then_inc(S["m_rstd"], 1)


        def gcn_tensor(pe):
            for u in range(U):
                pe.wait_ge(S["normed"], nth(2, u))
                pe.wait_ge(S[f"adjT_in{u}"], 16)
                for t in range(T):
                    mm = nc.tensor.matmul(PS[u][:, 0, :], xh[u][:, t, :], adjT[u][:, t, :], start=(t == 0), stop=(t == T - 1))
                mm.then_inc(S["gcn_sum"], 1)
            for u in range(U):
                pe.wait_ge(S["gcn_chan"], nth(0, u))
                for t in range(T):
                    nc.tensor.matmul(PS[u][:, 1, cols(t)], ones_row[:], gcn_b[:], start=True, stop=False)
                    mm = nc.tensor.matmul(PS[u][:, 1, cols(t)], work[u][:, 0, cols(t)], gcn_w[:], start=False, stop=True)
                mm.then_inc(S["gcn_out"], 1)

        def gcn_scalar(act):
            for u in range(U):
                act.wait_ge(S["gcn_sum"], nth(0, u))
                nc.scalar.activation(work[u][:, 0, :], PS[u][:, 0, :], ACT.Copy).then_inc(S["gcn_chan"], 1)

        def gcn_vector(dve, ch, ready):
            norm_vector(dve, ch, 2, x, xh, ready)

            def update(u):
                dve.wait_ge(S["gcn_out"], nth(0, u))
                nc.vector.tensor_tensor(x[u][:], x[u][:], tok(PS[u][:, 1, :]), ALU.add).then_inc(S["x"], 1)
            return update

        def gcn_gpsimd(pool, ch):
            rstd_gpsimd(pool, 2)

        G1 = E1 // 4

        def not_chosen(u):
            return work[u][0:E1, 9, 0:N // 2].bitcast(BF16)

        def top1_tensor(pe):

            def products(u):
                pe.wait_ge(S["chan"], nth(2, u))
                for t in range(T):
                    mm = nc.tensor.matmul(PS[u][:, 1, E1 * t:E1 * (t + 1)], xT[u][:, cols(t)], e1_router[:], start=True, stop=True)
                mm.then_inc(S["e1_logits"], 1)

            turn_tensor(pe, 2, lambda u: xh[u], lambda u: pe.wait_ge(S["normed"], nth(3, u)), products)
            for u in range(U):
                pe.wait_ge(S["e1_hot"], nth(0, u))
                for t in range(T):
                    mm = nc.tensor.transpose(PS[u][0:E1, 2, cols(t)], oh[u][:, t, :], ident[:])
                mm.then_inc(S["e1_hot_turned"], 1)
            for g in range(G1):
                for u in range(U):
                    if g == 0:
                        pe.wait_ge(S["e1_not_chosen"], nth(0, u))
                    else:
                        if g >= 2:
                            pe.wait_ge(S["e1_hidden"], nth(g - 2, u))
                    b = 3 * (g % 2)
                    nc.tensor.matmul(PS[u][:, b, :], e1_w1[:, g, :], xT[u][:], start=True, stop=False)
                    nc.tensor.matmul(PS[u][:, b, :], pick[:, g, :], not_chosen(u), start=False, stop=True)\
                        .then_inc(S["e1_up"], 1)
            for u in range(U):
                pe.wait_ge(S["e1_hidden"], nth(G1 - 1, u))
                for t in range(T):
                    nc.tensor.matmul(PS[u][:, 1, cols(t)], work[u][0:E1, 8, cols(t)], e1_b2[:], start=True, stop=False)
                    for g in range(G1):
                        mm = nc.tensor.matmul(PS[u][:, 1, cols(t)], work[u][:, g, cols(t)], e1_w2[:, g, :],
                                              start=False, stop=(g == G1 - 1))
                mm.then_inc(S["e1_out"], 1)

        def top1_scalar(act):
            turn_scalar(act, 2, lambda u: xT[u][:])
            for g in range(G1):
                for u in range(U):
                    act.wait_ge(S["e1_up"], nth(g, u))
                    nc.scalar.activation(work[u][:, g, :], PS[u][:, 3 * (g % 2), :], ACT.Relu, bias=e1_b1[:, g:g + 1])\
                        .then_inc(S["e1_hidden"], 1)

        def top1_vector(dve, ch, ready):
            norm_vector(dve, ch, 3, x, xh, ready)
            for u in range(U):
                dve.wait_ge(S["e1_logits"], nth(0, u))
                ch.link(nc.vector.tensor_tensor(lg[u][:], PS[u][:, 1, 0:T * E1].rearrange("p (t e) -> p t e", t=T),
                                                e1_rb[:].unsqueeze(1).to_broadcast([P, T, E1]), ALU.add))
                top_index(dve, ch, u, E1)
                one_hot(oh[u], u, 0, E1).then_inc(S["e1_hot"], 1)
            for u in range(U):
                dve.wait_ge(S["e1_hot_turned"], nth(0, u))
                nc.vector.tensor_copy(work[u][0:E1, 8, :], PS[u][0:E1, 2, :])
                nc.vector.tensor_scalar(not_chosen(u), PS[u][0:E1, 2, :], 1.0, None, ALU.subtract)\
                    .then_inc(S["e1_not_chosen"], 1)

            def update(u):
                dve.wait_ge(S["e1_out"], nth(0, u))
                nc.vector.scalar_tensor_tensor(out=x[u][:], in0=tok(PS[u][:, 1, :]), scalar=0.0, in1=x[u][:],
                                               op0=ALU.max, op1=ALU.add).then_inc(S["x"], 1)
            return update

        def top1_gpsimd(pool, ch):
            rstd_gpsimd(pool, 3)

        SE = 96

        def gru_tensor(pe):

            def products(u):
                pe.wait_ge(S["chan"], nth(3, u))
                nc.tensor.matmul(PS[u][:, 1, :], g_c1[:], xT[u][:], start=True, stop=True).then_inc(S["g_conv1"], 1)
                nc.tensor.matmul(PS[u][0:SE, 2, :], g_se[:], xT[u][:], start=True, stop=True).then_inc(S["g_struct"], 1)
                for t in range(T):
                    nc.tensor.matmul(PS[u][:, 3, cols(t)], ones_row[:], g_msgb[:], start=True, stop=False)
                    mm = nc.tensor.matmul(PS[u][:, 3, cols(t)], xT[u][:, cols(t)], g_msg[:], start=False, stop=True)
                mm.then_inc(S["g_msg"], 1)

            turn_tensor(pe, 3, lambda u: xh[u], lambda u: pe.wait_ge(S["normed"], nth(4, u)), products)
            for u in range(U):
                pe.wait_ge(S["g_padded"], nth(0, u))
                pe.wait_ge(S["g_hidden"], nth(0, u))
                for k in range(TAPS):
                    mm = nc.tensor.matmul(PS[u][:, 0, :], g_c2[:, k, :], slot(u, 0, 2)[:, k:k + N],
                                          start=(k == 0), stop=(k == TAPS - 1))
                mm.then_inc(S["g_conv2"], 1)
            for t in range(T):
                for u in range(U):
                    if t == 0:
                        pe.wait_ge(S["g_factors"], nth(0, u))
                    if t >= 2:
                        pe.wait_ge(S["g_near"], nth(t - 2, u))
                    nc.tensor.matmul(PS[u][:, 1 + t % 2, :], work[u][0:SE, 2, cols(t)], work[u][0:SE, 3, :],
                                     start=True, stop=True).then_inc(S["g_dist"], 1)
            for u in range(U):
                pe.wait_ge(S["g_affinity"], nth(T - 1, u))
                pe.wait_ge(S["g_msg_tok"], nth(0, u))
                for t in range(T):
                    mm = nc.tensor.matmul(PS[u][:, 3, :], work[u][:, 4, cols(t)], work[u][:, 6 + t, :],
                                          start=(t == 0), stop=(t == T - 1))
                mm.then_inc(S["g_received"], 1)
            for u in range(U):
                pe.wait_ge(S["g_conv_out"], nth(0, u))
                pe.wait_ge(S["g_received_sb"], nth(0, u))
                for g in range(3):
                    w = slice(P * g, P * (g + 1))
                    nc.tensor.matmul(PS[u][:, g, :], g_ih[:, 0, w], work[u][:, 5, :], start=True, stop=False)
                    nc.tensor.matmul(PS[u][:, g, :], g_ih[:, 1, w], work[u][:, 10, :], start=False, stop=(g == 2))
                    mm = nc.tensor.matmul(PS[u][:, g if g < 2 else 3, :], g_hh[:, w], xT[u][:], start=(g == 2), stop=True)
                mm.then_inc(S["g_gates"], 1)
            for u in range(U):
                pe.wait_ge(S["g_new"], nth(0, u))
                for t in range(T):
                    mm = nc.tensor.transpose(PS[u][:, 0, cols(t)], work[u][:, 1, cols(t)], ident[:])
                mm.then_inc(S["g_new_tok"], 1)

        def gru_scalar(act):
            turn_scalar(act, 3, lambda u: xT[u][:])
            for u in range(U):
                act.wait_ge(S["g_conv1"], nth(0, u))
                nc.scalar.activation(slot(u, 0, 2)[:, PAD:PAD + N], PS[u][:, 1, :], ACT.Relu, bias=g_c[:, 0:1],
                                     scale=g_s[:, 0:1]).then_inc(S["g_hidden"], 1)
                act.wait_ge(S["g_struct"], nth(0, u))
                act.wait_ge(S["g_padded"], nth(0, u))
                nc.scalar.activation(work[u][0:32, 2, :], PS[u][0:32, 2, :], ACT.Identity, bias=g_seb[0:32, :])
                nc.scalar.activation(work[u][32:64, 2, :], PS[u][32:64, 2, :], ACT.Square, bias=g_seb[32:64, :])
                nc.scalar.activation(work[u][0:32, 3, :], PS[u][0:32, 2, :], ACT.Identity, bias=g_seb2[:], scale=2.0)
                nc.scalar.activation(work[u][64:SE, 3, :], PS[u][64:SE, 2, :], ACT.Square, bias=g_seb[64:SE, :])\
                    .then_inc(S["g_factors"], 1)
            for u in range(U):
                act.wait_ge(S["g_msg"], nth(0, u))
                nc.scalar.activation(work[u][:, 4, :], PS[u][:, 3, :], ACT.Relu).then_inc(S["g_msg_tok"], 1)
            for t in range(T):
                for u in range(U):
                    act.wait_ge(S["g_dist"], nth(t, u))
                    nc.scalar.activation(work[u][:, 6 + t, :], PS[u][:, 1 + t % 2, :], ACT.Exp).then_inc(S["g_near"], 1)
            for u in range(U):
                act.wait_ge(S["g_conv_sum"], nth(0, u))
                nc.scalar.activation(work[u][:, 5, :], work[u][:, 5, :], ACT.Relu, bias=g_c[:, 1:2]).then_inc(S["g_conv_out"], 1)
                act.wait_ge(S["g_received"], nth(0, u))
                nc.scalar.activation(work[u][:, 10, :], PS[u][:, 3, :], ACT.Copy).then_inc(S["g_received_sb"], 1)
            for u in range(U):
                act.wait_ge(S["g_gates"], nth(0, u))
                nc.scalar.activation(work[u][:, 13, :], PS[u][:, 3, :], ACT.Identity, bias=g_half[:, 2:3], scale=0.5)
                nc.scalar.activation(work[u][:, 11, :], PS[u][:, 0, :], ACT.Tanh, bias=g_half[:, 0:1], scale=0.5)\
                    .then_inc(S["g_r"], 1)
                nc.scalar.activation(work[u][:, 12, :], PS[u][:, 1, :], ACT.Tanh, bias=g_half[:, 1:2], scale=0.5)\
                    .then_inc(S["g_z"], 1)
            for u in range(U):
                act.wait_ge(S["g_n_sum"], nth(0, u))
                nc.scalar.activation(work[u][:, 14, :], work[u][:, 13, :], ACT.Tanh, bias=g_bi[:, 2:3]).then_inc(S["g_n"], 1)

        def gru_vector(dve, ch, ready):
            norm_vector(dve, ch, 4, x, xh, ready)
            for t in range(T):
                for u in range(U):
                    dve.wait_ge(S["g_near"], nth(t, u))
                    nc.vector.tensor_tensor(work[u][:, 6 + t, :], work[u][:, 6 + t, :], adjT[u][:, t, :], ALU.mult)\
                        .then_inc(S["g_affinity"], 1)
            for u in range(U):
                dve.wait_ge(S["g_conv2"], nth(0, u))
                nc.vector.scalar_tensor_tensor(out=work[u][:, 5, :], in0=PS[u][:, 0, :], scalar=g_s[:, 1:2], in1=xT[u][:],
                                               op0=ALU.mult, op1=ALU.add).then_inc(S["g_conv_sum"], 1)
            for u in range(U):
                h_n = work[u][:, 13, :]
                dve.wait_ge(S["g_r"], nth(0, u))
                ch.link(nc.vector.scalar_tensor_tensor(out=h_n, in0=work[u][:, 11, :], scalar=1.0, in1=h_n,
                                                       op0=ALU.add, op1=ALU.mult))
                nc.vector.tensor_tensor(h_n, h_n, PS[u][:, 2, :], ALU.add).then_inc(S["g_n_sum"], 1)
            for u in range(U):
                diff = work[u][:, 0, :]
                dve.wait_ge(S["g_n"], nth(0, u))
                ch.link(nc.vector.tensor_tensor(diff, xT[u][:], work[u][:, 14, :], ALU.subtract))
                dve.wait_ge(S["g_z"], nth(0, u))
                ch.link(nc.vector.scalar_tensor_tensor(out=diff, in0=work[u][:, 12, :], scalar=1.0, in1=diff,
                                                       op0=ALU.add, op1=ALU.mult))
                nc.vector.scalar_tensor_tensor(out=work[u][:, 1, :], in0=diff, scalar=0.5, in1=work[u][:, 14, :],
                                               op0=ALU.mult, op1=ALU.add).then_inc(S["g_new"], 1)

            def update(u):
                dve.wait_ge(S["g_new_tok"], nth(0, u))
                nc.vector.tensor_tensor(x[u][:], x[u][:], tok(PS[u][:, 0, :]), ALU.add).then_inc(S["x"], 1)
            return update

        def gru_gpsimd(pool, ch):
            rstd_gpsimd(pool, 4)
            for u in range(U):
                pool.wait_ge(S["normed"], nth(4, u))
                nc.gpsimd.memset(slot(u, 0, 2)[:, 0:PAD], 0.0)
                ch.link(nc.gpsimd.memset(slot(u, 0, 2)[:, PAD + N:PAD + N + PAD], 0.0))
                ch.link(nc.gpsimd.memset(work[u][64:SE, 2, :], -1.0))
                nc.gpsimd.memset(work[u][32:64, 3, :], -1.0).then_inc(S["g_padded"], 1)
                pool.wait_ge(S["g_padded"], nth(0, u))

        def route_tensor(pe, n):
            for u in range(U):
                pe.wait_ge(S["route_chosen"], nth(0, u))
                for t in range(T):
                    for s in range(t):
                        nc.tensor.matmul(PS[u][:, 1, n * t:n * (t + 1)], ones_h[:], chosen[u][:, s, 0:n],
                                         start=(s == 0), stop=False)
                    nc.tensor.matmul(PS[u][:, 1, n * t:n * (t + 1)], strict[:], chosen[u][:, t, 0:n],
                                     start=(t == 0), stop=True)
                for t in range(T):
                    mm = nc.tensor.matmul(PS[u][:, 2, 0:n], ones_h[:], chosen[u][:, t, 0:n], start=(t == 0), stop=(t == T - 1))
                mm.then_inc(S["route_ranks"], 1)

        def route_scalar(act, n):
            for u in range(U):
                act.wait_ge(S["route_diff"], nth(0, u))
                nc.scalar.activation(wts[u][:], wts[u][:], ACT.Exp).then_inc(S["route_exp"], 1)

        def route_vector(dve, ch, turn, n, logits, extra):
            for u in range(U):
                logits(u)
                top_index(dve, ch, u, n)
                if n < E3:
                    nc.vector.memset(wts[u][:, :, n:E3], 0.0)
                nc.vector.tensor_tensor(wts[u][:, :, 0:n], lg[u][:, :, 0:n], top[u][:, :, 0:1].to_broadcast([P, T, n]),
                                        ALU.subtract)
                nc.vector.tensor_tensor(wts[u][:, :, E3:E3 + 2], top[u][:, :, 0:2], top[u][:, :, 0:1].to_broadcast([P, T, 2]),
                                        ALU.subtract).then_inc(S["route_diff"], 1)
                one_hot(oh[u], u, 0, n)
                ch.link(one_hot(oh2[u], u, 1, n))
                nc.vector.tensor_tensor(chosen[u][:, :, 0:n], oh[u][:, :, 0:n], oh2[u][:, :, 0:n], ALU.add)\
                    .then_inc(S["route_chosen"], 1)
            for u in range(U):
                dve.wait_ge(S["route_exp"], nth(0, u))
                if extra:
                    nc.vector.tensor_reduce(den2[u][:], wts[u][:, :, 0:n], AX.X, ALU.add)
                ch.link(nc.vector.tensor_reduce(den[u][:], wts[u][:, :, E3:E3 + 2], AX.X, ALU.add))
                if extra:
                    ch.link(nc.vector.scalar_tensor_tensor(out=den[u][:], in0=den2[u][:], scalar=extra, in1=den[u][:],
                                                           op0=ALU.mult, op1=ALU.add))
                ch.link(nc.vector.reciprocal(den[u][:], den[u][:]))
                nc.vector.tensor_tensor(weight_of[:, bass.ds(turn * U * T + u * T, T), :], wts[u][:, :, E3:E3 + 2],
                                        den[u][:].unsqueeze(2).to_broadcast([P, T, 2]), ALU.mult)
            for u in range(U):
                dve.wait_ge(S["route_ranks"], nth(0, u))
                if u:
                    dve.wait_ge(S["route_placed"], u)
                row = lg[u][:, :, 0:n]
                ch.link(nc.vector.tensor_tensor(row, PS[u][:, 1, 0:T * n].rearrange("p (t e) -> p t e", t=T),
                                                    place[:, 0:n].unsqueeze(1).to_broadcast([P, T, n]), ALU.add))
                nc.vector.tensor_tensor(place[:, 0:n], place[:, 0:n], PS[u][:, 2, 0:n], ALU.add).then_inc(S["route_placed"], 1)
                nc.vector.tensor_tensor(oh[u][:, :, 0:n], oh[u][:, :, 0:n], row, ALU.mult)
                ch.link(nc.vector.tensor_tensor(oh2[u][:, :, 0:n], oh2[u][:, :, 0:n], row, ALU.mult))
                nc.vector.tensor_reduce(idxf[u][:, :, 0], oh[u][:, :, 0:n], AX.X, ALU.add)
                ch.link(nc.vector.tensor_reduce(idxf[u][:, :, 1], oh2[u][:, :, 0:n], AX.X, ALU.add))
                nc.vector.tensor_copy(sent_to[u][:], idxf[u][:])
                nc.vector.tensor_copy(row_of[:, bass.ds(turn * U * T + u * T, T), :], idxf[u][:])

        def scatter_gpsimd(pool):
            for u in range(U):
                for t in range(T):
                    for k in range(2):
                        nc.gpsimd.indirect_dma_start(
                            out=moe_in, out_offset=bass.IndirectOffsetOnAxis(ap=sent_to[u][:, t, k:k + 1], axis=0),
                            in_=sent[u][:, t, :], in_offset=None).then_inc(S["scattered"], 16)

        def recall_rows(dve, turn):
            for u in range(U):
                nc.vector.tensor_copy(rows[u][:], row_of[:, bass.ds(turn * U * T + u * T, T), :]).then_inc(S["rows"], 1)

        def recall_weights(dve, turn):
            for u in range(U):
                nc.vector.tensor_copy(idxf[u][:], weight_of[:, bass.ds(turn * U * T + u * T, T), :]).then_inc(S["recalled"], 1)

        def gather_gpsimd(pool, n, u):
            pool.wait_ge(S["rows"], nth(0, u))
            for t in range(T):
                for k in range(2):
                    nc.gpsimd.indirect_dma_start(
                        out=work[u][:, 9 + k, cols(t)], out_offset=None, in_=moe_out[0:P * TILES(n)],
                        in_offset=bass.IndirectOffsetOnAxis(ap=rows[u][:, t, k:k + 1], axis=0)).then_inc(S[f"gathered{u}"], 16)

        def first_gather(n):
            with nc.Block() as block:
                @block.vector
                def _(dve):
                    recall_rows(dve, 0)

                @block.gpsimd
                def _(pool):
                    for u in range(U):
                        gather_gpsimd(pool, n, u)
                    for u in range(U):
                        pool.wait_ge(S[f"gathered{u}"], 16 * 2 * T)
            clear()

        def combine_vector(dve, ch, u, acc, sem):
            dve.wait_ge(S["recalled"], nth(0, u))
            for k in range(2):
                for t in range(T):
                    ins = nc.vector.scalar_tensor_tensor(out=acc[:, t, :], in0=work[u][:, 9 + k, cols(t)],
                                                         scalar=idxf[u][:, t, k:k + 1], in1=acc[:, t, :],
                                                         op0=ALU.mult, op1=ALU.add)
                    if k == 0:
                        m = ch.mark(ins)
                if k == 0:
                    ch.wait(m)
            ins.then_inc(sem, 1)

        def rms_scalar(act, k, src_ready):
            for u in range(U):
                src_ready(u)
                for t in range(T):
                    ins = nc.scalar.activation(work[u][:, 3, cols(t)], xh[u][:, t, :], ACT.Square,
                                               accum_out=sm[u][:, 0, t:t + 1])
                ins.then_inc(S["a_squares"], 1)

        def rms_vector(dve, k, dst):
            for u in range(U):
                dve.wait_ge(S["a_squares"], nth(k, u))
                nc.vector.tensor_scalar(den[u][:], sm[u][:, 0, 0:T], 1.0 / P, RMS_EPS, ALU.mult, ALU.add)\
                    .then_inc(S["a_mean_sq"], 1)
            for u in range(U):
                dve.wait_ge(S["a_rms"], nth(k, u))
                nc.vector.tensor_tensor(dst(u), xh[u][:], den2[u][:].unsqueeze(2).to_broadcast([P, T, P]),
                                        ALU.mult).then_inc(S["a_normed"], 1)

        def rms_gpsimd(pool, k):
            for u in range(U):
                pool.wait_ge(S["a_mean_sq"], nth(k, u))
                nc.gpsimd.tensor_tensor(den2[u][:], den[u][:], minus_half[:], ALU.pow).then_inc(S["a_rms"], 1)

        LANES = [(g, u) for g in range(NHA // 2) for u in range(U)]

        def by_lane(t, g, u):
            return len(LANES) * t + U * g + u + 1

        def turned_ps(u, g, t):
            return PS[u][:, 2 * g:2 * g + 2, :].rearrange("p b (s n) -> p (b s) n", s=2)[:, 0:t + 1, :]

        def turned_heads(u, g, t):
            return work[u][:, 11:12 + t, 256 * g:256 * (g + 1)]

        def attn_tensor(pe):

            def products(u):
                pe.wait_ge(S["chan"], nth(4, u))
                for i in range(4):
                    mm = nc.tensor.matmul(PS[u][:, i, :], a_qk[:, i, :], work[u][:, 1, :], start=True, stop=True)
                mm.then_inc(S["a_qk"], 1)

            turn_tensor(pe, 4, lambda u: tok(work[u][:, 0, :]), lambda u: pe.wait_ge(S["a_normed"], nth(0, u)), products)
            for u in range(U):
                pe.wait_ge(S["a_parts"], nth(0, u))
                for t in range(T):
                    mm = nc.tensor.matmul(PS[u][:, 0, 64 * t:64 * (t + 1)], work[u][:, 1, cols(t)], a_v[:],
                                          start=True, stop=True)
                mm.then_inc(S["a_v_ps"], 1)
            for t in range(T):
                w = P * (t + 1)
                for g, u in LANES:
                    if t == 0:
                        pe.wait_ge(S["a_rotated"], nth(0, u))
                        pe.wait_ge(S["a_v"], nth(0, u))
                    else:
                        pe.wait_ge(S["a_y"], by_lane(t - 1, g, u))
                    for h in (2 * g, 2 * g + 1):
                        r = slice(HDA * h, HDA * (h + 1))
                        nc.tensor.matmul(PS[u][:, h, 0:w], work[u][r, 2, cols(t)], work[u][r, 4, 0:w], start=True, stop=False)
                        mm = nc.tensor.matmul(PS[u][:, h, w - P:w], ident_h[:], causal[:], start=False, stop=True)
                    mm.then_inc(S["a_scores"], 1)
                for g, u in LANES:
                    pe.wait_ge(S["a_p"], by_lane(t, g, u))
                    for s in range(t + 1):
                        for i in range(2):
                            mm = nc.tensor.transpose(PS[u][:, 2 * g + s // 2, cols(2 * (s % 2) + i)],
                                                     work[u][:, 7 + 2 * g + i, cols(s)], ident[:])
                    mm.then_inc(S["a_p_turned"], 1)
                for g, u in LANES:
                    if g == 0:
                        pe.wait_ge(S["a_pT_dve"], nth(t, u))
                    else:
                        pe.wait_ge(S["a_pT_act"], nth(t, u))
                    for i in range(2):
                        for s in range(t + 1):
                            kv = 64 * s + HDA * g
                            mm = nc.tensor.matmul(PS[u][:, 2 * g, HDA * i:HDA * (i + 1)], work[u][:, 11 + s, cols(2 * g + i)],
                                                  work[u][:, 6, kv:kv + HDA], start=(s == 0), stop=(s == t))
                    mm.then_inc(S["a_pv"], 1)

            def products(u):
                pe.wait_ge(S["chan"], nth(5, u))
                for t in range(T):
                    mm = nc.tensor.matmul(PS[u][:, 1, cols(t)], work[u][:, 1, cols(t)], a_o[:], start=True, stop=True)
                mm.then_inc(S["a_out"], 1)

            turn_tensor(pe, 5, lambda u: tok(work[u][:, 5, :]), lambda u: pe.wait_ge(S["a_y"], by_lane(T - 1, 1, u)), products)

            def products(u):
                pe.wait_ge(S["chan"], nth(6, u))
                for t in range(T):
                    mm = nc.tensor.matmul(PS[u][:, 1, E2 * t:E2 * (t + 1)], work[u][:, 1, cols(t)], e2_router[:],
                                          start=True, stop=True)
                mm.then_inc(S["e2_logits"], 1)

            turn_tensor(pe, 6, lambda u: sent[u][:], lambda u: pe.wait_ge(S["a_normed"], nth(1, u)), products)
            route_tensor(pe, E2)

        def attn_scalar(act):
            rms_scalar(act, 0, lambda u: act.wait_ge(S["normed"], nth(5, u)))
            turn_scalar(act, 4, lambda u: work[u][:, 1, :], a_ln1[:])
            for u in range(U):
                act.wait_ge(S["a_v_ps"], nth(0, u))
                nc.scalar.activation(work[u][:, 6, 0:256], PS[u][:, 0, 0:256], ACT.Copy).then_inc(S["a_v"], 1)
            for t in range(T):
                w = P * (t + 1)
                for g, u in LANES:
                    act.wait_ge(S["a_max"], by_lane(t, g, u))
                    for h in (2 * g, 2 * g + 1):
                        ins = nc.scalar.activation(work[u][:, 7 + h, 0:w], PS[u][:, h, 0:w], ACT.Exp, scale=HDA ** -0.5,
                                                   bias=sm[u][:, 1 + t, h:h + 1], accum_out=sm[u][:, 1 + t, 4 + h:5 + h])
                    ins.then_inc(S["a_p"], 1)
                for u in range(U):
                    act.wait_ge(S["a_p_turned"], by_lane(t, 1, u))
                    nc.scalar.activation(turned_heads(u, 1, t), turned_ps(u, 1, t), ACT.Copy).then_inc(S["a_pT_act"], 1)
            turn_scalar(act, 5, lambda u: work[u][:, 1, :])
            rms_scalar(act, 1, lambda u: act.wait_ge(S["a_x"], nth(0, u)))
            turn_scalar(act, 6, lambda u: work[u][:, 1, :], a_ln2[:])
            route_scalar(act, E2)

        def attn_vector(dve, ch, turn, ready):
            norm_vector(dve, ch, 5, x, xh, ready)
            rms_vector(dve, 0, lambda u: tok(work[u][:, 0, :]))
            for u in range(U):
                dve.wait_ge(S["a_qk"], nth(0, u))
                for i in range(4):
                    ins = nc.vector.tensor_tensor(work[u][:, 2 + i, :], PS[u][:, i, :], (a_cos, a_sin)[i % 2][:], ALU.mult)
                ins.then_inc(S["a_parts"], 1)
            for t in range(T):
                w = P * (t + 1)
                for g, u in LANES:
                    pair = slice(2 * g, 2 * g + 2)
                    dve.wait_ge(S["a_scores"], by_lane(t, g, u))
                    ch.link(nc.vector.tensor_reduce(sm[u][:, 5, pair], PS[u][:, pair, 0:w], AX.X, ALU.max))
                    nc.vector.tensor_scalar(sm[u][:, 1 + t, pair], sm[u][:, 5, pair], -HDA ** -0.5, None, ALU.mult)\
                        .then_inc(S["a_max"], 1)
                for u in range(U):
                    dve.wait_ge(S["a_p_turned"], by_lane(t, 0, u))
                    nc.vector.tensor_copy(turned_heads(u, 0, t), turned_ps(u, 0, t)).then_inc(S["a_pT_dve"], 1)
                for g, u in LANES:
                    pair = slice(2 * g, 2 * g + 2)
                    dve.wait_ge(S["a_p"], by_lane(t, g, u))
                    ch.link(nc.vector.reciprocal(sm[u][:, 6, pair], sm[u][:, 1 + t, 4 + 2 * g:6 + 2 * g]))
                    dve.wait_ge(S["a_pv"], by_lane(t, g, u))
                    nc.vector.tensor_tensor(work[u][:, 5, P * t + 64 * g:P * t + 64 * (g + 1)].rearrange("p (h w) -> p h w", h=2),
                                            PS[u][:, 2 * g, 0:64].rearrange("p (h w) -> p h w", h=2),
                                            sm[u][:, 6, pair].unsqueeze(2).to_broadcast([P, 2, HDA]), ALU.mult)\
                        .then_inc(S["a_y"], 1)
            for u in range(U):
                dve.wait_ge(S["a_out"], nth(0, u))
                nc.vector.tensor_tensor(xh[u][:], xh[u][:], tok(PS[u][:, 1, :]), ALU.add).then_inc(S["a_x"], 1)
            dve.wait_ge(S["scattered"], 16 * 2 * T * U)
            rms_vector(dve, 1, lambda u: sent[u][:])

            def e2_logits(u):
                dve.wait_ge(S["e2_logits"], nth(0, u))
                ch.link(nc.vector.tensor_copy(lg[u][:, :, 0:E2], PS[u][:, 1, 0:T * E2].rearrange("p (t e) -> p t e", t=T)))

            route_vector(dve, ch, turn, E2, e2_logits, 1e-9)

        def attn_gpsimd(pool, ch):
            rstd_gpsimd(pool, 5)
            rms_gpsimd(pool, 0)
            for u in range(U):
                pool.wait_ge(S["a_parts"], nth(0, u))
                nc.gpsimd.tensor_tensor(work[u][:, 2, :], work[u][:, 2, :], work[u][:, 3, :], ALU.add)
                nc.gpsimd.tensor_tensor(work[u][:, 4, :], work[u][:, 4, :], work[u][:, 5, :], ALU.add)\
                    .then_inc(S["a_rotated"], 1)
            for u in range(U):
                pool.wait_ge(S["a_x"], nth(0, u))
                nc.gpsimd.tensor_tensor(x[u][:], x[u][:], xh[u][:], ALU.add).then_inc(S["e2_base"], 1)
            rms_gpsimd(pool, 1)

        def root_tensor(pe):

            def products(u):
                pe.wait_ge(S[f"adjT_in{u}"], 16)
                for t in range(T):
                    mm = nc.tensor.matmul(PS[u][:, 1, :], work[u][:, 0, cols(t)], adjT[u][:, t, :], start=(t == 0), stop=(t == T - 1))
                mm.then_inc(S["r_sum"], 1)

            turn_tensor(pe, 0, lambda u: tok(work[u][:, 0, :]), lambda u: pe.wait_ge(S["r_h"], nth(0, u)), products)
            for u in range(U):
                pe.wait_ge(S["chan"], nth(0, u))
                pe.wait_ge(S["r_sum_sb"], nth(0, u))
                for t in range(T):
                    nc.tensor.matmul(PS[u][:, 2, cols(t)], ones_row[:], r_b[:], start=True, stop=False)
                    nc.tensor.matmul(PS[u][:, 2, cols(t)], work[u][:, 2, cols(t)], r_rel[:], start=False, stop=False)
                    mm = nc.tensor.matmul(PS[u][:, 2, cols(t)], work[u][:, 1, cols(t)], r_root[:], start=False, stop=True)
                mm.then_inc(S["r_out"], 1)

        def root_scalar(act):
            turn_scalar(act, 0, lambda u: work[u][:, 1, :])
            for u in range(U):
                act.wait_ge(S["r_sum"], nth(0, u))
                nc.scalar.activation(work[u][:, 2, :], PS[u][:, 1, :], ACT.Copy).then_inc(S["r_sum_sb"], 1)

        def root_vector(dve, ch, turn):
            recall_weights(dve, turn)
            recall_rows(dve, turn + 1)

            def combined(u):
                dve.wait_ge(S[f"x_in{u}"], 16)
                combine_vector(dve, ch, u, x[u], S["combined"])
                dve.wait_ge(S["combined"], nth(0, u))

            norm_vector(dve, ch, 0, x, xh, combined, True)
            h = [tok(work[u][:, 0, :]) for u in range(U)]
            norm_vector(dve, ch, 1, xh, h, lambda u: dve.wait_ge(S["normed"], nth(0, u)), True)
            for u in range(U):
                dve.wait_ge(S["normed"], nth(1, u))
                ch.link(nc.vector.tensor_tensor(h[u], h[u], r_gamma.unsqueeze(1).to_broadcast([P, T, P]), ALU.mult))
                nc.vector.tensor_tensor(h[u], h[u], r_beta.unsqueeze(1).to_broadcast([P, T, P]), ALU.add)\
                    .then_inc(S["r_h"], 1)

            def update(u):
                dve.wait_ge(S["r_out"], nth(0, u))
                dve.wait_ge(S["r_base"], nth(0, u))
                nc.vector.scalar_tensor_tensor(out=x[u][:], in0=tok(PS[u][:, 2, :]), scalar=0.0, in1=x[u][:],
                                               op0=ALU.max, op1=ALU.add).then_inc(S["x"], 1)
            return update

        def root_gpsimd(pool, ch):
            rstd_gpsimd(pool, 0)
            rstd_gpsimd(pool, 1)
            for u in range(U):
                nc.gpsimd.tensor_tensor(x[u][:], x[u][:], xh[u][:], ALU.add).then_inc(S["r_base"], 1)
            scatter_gpsimd(pool)


        def top2_tensor(pe):

            def products(u):
                pe.wait_ge(S["chan"], nth(1, u))
                for t in range(T):
                    mm = nc.tensor.matmul(PS[u][:, 1, E3 * t:E3 * (t + 1)], xT[u][:, cols(t)], e3_gate[:], start=True, stop=True)
                mm.then_inc(S["e3_logits"], 1)

            turn_tensor(pe, 1, lambda u: sent[u], lambda u: pe.wait_ge(S["normed"], nth(2, u)), products)
            route_tensor(pe, E3)

        def top2_scalar(act):
            turn_scalar(act, 1, lambda u: xT[u][:])
            route_scalar(act, E3)

        def top2_vector(dve, ch, turn, ready):
            dve.wait_ge(S["scattered"], 16 * 2 * T * U)
            norm_vector(dve, ch, 2, x, sent, ready)

            def e3_logits(u):
                dve.wait_ge(S["e3_logits"], nth(0, u))
                ch.link(nc.vector.tensor_tensor(lg[u][:, :, 0:E3], PS[u][:, 1, 0:T * E3].rearrange("p (t e) -> p t e", t=T),
                                                e3_gb[:].unsqueeze(1).to_broadcast([P, T, E3]), ALU.add))

            route_vector(dve, ch, turn, E3, e3_logits, None)

        def top2_gpsimd(pool, ch):
            rstd_gpsimd(pool, 2)
            for u in range(U):
                pool.wait_ge(S["combined"], nth(0, u))
                gather_gpsimd(pool, E2, u)

        def last_vector(dve, ch, turn):
            recall_weights(dve, turn)
            recall_rows(dve, turn + 1)

            def combined(u):
                dve.wait_ge(S[f"h_in{u}"], 16)
                combine_vector(dve, ch, u, xh[u], S["combined"])
                dve.wait_ge(S["combined"], nth(0, u))

            y = [tok(work[u][:, 0, :]) for u in range(U)]
            norm_vector(dve, ch, 0, xh, y, combined, True)
            for u in range(U):
                dve.wait_ge(S["normed"], nth(0, u))
                dve.wait_ge(S[f"x_in{u}"], 16)
                nc.vector.tensor_tensor(x[u][:], x[u][:], e3_beta.unsqueeze(1).to_broadcast([P, T, P]), ALU.add)
                ch.link(nc.vector.tensor_tensor(y[u], y[u], e3_gamma.unsqueeze(1).to_broadcast([P, T, P]), ALU.mult))
                nc.vector.tensor_tensor(x[u][:], x[u][:], y[u], ALU.add).then_inc(S["x"], 1)

        def last_gpsimd(pool, ch):
            rstd_gpsimd(pool, 0)
            for u in range(U):
                pool.wait_ge(S["combined"], nth(0, u))
                gather_gpsimd(pool, E3, u)

        def table_phase(n, jobs):
            grid = slot(0, 0, SLOTS)[0:1, 0:jobs * n].rearrange("p (j e) -> p j e", j=jobs)
            count_j = work[1][0:1, 0, 0:jobs]
            job_e, base, dummy, read = (work[1][0:1, k, 0:jobs] for k in range(1, 5))
            tiles_e, upto, offset, step, ones = (work[1][:, 6, 16 * k:16 * k + n] for k in range(5))
            tiles_i = work[1][:, 7, 0:n].bitcast(I32)
            nodes = 2 * B * T
            row_in, shift = work[1][:, 11, 0:nodes], work[1][:, 12, 0:nodes]
            beyond = slot(0, 5, 4)[:, 0:nodes * n].rearrange("p (r e) -> p r e", r=nodes)
            row_flat = row_of[:, 0:B * T, :].rearrange("p t k -> p (t k)")
            with nc.Block() as block:
                @block.gpsimd
                def _(pool):
                    ch = Chain(pool, S["pool_own"])
                    scatter_gpsimd(pool)
                    nc.gpsimd.memset(work[1][:, 8, 0:P], 0.0)
                    nc.gpsimd.iota(count_j, [[1, jobs]], base=0, channel_multiplier=0,
                                   allow_small_or_imprecise_dtypes=True).then_inc(S["count_j"], 1)
                    ch.link(nc.gpsimd.iota(work[1][:, 9, 0:n], [[0, n]], base=0, channel_multiplier=1,
                                           allow_small_or_imprecise_dtypes=True))
                    ch.link(nc.gpsimd.tensor_tensor(work[1][:, 9, 0:n], work[1][:, 9, 0:n], place[:, 0:n], ALU.add))
                    ch.link(nc.gpsimd.tensor_copy(work[1][:, 10, 0:n].bitcast(I32), work[1][:, 9, 0:n]))
                    nc.gpsimd.dma_start(moe_in[n * REGION:n * REGION + P, :], work[1][:, 8, 0:P]).then_inc(S["scattered"], 16)
                    for e in range(n):
                        nc.gpsimd.indirect_dma_start(
                            out=moe_in, out_offset=bass.IndirectOffsetOnAxis(ap=work[1][:, 10, e:e + 1].bitcast(I32), axis=0),
                            in_=work[1][:, 8, 0:P], in_offset=None).then_inc(S["scattered"], 16)
                    pool.wait_ge(S["scattered"], 16 * (n + 1 + 2 * T * U))

                @block.vector
                def _(dve):
                    ch = Chain(dve, S["dve_own"])
                    tt, ts = nc.vector.tensor_tensor, nc.vector.tensor_scalar
                    first = region_of[:, 0:n]
                    wide = [1, jobs, n]
                    ch.link(tt(tiles_e, place[:, 0:n], first, ALU.subtract))
                    ch.link(ts(tiles_e, tiles_e, float(P - 1), None, ALU.add))
                    ch.link(nc.vector.tensor_copy(tiles_i, tiles_e))
                    ch.link(ts(tiles_i, tiles_i, 7, None, ALU.logical_shift_right))
                    ch.link(nc.vector.tensor_copy(tiles_e, tiles_i))
                    ch.link(nc.vector.memset(ones, 1.0))
                    ch.link(nc.vector.tensor_tensor_scan(upto, ones, tiles_e, 0.0, ALU.mult, ALU.add))
                    ch.link(tt(offset, tiles_e, upto, ALU.subtract))
                    ch.link(nc.vector.scalar_tensor_tensor(out=offset, in0=offset, scalar=float(P), in1=first,
                                                           op0=ALU.mult, op1=ALU.add))
                    nc.vector.tensor_copy(row_in, row_flat)
                    nc.vector.tensor_copy(step[:, 0:1], offset[:, 0:1])
                    ch.link(tt(step[:, 1:n], offset[:, 1:n], offset[:, 0:n - 1], ALU.subtract))
                    by_node = [P, nodes, n]
                    ch.link(tt(beyond, row_in.unsqueeze(2).to_broadcast(by_node), first.unsqueeze(1).to_broadcast(by_node),
                               ALU.is_ge))
                    ch.link(tt(beyond, beyond, step.unsqueeze(1).to_broadcast(by_node), ALU.mult))
                    ch.link(nc.vector.tensor_reduce(shift, beyond, AX.X, ALU.add))
                    ch.link(tt(row_in, row_in, shift, ALU.subtract))
                    nc.vector.tensor_copy(row_flat, row_in)
                    dve.wait_ge(S["count_j"], 1)
                    ch.link(tt(grid, count_j.unsqueeze(2).to_broadcast(wide), upto[0:1].unsqueeze(1).to_broadcast(wide), ALU.is_ge))
                    ch.link(nc.vector.tensor_reduce(job_e, grid, AX.X, ALU.add))
                    ch.link(tt(grid, job_e.unsqueeze(2).to_broadcast(wide), iota32[0:1, 0:n].unsqueeze(1).to_broadcast(wide),
                               ALU.is_equal))
                    ch.link(tt(grid, grid, offset[0:1].unsqueeze(1).to_broadcast(wide), ALU.mult))
                    ch.link(nc.vector.tensor_reduce(base, grid, AX.X, ALU.add))
                    ch.link(nc.vector.scalar_tensor_tensor(out=base, in0=count_j, scalar=float(P), in1=base,
                                                           op0=ALU.mult, op1=ALU.add))
                    ch.link(ts(dummy, job_e, float(n), None, ALU.is_ge))
                    ch.link(ts(read, base, -1.0, float(n * REGION), ALU.mult, ALU.add))
                    ch.link(tt(read, read, dummy, ALU.mult))
                    ch.link(tt(read, read, base, ALU.add))
                    nc.vector.tensor_copy(job[:, 1, 0:jobs], read)
                    ch.link(ts(job_e, job_e, float(n - 1), None, ALU.min))
                    nc.vector.tensor_copy(job[:, 0, 0:jobs], job_e)
            clear()
            with nc.Block() as block:
                @block.vector
                def _(dve):
                    nc.vector.tensor_copy(place[:], region_of[:])
            clear()

        def experts_phase(n, jobs, hidden, chunks, up, down, finish_x, finish_up, finish_hT, bias):
            group = max(g for g in range(1, 19) if jobs % g == 0)
            why = "the table holds rows of the regions"

            def loaded(eng, turn, k, j, top):
                return eng.value_load(job[0:1, k, bass.ds(turn * group + j, 1)], min_val=0, max_val=top)

            def rows_at(u, first, j):
                return work[u][:, first + (j // 2) // 4, cols((j // 2) % 4)]

            with nc.Fori(0, jobs // group) as turn:
                with nc.Block() as block:
                    @block.sync
                    def _(sp):
                        for j in range(group):
                            r = loaded(sp, turn, 1, j, n * REGION)
                            sp.dma_start(rows_at(j % 2, 0, j), moe_in[bass.ds(r, P), :]).then_inc(S[f"rows_in{j}"], 16)
                            if bias is not None:
                                e = loaded(sp, turn, 0, j, n - 1)
                                sp.dma_start(rows_at(j % 2, 4, j)[0:1, :], bias[bass.ds(e, 1), :]).then_inc(S[f"rows_in{j}"], 16)

                    per_tile = 16 if bias is None else 32

                    @block.tensor
                    def _(pe):
                        expert = {}
                        for s in range(group + 3):
                            j = s
                            if j < group:
                                expert[j] = loaded(pe, turn, 0, j, n - 1)
                                pe.wait_ge(S[f"rows_in{j}"], per_tile)
                                if j >= 2:
                                    pe.wait_ge(S["t_x_chan"], j - 1)
                                nc.tensor.transpose(PS[j % 2][:, 0, 0:P], rows_at(j % 2, 0, j), ident[:]).then_inc(S["t_x"], 1)
                            j = s - 1
                            if 0 <= j < group:
                                pe.wait_ge(S["t_x_chan"], j + 1)
                                if j >= 2:
                                    pe.wait_ge(S["t_hidden"], j - 1)
                                for b, w in enumerate(up):
                                    mm = nc.tensor.matmul(PS[j % 2][:, 1 + b, 0:hidden], work[j % 2][:, 3, cols((j // 2) % 2)],
                                                          w(expert[j]), start=True, stop=True)
                                mm.then_inc(S["t_up"], 1)
                            j = s - 2
                            if 0 <= j < group:
                                pe.wait_ge(S["t_hidden"], j + 1)
                                if j >= 2:
                                    pe.wait_ge(S["t_out_sb"], j - 1)
                                for f, w in enumerate(chunks):
                                    mm = nc.tensor.transpose(PS[j % 2][0:w, 3, cols(f)],
                                                             work[j % 2][:, 8 + (j // 2) % 2, P * f:P * f + w], ident[:])
                                mm.then_inc(S["t_turned"], 1)
                            j = s - 3
                            if 0 <= j < group:
                                pe.wait_ge(S["t_hT"], j + 1)
                                if bias is not None:
                                    nc.tensor.matmul(PS[j % 2][:, 3, 3 * P:4 * P], ones_row[:], rows_at(j % 2, 4, j)[0:1, :], start=True, stop=False)
                                for f, w in enumerate(chunks):
                                    mm = nc.tensor.matmul(PS[j % 2][:, 3, 3 * P:4 * P], work[j % 2][0:w, 10 + (j // 2) % 2, cols(f)],
                                                          down(expert[j], f, w), start=(f == 0 and bias is None),
                                                          stop=(f == len(chunks) - 1))
                                mm.then_inc(S["t_out"], 1)

                    @block.scalar
                    def _(act):
                        for s in range(group + 3):
                            if s < group:
                                j = s
                                act.wait_ge(S["t_x"], j + 1)
                                if j >= 4:
                                    act.wait_ge(S["t_up"], j - 3)
                                finish_x(work[j % 2][:, 3, cols((j // 2) % 2)], PS[j % 2][:, 0, 0:P]).then_inc(S["t_x_chan"], 1)
                            j = s - 1
                            if 0 <= j < group:
                                act.wait_ge(S["t_up"], j + 1)
                                finish_up[0](act, j)
                            j = s - 2
                            if 0 <= j < group:
                                act.wait_ge(S["t_turned"], j + 1)
                                if j >= 4:
                                    act.wait_ge(S["t_out"], j - 3)
                                finish_hT(act, lambda: loaded(act, turn, 0, j, n - 1), j)
                            j = s - 3
                            if 0 <= j < group:
                                act.wait_ge(S["t_out_sb"], j + 1)
                                act.dma_start(moe_out[bass.ds(turn * (group * P) + j * P, P), :], rows_at(j % 2, 12, j))\
                                    .then_inc(S["out_written"], 16)
                        act.wait_ge(S["out_written"], 16 * group)

                    @block.vector
                    def _(dve):
                        ch = Chain(dve, S["dve_own"])
                        for s in range(group + 2):
                            j = s
                            if j < group:
                                finish_up[1](dve, ch, j)
                            j = s - 2
                            if j >= 0:
                                dve.wait_ge(S["t_out"], j + 1)
                                nc.vector.tensor_copy(rows_at(j % 2, 12, j), PS[j % 2][:, 3, 3 * P:4 * P]).then_inc(S["t_out_sb"], 1)
                clear()

        def swiglu_experts():
            def tanh(act, j):
                if j >= 4:
                    act.wait_ge(S["t_hidden"], j - 3)
                nc.scalar.activation(work[j % 2][:, 4 + (j // 2) % 2, 0:HID], PS[j % 2][:, 1, 0:HID], ACT.Tanh, scale=0.5)\
                    .then_inc(S["t_tanh"], 1)

            def silu_up(dve, ch, j):
                v = (j // 2) % 2
                gate = work[j % 2][:, 6 + v, 0:HID]
                dve.wait_ge(S["t_tanh"], j + 1)
                ch.link(nc.vector.scalar_tensor_tensor(out=gate, in0=work[j % 2][:, 4 + v, 0:HID], scalar=1.0,
                                                       in1=PS[j % 2][:, 1, 0:HID], op0=ALU.add, op1=ALU.mult))
                if j >= 4:
                    dve.wait_ge(S["t_turned"], j - 3)
                nc.vector.scalar_tensor_tensor(out=work[j % 2][:, 8 + v, 0:HID], in0=gate, scalar=0.5,
                                               in1=PS[j % 2][:, 2, 0:HID], op0=ALU.mult, op1=ALU.mult)\
                    .then_inc(S["t_hidden"], 1)

            def hT(act, e, j):
                v = (j // 2) % 2
                nc.scalar.activation(work[j % 2][:, 10 + v, 0:2 * P], PS[j % 2][:, 3, 0:2 * P], ACT.Copy)
                nc.scalar.activation(work[j % 2][0:FW[2], 10 + v, 2 * P:3 * P], PS[j % 2][0:FW[2], 3, 2 * P:3 * P], ACT.Copy)\
                    .then_inc(S["t_hT"], 1)

            experts_phase(
                E2, TILES(E2), HID, FW,
                [lambda e: e2_w1[:, bass.ds(e, 1), :].rearrange("c o m -> c (o m)"),
                 lambda e: e2_w3[:, bass.ds(e, 1), :].rearrange("c o m -> c (o m)")],
                lambda e, f, w: e2_w2[0:w, bass.ds(e, 1), f, :].rearrange("m o c -> m (o c)"),
                lambda dst, src: nc.scalar.activation(dst, src, ACT.Copy, scale=a_ln2[:]),
                (tanh, silu_up), hT, None)

        def relu_experts():
            def nothing(act, j):
                pass

            def hidden(dve, ch, j):
                dve.wait_ge(S["t_up"], j + 1)
                if j >= 4:
                    dve.wait_ge(S["t_turned"], j - 3)
                nc.vector.tensor_copy(work[j % 2][:, 8 + (j // 2) % 2, 0:2 * P], PS[j % 2][:, 1, 0:2 * P])\
                    .then_inc(S["t_hidden"], 1)

            def hT(act, e, j):
                expert = e()
                for f in range(2):
                    ins = nc.scalar.activation(work[j % 2][:, 10 + (j // 2) % 2, cols(f)], PS[j % 2][:, 3, cols(f)], ACT.Relu,
                                               bias=e3_b1[:, bass.ds(expert, 1), f])
                ins.then_inc(S["t_hT"], 1)

            experts_phase(
                E3, TILES(E3), 2 * P, [P, P],
                [lambda e: e3_w1[:, bass.ds(e, 1), :, :].rearrange("c o f m -> c (o f m)")],
                lambda e, f, w: e3_w2[:, bass.ds(e, 1), f, :].rearrange("m o c -> m (o c)"),
                lambda dst, src: nc.scalar.activation(dst, src, ACT.Copy),
                (nothing, hidden), hT, d["e3_b2"])

        engines = {e.engine for e in (nc.tensor, nc.vector, nc.scalar, nc.gpsimd, nc.sync)}

        def clear():
            nc.gpsimd.dma_reset(S.numbers())
            nc.multi_engine_barrier(engines, sems_to_clear=S.numbers())

        def graph(t, turn, u):
            return t[bass.ds(U * turn + u, 1)].rearrange("o (t p) c -> p (o t) c", p=P)

        def broadcast_rows(*pairs):
            with nc.Block() as block:
                @block.sync
                def _(sp):
                    for dst, src in pairs:
                        sp.dma_start(dst, src.partition_broadcast(P)).then_inc(S["weights_in"], 16)
                    sp.wait_ge(S["weights_in"], 16 * len(pairs))

        def first_phase():
            with nc.Fori(0, B // U) as turn:
                with nc.Block() as block:
                    @block.sync
                    def _(sp):
                        for u in range(U):
                            sp.dma_start(x[u][:], graph(d["x"], turn, u)).then_inc(S[f"x_in{u}"], 16)
                            sp.dma_start(work[u][:, 9:13, :], graph(d["adj"], turn, u)).then_inc(S[f"adj_in{u}"], 16)
                        for u in range(U):
                            sp.dma_start(adjT[u][:], graph(d["adj_t"], turn, u)).then_inc(S[f"adjT_in{u}"], 16)
                        for u in range(U):
                            sp.wait_ge(S["e2_base"], nth(0, u))
                            sp.dma_start(graph(carry_x, turn, u), x[u][:]).then_inc(S["out_written"], 16)
                        sp.wait_ge(S["out_written"], 16 * U)

                    @block.tensor
                    def _(pe):
                        gat_tensor(pe)
                        mamba_tensor(pe)
                        gcn_tensor(pe)
                        top1_tensor(pe)
                        gru_tensor(pe)
                        attn_tensor(pe)

                    @block.scalar
                    def _(act):
                        gat_scalar(act)
                        mamba_scalar(act)
                        gcn_scalar(act)
                        top1_scalar(act)
                        gru_scalar(act)
                        attn_scalar(act)

                    @block.vector
                    def _(dve):
                        ch = Chain(dve, S["dve_own"])
                        x_0 = gat_vector(dve, ch)
                        x_1 = mamba_vector(dve, ch, updated(dve, 0, x_0))
                        x_2 = gcn_vector(dve, ch, updated(dve, 1, x_1))
                        x_3 = top1_vector(dve, ch, updated(dve, 2, x_2))
                        x_4 = gru_vector(dve, ch, updated(dve, 3, x_3))
                        attn_vector(dve, ch, turn, updated(dve, 4, x_4))

                    @block.gpsimd
                    def _(pool):
                        ch = Chain(pool, S["pool_own"])
                        gat_gpsimd(pool, ch)
                        mamba_gpsimd(pool, ch)
                        gcn_gpsimd(pool, ch)
                        top1_gpsimd(pool, ch)
                        scatter_gpsimd(pool)
                        gru_gpsimd(pool, ch)
                        attn_gpsimd(pool, ch)
                clear()

        def second_phase():
            broadcast_rows((r_gamma, d["r_gamma"]), (r_beta, d["r_beta"]))
            first_gather(E2)
            with nc.Fori(0, B // U) as turn:
                with nc.Block() as block:
                    @block.sync
                    def _(sp):
                        for u in range(U):
                            sp.dma_start(x[u][:], graph(carry_x, turn, u)).then_inc(S[f"x_in{u}"], 16)
                            sp.dma_start(adjT[u][:], graph(d["adj_t"], turn, u)).then_inc(S[f"adjT_in{u}"], 16)
                        for u in range(U):
                            sp.wait_ge(S[f"x_in{u}"], 16)
                            sp.wait_ge(S["x"], nth(0, u))
                            sp.dma_start(graph(carry_x, turn, u), x[u][:]).then_inc(S["out_written"], 16)
                            sp.wait_ge(S["normed"], nth(2, u))
                            sp.dma_start(graph(carry_h, turn, u), sent[u][:]).then_inc(S["out_written"], 16)
                        sp.wait_ge(S["out_written"], 32 * U)

                    @block.tensor
                    def _(pe):
                        root_tensor(pe)
                        top2_tensor(pe)

                    @block.scalar
                    def _(act):
                        root_scalar(act)
                        top2_scalar(act)

                    @block.vector
                    def _(dve):
                        ch = Chain(dve, S["dve_own"])
                        x_6 = root_vector(dve, ch, turn)
                        top2_vector(dve, ch, turn, updated(dve, 0, x_6))

                    @block.gpsimd
                    def _(pool):
                        ch = Chain(pool, S["pool_own"])
                        root_gpsimd(pool, ch)
                        top2_gpsimd(pool, ch)
                        for u in range(U):
                            pool.wait_ge(S[f"gathered{u}"], 16 * 2 * T)
                clear()

        def last_phase():
            broadcast_rows((e3_gamma, d["e3_gamma"]), (e3_beta, d["e3_beta"]))
            first_gather(E3)
            with nc.Fori(0, B // U) as turn:
                with nc.Block() as block:
                    @block.sync
                    def _(sp):
                        for u in range(U):
                            sp.dma_start(xh[u][:], graph(carry_h, turn, u)).then_inc(S[f"h_in{u}"], 16)
                            sp.dma_start(x[u][:], graph(carry_x, turn, u)).then_inc(S[f"x_in{u}"], 16)
                        for u in range(U):
                            sp.wait_ge(S["x"], nth(0, u))
                            sp.dma_start(graph(out, turn, u), x[u][:]).then_inc(S["out_written"], 16)
                        sp.wait_ge(S["out_written"], 16 * U)

                    @block.vector
                    def _(dve):
                        last_vector(dve, Chain(dve, S["dve_own"]), turn)

                    @block.gpsimd
                    def _(pool):
                        last_gpsimd(pool, None)
                        for u in range(U):
                            pool.wait_ge(S[f"gathered{u}"], 16 * 2 * T)
                clear()

        clear()
        S.release()
        for phase in (first_phase, lambda: table_phase(E2, TILES(E2)), swiglu_experts, second_phase,
                      lambda: table_phase(E3, TILES(E3)), relu_experts, last_phase):
            phase()
            S.release()


def kernel(**inputs):
    import numpy as np
    import concourse.bacc as bacc
    from concourse.bass_utils import run_bass_kernel_spmd

    g = {k: np.asarray(v) for k, v in inputs.items()}

    def experts_out(w):
        return w.transpose(2, 0, 1)

    def rows(w):
        return w.reshape(-1, P, *w.shape[1:]).swapaxes(0, 1)

    head = np.arange(HDA)
    swap = (head + HDA // 2) % HDA
    q_cols = np.arange(NHA * HDA)
    q_swap = (q_cols // HDA) * HDA + swap[q_cols % HDA]
    k_cols = (q_cols // HDA // 2) * HDA + q_cols % HDA
    k_swap = (q_cols // HDA // 2) * HDA + swap[q_cols % HDA]
    wq, wk = g["L2_ffn_wq"], g["L2_ffn_wk"]
    a_qk = np.concatenate([wq[q_cols].T, wq[q_swap].T, wk[k_cols].T, wk[k_swap].T], axis=1).reshape(P, 4, P)

    inv_freq = 1.0 / 10000.0 ** (np.arange(0, HDA, 2, dtype=np.float32) / HDA)
    freqs = np.outer(np.arange(N, dtype=np.float32), inv_freq)
    emb = np.concatenate([freqs, freqs], axis=-1)
    sign = np.where(head < HDA // 2, -1.0, 1.0).astype(np.float32)
    a_cos = np.tile(np.cos(emb).T, (NHA, 1)).astype(np.float32)
    a_sin = np.tile((np.sin(emb) * sign).T, (NHA, 1)).astype(np.float32)

    arrays = {
        "x": g["x"], "adj": g["adj"], "adj_t": g["adj"].transpose(0, 2, 1),
        "gat_w": g["L0_gnn_W"], "gat_wt": g["L0_gnn_W"].T, "gat_a": g["L0_gnn_a"].reshape(2, P).T,
        "m_in": g["L0_ffn_W_in"], "m_conv_w": rows(g["L0_ffn_conv_w"]), "m_conv_b": rows(g["L0_ffn_conv_b"]),
        "m_dt_bias": g["L0_ffn_dt_bias"], "m_a_log": g["L0_ffn_A_log"], "m_d": g["L0_ffn_D"],
        "m_norm_w": rows(g["L0_ffn_norm_w"]), "m_out_t": g["L0_ffn_W_out"].T, "m_lin": g["L0_ffn_W_lin"],
        "m_b_lin": g["L0_ffn_b_lin"],
        "gcn_w": g["L1_gnn_weight"], "gcn_b": g["L1_gnn_bias"],
        "e1_router_t": g["L1_ffn_router_w"].T, "e1_rb": g["L1_ffn_router_b"],
        "e1_w1": g["L1_ffn_W1"].transpose(1, 0, 2).reshape(P, 8, P), "e1_b1": rows(g["L1_ffn_b1"].reshape(-1)),
        "e1_w2": rows(g["L1_ffn_W2"].reshape(-1, P)), "e1_b2": g["L1_ffn_b2"],
        "g_se_t": g["L2_gnn_w_se"].T, "g_se_b": g["L2_gnn_b_se"][:, None],
        "g_c1_t": g["L2_gnn_conv1_w"][:, :, 0].T, "g_c2_t": g["L2_gnn_conv2_w"].transpose(1, 2, 0),
        "g_msg_t": g["L2_gnn_w_msg"].T, "g_msg_b": g["L2_gnn_b_msg"],
        "g_ih_t": rows(g["L2_gnn_w_ih"].T), "g_hh_t": g["L2_gnn_w_hh"].T,
        "g_b_ih": rows(g["L2_gnn_b_ih"]), "g_b_hh": rows(g["L2_gnn_b_hh"]),
        "a_ln1": g["L2_ffn_ln1_w"][:, None], "a_ln2": g["L2_ffn_ln2_w"][:, None], "a_qk": a_qk,
        "a_v_t": g["L2_ffn_wv"].T, "a_o_t": g["L2_ffn_wo"].T, "a_cos": a_cos, "a_sin": a_sin,
        "e2_router_t": g["L2_ffn_router_w"].T, "e2_w1_t": experts_out(g["L2_ffn_w1"]),
        "e2_w3_t": experts_out(g["L2_ffn_w3"]), "e2_w2_t": experts_out(g["L2_ffn_w2"]),
        "r_rel": g["L3_gnn_W_rel"], "r_root": g["L3_gnn_W_root"], "r_b": g["L3_gnn_b_rel"],
        "r_gamma": g["L3_gnn_ln_gamma"], "r_beta": g["L3_gnn_ln_beta"],
        "e3_gate": g["L3_ffn_gate_w"], "e3_gb": g["L3_ffn_gate_b"], "e3_w1": g["L3_ffn_w1"].transpose(1, 0, 2).reshape(P, E3, 2, P),
        "e3_b1": g["L3_ffn_b1"].reshape(E3, 2, P).transpose(2, 0, 1),
        "e3_w2": g["L3_ffn_w2"].reshape(E3, 2, P, P).transpose(2, 0, 1, 3), "e3_b2": g["L3_ffn_b2"],
        "e3_gamma": g["L3_ffn_gamma"], "e3_beta": g["L3_ffn_beta"],
    }
    arrays["g_bn"] = np.stack([g[f"L2_gnn_bn{n}_{k}"] for n in (1, 2) for k in "gbmv"], axis=1)

    nc = bacc.Bacc("TRN2", target_bir_lowering=False, num_devices=1)
    feed, d = {}, {}
    for name, a in arrays.items():
        a = np.ascontiguousarray(a)
        feed[f"in_{name}_dram"] = a
        d[name] = nc.dram_tensor(f"in_{name}_dram", a.shape, mybir.dt.from_np(a.dtype), kind="ExternalInput").ap()
    out = nc.dram_tensor("out_0_dram", g["x"].shape, F32, kind="ExternalOutput").ap()
    build_network(nc, d, out)
    return run_bass_kernel_spmd(nc, [feed], core_ids=[0]).results[0]["out_0_dram"]
```

```python
from contextlib import ExitStack

import concourse.bass as bass
from concourse import mybir
from concourse.alu_op_type import AluOpType as ALU

ACT = mybir.ActivationFunctionType
AX = mybir.AxisListType
F32 = mybir.dt.float32
F32R = mybir.dt.float32r
BF16 = mybir.dt.bfloat16
U32 = mybir.dt.uint32
I32 = mybir.dt.int32

P = 128
N = 512
T = N // P
U = 2
NEG = -9.0e15
LN_EPS = 1e-5
RMS_EPS = 1e-6
HID, FCH = 341, 3
FW = [min(P, HID - P * f) for f in range(FCH)]
E1, E2, E3 = 32, 8, 16
TAPS, PAD = 17, 8
NHM, HDM, DST = 4, 64, 64
NHA, HDA = 4, 32
SLOTS = 15


def nth(k, u):
    return U * k + u + 1


class Semaphores:

    def __init__(self, ctx, nc):
        self.ctx, self.nc, self.all, self.of = ctx, nc, [], {}

    def __getitem__(self, name):
        if name not in self.of:
            if len(self.of) == len(self.all):
                self.all.append(self.ctx.enter_context(self.nc.semaphore(f"signal_{len(self.all)}")))
            self.of[name] = self.all[len(self.of)]
        return self.of[name]

    def numbers(self):
        used = [self.all[k].num for k in range(len(self.of))]
        assert used == list(range(used[0], used[0] + len(used)))
        return range(used[0], used[0] + len(used))

    def release(self):
        self.of = {}


class Chain:

    def __init__(self, engine, sem):
        self.engine, self.sem, self.n = engine, sem, 0

    def mark(self, ins):
        ins.then_inc(self.sem, 1)
        self.n += 1
        return self.n

    def wait(self, n):
        self.engine.wait_ge(self.sem, n)

    def link(self, ins):
        self.wait(self.mark(ins))


def build_network(nc, d, out):
    B = out.shape[0]
    REGION = B * N + P

    def TILES(n):
        return 2 * B * T + n

    with ExitStack() as ctx:
        def sb(name, shape, dt=F32):
            return ctx.enter_context(nc.sbuf_tensor(name, shape, dt))

        S = Semaphores(ctx, nc)

        ident = sb("ident", [P, P])
        ident_h = sb("ident_h", [P, P], BF16)
        upper = sb("upper", [P, P])
        causal = sb("causal", [P, P], BF16)
        minus_half = sb("minus_half", [P, T])
        iota32 = sb("iota32", [P, E1])
        pick = sb("pick", [E1, E1 // 4, P], BF16)

        gat_w = sb("gat_w", [P, P])
        gat_a = sb("gat_a", [P, 2])
        gat_wa = sb("gat_wa", [P, 2])
        gat_wdst = sb("gat_wdst", [P, P])

        m_in = sb("m_in", [P, 644])
        m_taps = sb("m_taps", [P, 3, 4])
        m_convb = sb("m_convb", [P, 3])
        m_dtb = sb("m_dtb", [P, NHM])
        m_a = sb("m_a", [P, NHM])
        m_d = sb("m_d", [P, NHM])
        m_norm = sb("m_norm", [P, 2])
        m_wol = sb("m_wol", [P, 2, P])
        m_blin = sb("m_blin", [P, P])

        PARTS = 96
        part_rows = sb("part_rows", [PARTS, 16], BF16)
        bias_parts = sb("bias_parts", [PARTS, 3 + E3, P], BF16)
        gcn_b, g_msgb, r_b = (bias_parts[:, k, :] for k in range(3))
        e3_b2 = bias_parts[:, 3:3 + E3, :]

        gcn_w = sb("gcn_w", [P, P])

        e1_router = sb("e1_router", [P, E1])
        e1_rb = sb("e1_rb", [P, E1])
        e1_w1 = sb("e1_w1", [P, 8, P])
        e1_b1 = sb("e1_b1", [P, 8])
        e1_w2 = sb("e1_w2", [P, 8, P])
        e1_b2 = sb("e1_b2", [E1, P])

        g_se = sb("g_se", [P, 96])
        g_seb = sb("g_seb", [96, 1])
        g_seb2 = sb("g_seb2", [32, 1])
        g_c1 = sb("g_c1", [P, P])
        g_c2_high = sb("g_c2_high", [P, TAPS, P], F32R)
        g_c2_low = sb("g_c2_low", [P, TAPS, P], F32R)
        g_bn = sb("g_bn", [P, 8])
        g_s = sb("g_s", [P, 2])
        g_c = sb("g_c", [P, 2])
        g_msg = sb("g_msg", [P, P])
        g_ih = sb("g_ih", [P, 2, 3 * P])
        g_hh = sb("g_hh", [P, 3 * P])
        g_bi = sb("g_bi", [P, 3])
        g_bh = sb("g_bh", [P, 3])
        g_half = sb("g_half", [P, 3])

        a_ln1 = sb("a_ln1", [P, 1])
        a_ln2 = sb("a_ln2", [P, 1])
        a_qk = sb("a_qk", [P, 4, P])
        a_v = sb("a_v", [P, 2 * HDA])
        a_o = sb("a_o", [P, P])
        a_cos = sb("a_cos", [P, N])
        a_sin = sb("a_sin", [P, N])
        e2_router = sb("e2_router", [P, E2])
        ups, downs = E2 * HID, E2 * FCH * P
        experts = sb("experts", [P, max(2 * ups + downs, 2 * E3 * 2 * P)])
        e2_w1 = experts[:, 0:ups].rearrange("p (e m) -> p e m", e=E2)
        e2_w3 = experts[:, ups:2 * ups].rearrange("p (e m) -> p e m", e=E2)
        e2_w2 = experts[:, 2 * ups:2 * ups + downs].rearrange("p (e f c) -> p e f c", e=E2, f=FCH)
        e3_w1, e3_w2 = (experts[:, E3 * 2 * P * k:E3 * 2 * P * (k + 1)].rearrange("p (e f c) -> p e f c", e=E3, f=2)
                        for k in range(2))

        r_rel = sb("r_rel", [P, P])
        r_root = sb("r_root", [P, P])

        e3_gate = sb("e3_gate", [P, E3])
        e3_gb = sb("e3_gb", [P, E3])
        e3_b1 = sb("e3_b1", [P, E3, 2])

        strict = sb("strict", [P, P], BF16)
        ones_h = sb("ones_h", [P, P], BF16)
        region_of = sb("region_of", [P, E3])
        place = sb("place", [P, E3])
        row_of = sb("row_of", [P, (B + 2 * U) * T, 2], I32)
        weight_of = sb("weight_of", [P, B * T, 2])
        moe_in = nc.dram_tensor("moe_in", (E3 * REGION + 2 * T * U * P, P), F32, kind="Internal").ap()
        moe_out = nc.dram_tensor("moe_out", (P * TILES(E3), P), F32, kind="Internal").ap()
        carry_x = nc.dram_tensor("carry_x", (B, N, P), F32, kind="Internal").ap()
        carry_h = nc.dram_tensor("carry_h", (B, N, P), F32, kind="Internal").ap()

        def per(name, shape, dt=F32):
            return [sb(f"{name}{u}", shape, dt) for u in range(U)]

        x = per("x", [P, T, P])
        xh = per("xh", [P, T, P])
        xT = per("xT", [P, N])
        adjT = per("adjT", [P, T, N])
        work = per("work", [P, SLOTS, N])
        stats = per("stats", [P, T, 6])
        mv = per("mv", [P, T, 2])
        var = per("var", [P, T])
        rstd = per("rstd", [P, T])
        lg = per("lg", [P, T, E1])
        top = per("top", [P, T, 8])
        idx = per("idx", [P, T, 8], U32)
        idxf = per("idxf", [P, T, 2])
        oh = per("oh", [P, T, E1])
        oh2 = per("oh2", [P, T, E3])
        wts = per("wts", [P, T, E3 + 2])
        rows = per("rows", [P, T, 2], I32)
        sent = per("sent", [P, T, P])
        sent_to = per("sent_to", [P, T, 2], I32)
        chosen = per("chosen", [P, T, E3], BF16)
        den = per("den", [P, T])
        den2 = per("den2", [P, T])
        sm = per("sm", [P, 8, 16])
        m_parts = per("m_parts", [PARTS, P], BF16)
        g_high = per("g_high", [P, N + 2 * PAD], F32R)
        g_low = per("g_low", [P, N + 2 * PAD], F32R)
        PS = [ctx.enter_context(nc.psum_tensor(f"PS{u}", [P, 4, N], F32)) for u in range(U)]

        def slot(u, a, n=1):
            return work[u][:, a:a + n, :].rearrange("p s n -> p (s n)")

        r_gamma, r_beta = work[0][:, 5, 0:P], work[0][:, 5, P:2 * P]
        e3_gamma, e3_beta = work[0][:, 5, 0:P], work[0][:, 5, P:2 * P]
        QUAD = 4

        def tiles_per_turn(jobs):
            return max(g for g in range(1, 41) if jobs % g == 0)

        def job_table(jobs):
            group = tiles_per_turn(jobs)
            aligned = -(-group // QUAD) * QUAD
            table = x[0][:, :, :].rearrange("p t c -> p (t c)")[0:1, 0:2 * (jobs // group) * aligned].bitcast(I32)
            return table.rearrange("p (k n j) -> p k n j", k=2, n=jobs // group)

        def tok(ap):
            return ap.rearrange("p (t c) -> p t c", t=T)

        def cols(t):
            return slice(P * t, P * (t + 1))

        with nc.Block() as block:
            loads = []
            g_c2 = slot(1, 0, 5)[:, 0:TAPS * P].rearrange("p (k c) -> p k c", k=TAPS)

            def load(dst, src):
                loads.append((dst, src))

            def bcast(ap, n=P):
                return ap.partition_broadcast(n)

            load(gat_w[:], d["gat_w"]); load(work[0][:, 2, 0:P], d["gat_wt"]); load(gat_a[:], d["gat_a"])
            load(m_in[:], d["m_in"])
            load(m_taps[:], d["m_conv_w"])
            load(m_convb[:], d["m_conv_b"])
            load(m_dtb[:], bcast(d["m_dt_bias"]))
            load(m_a[:], bcast(d["m_a_log"]))
            load(m_d[:], bcast(d["m_d"]))
            load(m_norm[:], d["m_norm_w"])
            load(m_blin[:], bcast(d["m_b_lin"]))
            load(work[0][:, 0, 0:256], d["m_out_t"])
            load(work[0][:, 1, 0:P], d["m_lin"])
            load(gcn_w[:], d["gcn_w"]);
            load(e1_router[:], d["e1_router_t"]); load(e1_rb[:], bcast(d["e1_rb"]))
            load(e1_w1[:], d["e1_w1"])
            load(e1_b1[:], d["e1_b1"])
            load(e1_w2[:], d["e1_w2"])
            load(e1_b2[:], d["e1_b2"])
            load(g_c1[:], d["g_c1_t"]); load(g_c2, d["g_c2_t"])
            load(g_bn[:], d["g_bn"])
            load(g_msg[:], d["g_msg_t"]);
            load(g_ih[:], d["g_ih_t"]); load(g_hh[:], d["g_hh_t"])
            load(g_bi[:], d["g_b_ih"])
            load(g_bh[:], d["g_b_hh"])
            load(a_ln1[:], d["a_ln1"]); load(a_ln2[:], d["a_ln2"])
            load(a_qk[:], d["a_qk"])
            load(a_v[:], d["a_v_t"]); load(a_o[:], d["a_o_t"])
            load(a_cos[:], d["a_cos"]); load(a_sin[:], d["a_sin"])
            load(e2_router[:], d["e2_router_t"])
            load(e2_w1[:], d["e2_w1_t"]); load(e2_w3[:], d["e2_w3_t"])
            for f in range(FCH):
                load(e2_w2[0:FW[f], :, f, :], d["e2_w2_t"][P * f:P * f + FW[f]])
            load(r_rel[:], d["r_rel"]); load(r_root[:], d["r_root"]);
            load(e3_gate[:], d["e3_gate"]); load(e3_gb[:], bcast(d["e3_gb"]))
            load(e3_b1[:], d["e3_b1"])
            late = []
            for k in range(3):
                late.append((g_se[:, 32 * k:32 * k + 3], d["g_se_t"]))
                late.append((g_seb[32 * k:32 * k + 3, :], d["g_se_b"]))
            late.append((g_seb2[0:3, :], d["g_se_b"]))
            all_loads = 16 * (len(loads) + len(late))
            bias = slot(0, 5, 5)[0:32, 0:(3 + E3) * P].rearrange("p (k c) -> p k c", k=3 + E3)
            middle = slot(0, 10, 3)[0:32, :].bitcast(BF16)[:, 0:(3 + E3) * P].rearrange("p (k c) -> p k c", k=3 + E3)
            biases = [(bias[0:1, 0, :], d["gcn_b"].unsqueeze(0)), (bias[0:1, 1, :], d["g_msg_b"].unsqueeze(0)),
                      (bias[0:1, 2, :], d["r_b"].unsqueeze(0)), (bias[0:1, 3:3 + E3, :], d["e3_b2"].unsqueeze(0))]

            @block.sync
            def _(sp):
                sp.wait_ge(S["bias_zeroed"], 1)
                for dst, src in biases:
                    sp.dma_start(dst, src).then_inc(S["biases_in"], 16)
                for dst, src in loads:
                    sp.dma_start(dst, src).then_inc(S["weights_in"], 16)
                sp.wait_ge(S["se_zeroed"], 1)
                for dst, src in late:
                    sp.dma_start(dst, src).then_inc(S["weights_in"], 16)
                sp.wait_ge(S["weights_in"], all_loads)

            @block.gpsimd
            def _(pool):
                ch = Chain(pool, S["pool_own"])
                nc.gpsimd.memset(bias, 0.0).then_inc(S["bias_zeroed"], 1)
                nc.gpsimd.memset(g_se[:], 0.0)
                nc.gpsimd.memset(g_seb2[:], 0.0)
                nc.gpsimd.memset(g_seb[:], 0.0).then_inc(S["se_zeroed"], 1)
                nc.gpsimd.memset(ident[:], 0.0)
                nc.gpsimd.memset(upper[:], 1.0)
                nc.gpsimd.memset(causal[:], 0.0)
                nc.gpsimd.memset(pick[:], 1.0e30)
                nc.gpsimd.memset(strict[:], 1.0)
                nc.gpsimd.memset(ones_h[:], 1.0)
                nc.gpsimd.memset(row_of[:], 0)
                for u in range(U):
                    nc.gpsimd.memset(m_parts[u][:], 0.0)
                    nc.gpsimd.memset(sent[u][:], 0.0)
                    nc.gpsimd.iota(sent_to[u][:], [[2 * P, T], [P, 2]], base=E3 * REGION + 2 * T * P * u, channel_multiplier=1)
                nc.gpsimd.iota(region_of[:], [[REGION, E3]], base=0, channel_multiplier=0,
                               allow_small_or_imprecise_dtypes=True)
                nc.gpsimd.iota(place[:], [[REGION, E3]], base=0, channel_multiplier=0,
                               allow_small_or_imprecise_dtypes=True)
                ch.link(nc.gpsimd.memset(minus_half[:], -0.5))
                nc.gpsimd.affine_select(out=strict[:], in_=strict[:], compare_op=ALU.is_gt, fill=0.0,
                                        base=0, pattern=[[1, P]], channel_multiplier=-1)
                nc.gpsimd.iota(iota32[:], [[1, E1]], base=0, channel_multiplier=0, allow_small_or_imprecise_dtypes=True)
                nc.gpsimd.affine_select(out=upper[:], in_=upper[:], compare_op=ALU.is_ge, fill=0.0,
                                        base=0, pattern=[[1, P]], channel_multiplier=-1)
                nc.gpsimd.affine_select(out=causal[:], in_=causal[:], compare_op=ALU.is_ge, fill=-1.0e30,
                                        base=0, pattern=[[-1, P]], channel_multiplier=1)
                ch.link(nc.gpsimd.affine_select(out=pick[:], in_=pick[:], compare_op=ALU.is_ge, fill=0.0, base=0,
                                                pattern=[[128, 8], [1, P]], channel_multiplier=-32))
                ch.link(nc.gpsimd.affine_select(out=pick[:], in_=pick[:], compare_op=ALU.is_ge, fill=0.0, base=31,
                                                pattern=[[-128, 8], [-1, P]], channel_multiplier=32))
                ch.link(nc.gpsimd.affine_select(out=ident[:], in_=ident[:], compare_op=ALU.not_equal, fill=1.0,
                                                base=0, pattern=[[-1, P]], channel_multiplier=1))
                ch.link(nc.gpsimd.tensor_copy(ident_h[:], ident[:]))
                for r in range(0, PARTS, 32):
                    ch.link(nc.gpsimd.tensor_copy(part_rows[r:r + 32, :], ident_h[r:r + 32, r:r + 16]))
                pool.wait_ge(S["bn_var"], 1)
                nc.gpsimd.tensor_tensor(g_s[:], sm[0][:, 0, 0:2], minus_half[:, 0:2], ALU.pow).then_inc(S["bn_pow"], 1)

            @block.tensor
            def _(pe):
                pe.wait_ge(S["weights_in"], all_loads)
                nc.tensor.matmul(PS[0][:, 0, 0:2], work[0][:, 2, 0:P], gat_a[:], start=True, stop=True)
                for i in range(2):
                    mm = nc.tensor.matmul(PS[0][:, 1 + i, 0:P], work[0][:, 0, cols(i)], work[0][:, 1, 0:P],
                                          start=True, stop=True)
                mm.then_inc(S["folded"], 1)

            @block.scalar
            def _(act):
                act.wait_ge(S["weights_in"], all_loads)
                nc.scalar.activation(m_a[:], m_a[:], ACT.Exp).then_inc(S["a_exp"], 1)

            @block.vector
            def _(dve):
                ch = Chain(dve, S["dve_own"])
                dve.wait_ge(S["biases_in"], 16 * len(biases))
                ch.link(nc.vector.tensor_copy(bias_parts[0:32, :, :], bias))
                ch.link(nc.vector.tensor_tensor(bias, bias, bias_parts[0:32, :, :], ALU.subtract))
                ch.link(nc.vector.tensor_copy(middle, bias))
                nc.vector.tensor_copy(bias_parts[32:64, :, :], middle)
                ch.link(nc.vector.tensor_tensor(bias, bias, middle, ALU.subtract))
                nc.vector.tensor_copy(bias_parts[64:PARTS, :, :], bias)
                dve.wait_ge(S["weights_in"], all_loads)
                bn = g_bn[:, :].rearrange("p (n k) -> p k n", k=4)
                nc.vector.tensor_scalar(sm[0][:, 0, 0:2], bn[:, 3, :], LN_EPS, None, ALU.add).then_inc(S["bn_var"], 1)
                ch.link(nc.vector.tensor_copy(g_c2_high[:], g_c2))
                nc.vector.tensor_tensor(g_c2_low[:], g_c2, g_c2_high[:].bitcast(F32), ALU.subtract)
                nc.vector.tensor_scalar(m_taps[:], m_taps[:], 0.5, None, ALU.mult)
                nc.vector.tensor_scalar(m_convb[:], m_convb[:], 0.5, None, ALU.mult)
                nc.vector.tensor_scalar(g_seb2[:], g_seb2[:], 2.0, None, ALU.mult)
                nc.vector.tensor_scalar(g_half[:, 2:3], g_bh[:, 2:3], 0.5, None, ALU.mult)
                ch.link(nc.vector.tensor_tensor(g_half[:, 0:2], g_bi[:, 0:2], g_bh[:, 0:2], ALU.add))
                nc.vector.tensor_scalar(g_half[:, 0:2], g_half[:, 0:2], 0.5, None, ALU.mult)
                dve.wait_ge(S["a_exp"], 1)
                nc.vector.tensor_scalar(m_a[:], m_a[:], -1.0, None, ALU.mult)
                dve.wait_ge(S["bn_pow"], 1)
                ch.link(nc.vector.tensor_tensor(g_s[:], g_s[:], bn[:, 0, :], ALU.mult))
                ch.link(nc.vector.tensor_tensor(sm[0][:, 0, 2:4], bn[:, 2, :], g_s[:], ALU.mult))
                nc.vector.tensor_tensor(g_c[:], bn[:, 1, :], sm[0][:, 0, 2:4], ALU.subtract)
                dve.wait_ge(S["folded"], 1)
                ch.link(nc.vector.tensor_copy(gat_wa[:], PS[0][:, 0, 0:2]))
                nc.vector.tensor_copy(gat_wdst[:], gat_wa[:, 1:2].to_broadcast([P, P]))
                for i in range(2):
                    nc.vector.tensor_scalar(m_wol[:, i, :], PS[0][:, 1 + i, 0:P], m_norm[:, i:i + 1], None, ALU.mult)

        def updated(dve, k, update):
            def ready(u):
                update(u)
                dve.wait_ge(S["x"], nth(k, u))
            return ready

        def norm_vector(dve, ch, k, src, dst, ready, together=False):
            def apply(u):
                dve.wait_ge(S["rstd"], nth(k, u))
                for t in range(T):
                    ins = nc.vector.tensor_scalar(dst[u][:, t, :], src[u][:, t, :], mv[u][:, t, 0:1],
                                                  rstd[u][:, t:t + 1], ALU.subtract, ALU.mult)
                ins.then_inc(S["normed"], 1)

            for u in range(U):
                ready(u)
                for t in range(T):
                    n = ch.mark(nc.vector.bn_stats(stats[u][:, t, :], src[u][:, t, :]))
                ch.wait(n)
                for t in range(T):
                    n = ch.mark(nc.vector.bn_aggr(mv[u][:, t, :], stats[u][:, t, :]))
                ch.wait(n)
                nc.vector.tensor_scalar(var[u][:], mv[u][:, :, 1], LN_EPS, None, ALU.add).then_inc(S["var"], 1)
                if not together:
                    apply(u)
            if together:
                for u in range(U):
                    apply(u)

        def rstd_gpsimd(pool, k):
            for u in range(U):
                pool.wait_ge(S["var"], nth(k, u))
                nc.gpsimd.tensor_tensor(rstd[u][:], var[u][:], minus_half[:], ALU.pow).then_inc(S["rstd"], 1)

        def turn_tensor(pe, k, src, ready, products):
            for u in range(U):
                ready(u)
                for t in range(T):
                    mm = nc.tensor.transpose(PS[u][:, 0, cols(t)], src(u)[:, t, :], ident[:])
                mm.then_inc(S["turned"], 1)
                if products:
                    products(u)

        def turn_scalar(act, k, dst, scale=None):
            for u in range(U):
                act.wait_ge(S["turned"], nth(k, u))
                if scale is None:
                    ins = nc.scalar.activation(dst(u), PS[u][:, 0, :], ACT.Copy)
                else:
                    ins = nc.scalar.activation(dst(u), PS[u][:, 0, :], ACT.Copy, scale=scale)
                ins.then_inc(S["chan"], 1)

        def top_index(dve, ch, u, n):
            for t in range(T):
                m = ch.mark(nc.vector.max(top[u][:, t, :], lg[u][:, t, 0:n]))
            ch.wait(m)
            for t in range(T):
                m = ch.mark(nc.vector.max_index(idx[u][:, t, :], top[u][:, t, :], lg[u][:, t, 0:n]))
            ch.wait(m)
            ch.link(nc.vector.tensor_copy(idxf[u][:], idx[u][:, :, 0:2]))

        def one_hot(dst, u, k, n):
            return nc.vector.tensor_tensor(dst[:, :, 0:n], iota32[:, 0:n].unsqueeze(1).to_broadcast([P, T, n]),
                                           idxf[u][:, :, k:k + 1].to_broadcast([P, T, n]), ALU.is_equal)

        def by_graph(u, it):
            return T * u + it + 1

        def gat_tensor(pe):
            turn_tensor(pe, 0, lambda u: xh[u], lambda u: pe.wait_ge(S["normed"], nth(0, u)), None)
            for u in range(U):
                pe.wait_ge(S["chan"], nth(0, u))
                nc.tensor.matmul(PS[u][:, 3, :], gat_wdst[:], xT[u][:], start=True, stop=True)
                for t in range(T):
                    mm = nc.tensor.matmul(PS[u][:, 2, t:t + 1], xT[u][:, cols(t)], gat_wa[:, 0:1], start=True, stop=True)
                mm.then_inc(S["gat_halves"], 1)
                for t in range(T):
                    mm = nc.tensor.matmul(PS[u][:, 1, cols(t)], xT[u][:, cols(t)], gat_w[:], start=True, stop=True)
                mm.then_inc(S["gat_products"], 1)
            for u in range(U):
                for it in range(T):
                    pe.wait_ge(S["gat_p"], by_graph(u, it))
                    if it == 0:
                        pe.wait_ge(S["gat_h"], nth(0, u))
                    if it == 1:
                        pe.wait_ge(S["gat_src"], nth(0, u))
                    if it >= 2:
                        pe.wait_ge(S[f"gat_pT{u}"], it - 1)
                    for jt in range(T):
                        mm = nc.tensor.transpose(PS[u][:, 1 + it % 2, cols(jt)], work[u][:, it, cols(jt)], ident[:])
                    mm.then_inc(S["gat_p_turned"], 1)
                for it in range(T):
                    pe.wait_ge(S[f"gat_pT{u}"], it + 1)
                    for jt in range(T):
                        mm = nc.tensor.matmul(PS[u][:, 0, cols(it)], work[u][:, 4 + it, cols(jt)],
                                              work[u][:, 8, cols(jt)], start=(jt == 0), stop=(jt == T - 1))
                mm.then_inc(S["gat_out"], 1)

        def gat_scalar(act):
            turn_scalar(act, 0, lambda u: xT[u][:])
            for u in range(U):
                act.wait_ge(S["gat_src"], nth(0, u))
                for it in range(T):
                    nc.scalar.activation(work[u][:, it, :], PS[u][:, 3, :], ACT.Identity,
                                         bias=sm[u][:, 0, it:it + 1]).then_inc(S["gat_sum"], 1)
                act.wait_ge(S["gat_products"], nth(0, u))
                nc.scalar.activation(work[u][:, 8, :], PS[u][:, 1, :], ACT.Copy).then_inc(S["gat_h"], 1)
            for u in range(U):
                for it in range(T):
                    act.wait_ge(S["gat_max"], by_graph(u, it))
                    nc.scalar.activation(work[u][:, it, :], work[u][:, it, :], ACT.Exp,
                                         bias=sm[u][:, 1, it:it + 1], accum_out=sm[u][:, 2, it:it + 1])\
                        .then_inc(S["gat_p"], 1)
            for it in range(T):
                act.wait_ge(S["gat_p_turned"], by_graph(1, it))
                nc.scalar.activation(work[1][:, 4 + it, :], PS[1][:, 1 + it % 2, :], ACT.Copy).then_inc(S["gat_pT1"], 1)

        def gat_vector(dve, ch):
            norm_vector(dve, ch, 0, x, xh, lambda u: None, True)
            for u in range(U):
                nc.vector.tensor_scalar(adjT[u][:], adjT[u][:], 0.0, NEG, ALU.is_le, ALU.mult).then_inc(S["gat_penalty"], 1)
                dve.wait_ge(S["gat_halves"], nth(0, u))
                nc.vector.tensor_copy(sm[u][:, 0, 0:T], PS[u][:, 2, 0:T]).then_inc(S["gat_src"], 1)
            tiles = [(u, it) for u in range(U) for it in range(T)]

            def leaky(u, it):
                e = work[u][:, it, :]
                dve.wait_ge(S["gat_sum"], by_graph(u, it))
                nc.vector.scalar_tensor_tensor(out=e, in0=e, scalar=0.2, in1=e, op0=ALU.mult, op1=ALU.max)\
                    .then_inc(S["gat_leaky"], 1)

            leaky(*tiles[0])
            leaky(*tiles[1])
            for u in range(U):
                for it in range(T):
                    e = work[u][:, it, :]
                    if T * u + it + 2 < len(tiles):
                        leaky(*tiles[T * u + it + 2])
                    dve.wait_ge(S["gat_masked"], by_graph(u, it))
                    nc.vector.tensor_reduce(sm[u][:, 1, it:it + 1], e, AX.X, ALU.max, negate=True).then_inc(S["gat_max"], 1)
                    if u == 1:
                        dve.wait_ge(S["gat_p_turned"], by_graph(0, it))
                        nc.vector.tensor_copy(work[0][:, 4 + it, :], PS[0][:, 1 + it % 2, :]).then_inc(S["gat_pT0"], 1)

            def update(u):
                dve.wait_ge(S["gat_p"], by_graph(u, T - 1))
                ch.link(nc.vector.reciprocal(den[u][:], sm[u][:, 2, 0:T]))
                dve.wait_ge(S["gat_out"], nth(0, u))
                for t in range(T):
                    ins = nc.vector.scalar_tensor_tensor(out=x[u][:, t, :], in0=PS[u][:, 0, cols(t)],
                                                         scalar=den[u][:, t:t + 1], in1=x[u][:, t, :],
                                                         op0=ALU.mult, op1=ALU.add)
                ins.then_inc(S["x"], 1)
            return update

        def gat_gpsimd(pool, ch):
            rstd_gpsimd(pool, 0)
            for u in range(U):
                pool.wait_ge(S["gat_penalty"], nth(0, u))
                for it in range(T):
                    e = work[u][:, it, :]
                    pool.wait_ge(S["gat_leaky"], by_graph(u, it))
                    nc.gpsimd.tensor_tensor(e, e, adjT[u][:, it, :], ALU.add).then_inc(S["gat_masked"], 1)

        def state(u, c):
            return work[u][0:DST, (5, 8)[c // 2], 256 * (c % 2):256 * (c % 2 + 1)]

        def heads(ap):
            return ap.rearrange("p (k w) -> p k w", k=T * NHM)

        def mamba_tensor(pe):

            def products(u):
                pe.wait_ge(S["chan"], nth(1, u))
                for i in range(3):
                    nc.tensor.matmul(PS[u][:, i, :], m_in[:, 256 + P * i:256 + P * (i + 1)], xT[u][:], start=True, stop=True)
                for c in range(T):
                    mm = nc.tensor.matmul(PS[u][:, 3, 4 * c:4 * c + 4], xT[u][:, cols(c)], m_in[:, 640:644],
                                          start=True, stop=True)
                mm.then_inc(S["m_projected"], 1)

            turn_tensor(pe, 1, lambda u: xh[u], lambda u: pe.wait_ge(S["normed"], nth(1, u)), products)
            for u in range(U):
                pe.wait_ge(S["m_silu"], nth(0, u))
                for c in range(T):
                    for i in range(2):
                        nc.tensor.transpose(PS[u][:, c // 2, cols(2 * (c % 2) + i)], work[u][:, 6 + i, cols(c)], ident[:])
                pe.wait_ge(S["m_silu_bc"], nth(0, u))
                for c in range(T):
                    nc.tensor.transpose(PS[u][:, 2, DST * c:DST * (c + 1)], work[u][0:DST, 8, cols(c)],
                                        ident[0:DST, 0:DST])
                pe.wait_ge(S["m_da"], nth(0, u))
                nc.tensor.matmul(PS[u][:, 3, 0:16], upper[:], sm[u][:, 1, :], start=True, stop=True)\
                    .then_inc(S["m_turned"], 1)
            for u in range(U):
                pe.wait_ge(S["m_x_tok"], nth(0, u))
                pe.wait_ge(S["m_cum"], nth(0, u))
                nc.tensor.transpose(PS[u][0:16, 1, 0:P], sm[u][:, 2, :], ident[:]).then_inc(S["m_cum_turned"], 1)
                for c in range(T):
                    mm = nc.tensor.matmul(PS[u][:, 0, cols(c)], work[u][0:DST, 8, cols(c)], work[u][0:DST, 9, cols(c)],
                                          start=True, stop=True)
                mm.then_inc(S["m_cb"], 1)
            for c in range(T):
                for u in range(U):
                    if c == 0:
                        pe.wait_ge(S["m_cum_parts"], nth(0, u))
                        pe.wait_ge(S["m_b_tok"], nth(0, u))
                    if c >= 2:
                        pe.wait_ge(S["m_diff"], nth(c - 2, u))
                    for h in range(NHM):
                        k = NHM * c + h
                        mm = nc.tensor.matmul(PS[u][:, 2 + c % 2, cols(h)], part_rows[:, k:k + 1].to_broadcast([PARTS, P]),
                                              m_parts[u][:], start=True, stop=True)
                    mm.then_inc(S["m_rows"], 1)
            for u in range(U):
                pe.wait_ge(S["m_xdd"], nth(0, u))
                for c in range(T - 1):
                    mm = nc.tensor.matmul(PS[u][0:DST, 2 + c // 2, 256 * (c % 2):256 * (c % 2 + 1)],
                                          work[u][:, 12, DST * c:DST * (c + 1)],
                                          slot(u, 6, 2)[:, 256 * c:256 * (c + 1)], start=True, stop=True)
                mm.then_inc(S["m_states"], 1)
            for u in range(U):
                pe.wait_ge(S["m_decays"], nth(0, u))
                for c in range(T):
                    for h in range(NHM):
                        k = NHM * c + h
                        mm = nc.tensor.matmul(PS[u][:, c // 2, 256 * (c % 2) + HDM * h:256 * (c % 2) + HDM * (h + 1)],
                                              slot(u, 0, 4)[:, P * k:P * (k + 1)],
                                              slot(u, 13, 2)[:, HDM * k:HDM * (k + 1)], start=True, stop=True)
                mm.then_inc(S["m_y_in"], 1)
                pe.wait_ge(S["m_scanned"], nth(0, u))
                for c in range(T):
                    mm = nc.tensor.matmul(PS[u][:, 2 + c // 2, 256 * (c % 2):256 * (c % 2 + 1)],
                                          work[u][0:DST, 9, cols(c)], state(u, c), start=True, stop=True)
                mm.then_inc(S["m_y_off"], 1)
            for u in range(U):
                pe.wait_ge(S["m_y"], nth(0, u))
                for t in range(T):
                    mm = nc.tensor.matmul(PS[u][:, t // 2, 256 * (t % 2):256 * (t % 2 + 1)], xT[u][:, cols(t)],
                                          m_in[:, 0:256], start=True, stop=True)
                mm.then_inc(S["m_z"], 1)
            for u in range(U):
                pe.wait_ge(S["m_gated"], nth(0, u))
                for i in range(2):
                    for t in range(T):
                        mm = nc.tensor.transpose(PS[u][:, 2 + i, cols(t)], slot(u, 6, 2)[:, 256 * t + P * i:256 * t + P * (i + 1)],
                                                 ident[:])
                mm.then_inc(S["m_y_turned"], 1)
            for u in range(U):
                pe.wait_ge(S["m_y_chan"], nth(0, u))
                for t in range(T):
                    for i in range(2):
                        mm = nc.tensor.matmul(PS[u][:, 0, cols(t)], work[u][:, i, cols(t)], m_wol[:, i, :],
                                              start=(i == 0), stop=(i == 1))
                mm.then_inc(S["m_out"], 1)

        def mamba_scalar(act):
            turn_scalar(act, 1, lambda u: xT[u][:])
            for u in range(U):
                act.wait_ge(S["m_dt_abs"], nth(0, u))
                nc.scalar.activation(sm[u][:, 3, :], sm[u][:, 2, :], ACT.Exp).then_inc(S["m_dt_exp"], 1)
                act.wait_ge(S["m_dt_exp"], nth(0, u))
                nc.scalar.activation(sm[u][:, 4, :], sm[u][:, 3, :], ACT.Ln, bias=1.0).then_inc(S["m_dt_ln"], 1)
                act.wait_ge(S["m_projected"], nth(0, u))
                nc.scalar.activation(work[u][:, 2, :], PS[u][:, 2, :], ACT.Identity, bias=m_convb[:, 2:3], scale=m_taps[:, 2, 3:4])
                for k in range(3):
                    ins = nc.scalar.activation(work[u][:, 8 + k, :], PS[u][:, 2, :], ACT.Copy, scale=m_taps[:, 2, k:k + 1])
                ins.then_inc(S["m_products_bc"], 1)
            for u in range(U):
                act.wait_ge(S["m_conv_bc"], nth(0, u))
                nc.scalar.activation(work[u][:, 5, :], work[u][:, 2, :], ACT.Tanh).then_inc(S["m_tanh_bc"], 1)
                act.wait_ge(S["m_conv"], nth(0, u))
                nc.scalar.activation(work[u][:, 3:5, :], work[u][:, 0:2, :], ACT.Tanh).then_inc(S["m_tanh"], 1)
            for u in range(U):
                act.wait_ge(S["m_turned"], nth(0, u))
                nc.scalar.activation(work[u][:, 10:12, :], PS[u][:, 0:2, :], ACT.Copy).then_inc(S["m_x_tok"], 1)
                nc.scalar.activation(work[u][:, 12, 0:256], PS[u][:, 2, 0:256], ACT.Copy).then_inc(S["m_b_tok"], 1)
            for u in range(U):
                act.wait_ge(S["m_ends"], nth(0, u))
                nc.scalar.activation(sm[u][:, 5:8, :], sm[u][:, 5:8, :], ACT.Exp).then_inc(S["m_ends_exp"], 1)
            for u in range(U):
                act.wait_ge(S["m_clamped"], nth(0, u))
                nc.scalar.activation(work[u][:, 0:4, :], work[u][:, 0:4, :], ACT.Exp).then_inc(S["m_exp"], 1)
                act.wait_ge(S["m_states"], nth(0, u))
                nc.scalar.activation(state(u, 1), PS[u][0:DST, 2, 0:256], ACT.Copy)
                nc.scalar.activation(work[u][0:DST, 8, :], PS[u][0:DST, 2:4, :].rearrange("n b f -> n (b f)")[:, 256:768],
                                     ACT.Copy).then_inc(S["m_added"], 1)
            for u in range(U):
                act.wait_ge(S["m_z"], nth(0, u))
                nc.scalar.activation(work[u][:, 13:15, :], PS[u][:, 0:2, :], ACT.Tanh, scale=0.5).then_inc(S["m_z_tanh"], 1)
            for u in range(U):
                act.wait_ge(S["m_gated"], nth(0, u))
                for t in range(T):
                    y_t = slot(u, 6, 2)[:, 256 * t:256 * (t + 1)]
                    ins = nc.scalar.activation(slot(u, 10, 2)[:, 256 * t:256 * (t + 1)], y_t, ACT.Square,
                                               accum_out=sm[u][:, 0, t:t + 1])
                ins.then_inc(S["m_square"], 1)
                act.wait_ge(S["m_y_turned"], nth(0, u))
                nc.scalar.activation(work[u][:, 0:2, :], PS[u][:, 2:4, :], ACT.Copy).then_inc(S["m_y_chan"], 1)

        def conv(ch, u, channels, done):
            for i in channels:
                m = ch.mark(nc.vector.tensor_scalar(work[u][:, i, :], PS[u][:, i, :], m_taps[:, i, 3:4], m_convb[:, i:i + 1],
                                                 ALU.mult, ALU.add))
            for k in (2, 1, 0):
                ch.wait(m)
                for i in channels:
                    s = 3 - k
                    ins = nc.vector.scalar_tensor_tensor(
                        out=work[u][:, i, s:N], in0=PS[u][:, i, 0:N - s], scalar=m_taps[:, i, k:k + 1],
                        in1=work[u][:, i, s:N], op0=ALU.mult, op1=ALU.add)
                    if k > 0 or i != channels[-1]:
                        m = ch.mark(ins)
            ins.then_inc(done, 1)

        def mamba_vector(dve, ch, ready):
            norm_vector(dve, ch, 1, x, xh, ready)
            for u in range(U):
                dve.wait_ge(S["m_projected"], nth(0, u))
                ch.link(nc.vector.tensor_tensor(sm[u][:, 0, :].rearrange("p (c h) -> p c h", c=T),
                                                PS[u][:, 3, 0:16].rearrange("p (c h) -> p c h", c=T),
                                                m_dtb[:].unsqueeze(1).to_broadcast([P, T, NHM]), ALU.add))
                nc.vector.scalar_tensor_tensor(out=sm[u][:, 2, :], in0=sm[u][:, 0, :], scalar=-1.0, in1=sm[u][:, 0, :],
                                               op0=ALU.mult, op1=ALU.min).then_inc(S["m_dt_abs"], 1)
                conv(ch, u, (0, 1), S["m_conv"])
            for u in range(U):
                dve.wait_ge(S["m_dt_ln"], nth(0, u))
                ch.link(nc.vector.scalar_tensor_tensor(out=sm[u][:, 0, :], in0=sm[u][:, 0, :], scalar=0.0,
                                                       in1=sm[u][:, 4, :], op0=ALU.max, op1=ALU.add))
                nc.vector.tensor_tensor(sm[u][:, 1, :].rearrange("p (c h) -> p c h", c=T),
                                        sm[u][:, 0, :].rearrange("p (c h) -> p c h", c=T),
                                        m_a[:].unsqueeze(1).to_broadcast([P, T, NHM]), ALU.mult).then_inc(S["m_da"], 1)
                dve.wait_ge(S["m_tanh"], nth(0, u))
                nc.vector.scalar_tensor_tensor(out=work[u][:, 6:8, :], in0=work[u][:, 3:5, :], scalar=1.0,
                                               in1=work[u][:, 0:2, :], op0=ALU.add, op1=ALU.mult).then_inc(S["m_silu"], 1)
                dve.wait_ge(S["m_tanh_bc"], nth(0, u))
                nc.vector.scalar_tensor_tensor(out=work[u][0:64, 8, :], in0=work[u][0:64, 5, :], scalar=1.0,
                                               in1=work[u][0:64, 2, :], op0=ALU.add, op1=ALU.mult)
                nc.vector.scalar_tensor_tensor(out=work[u][0:64, 9, :], in0=work[u][64:P, 5, :], scalar=1.0,
                                               in1=work[u][64:P, 2, :], op0=ALU.add, op1=ALU.mult).then_inc(S["m_silu_bc"], 1)
            for u in range(U):
                dve.wait_ge(S["m_turned"], nth(0, u))
                nc.vector.tensor_copy(sm[u][:, 2, :], PS[u][:, 3, 0:16]).then_inc(S["m_cum"], 1)
                dve.wait_ge(S["m_x_tok"], nth(0, u))
                m = ch.mark(nc.vector.tensor_tensor(heads(slot(u, 13, 2)), heads(slot(u, 10, 2)),
                                                    sm[u][:, 0, :].unsqueeze(2).to_broadcast([P, 16, HDM]), ALU.mult))
            left = [work[u][0:16, 5, 0:P] for u in range(U)]
            middle = [work[u][0:16, 5, P:P + P // 2].bitcast(BF16) for u in range(U)]
            for u in range(U):
                dve.wait_ge(S["m_cum_turned"], nth(0, u))
                m = ch.mark(nc.vector.tensor_copy(m_parts[u][0:16, :], PS[u][0:16, 1, 0:P]))
            ch.wait(m)
            for u in range(U):
                m = ch.mark(nc.vector.tensor_tensor(left[u], PS[u][0:16, 1, 0:P], m_parts[u][0:16, :], ALU.subtract))
            ch.wait(m)
            for u in range(U):
                m = ch.mark(nc.vector.tensor_copy(middle[u], left[u]))
            ch.wait(m)
            for u in range(U):
                nc.vector.tensor_copy(m_parts[u][32:48, :], middle[u])
                m = ch.mark(nc.vector.tensor_tensor(left[u], left[u], middle[u], ALU.subtract))
            ch.wait(m)
            for u in range(U):
                nc.vector.tensor_copy(m_parts[u][64:80, :], left[u]).then_inc(S["m_cum_parts"], 1)
            for u in range(U):
                dve.wait_ge(S["m_cb"], nth(0, u))
                nc.vector.tensor_tensor(tok(work[u][:, 4, :]), PS[u][:, 0, :].rearrange("p (c l) -> p c l", c=T),
                                        upper[:].unsqueeze(1).to_broadcast([P, T, P]), ALU.mult).then_inc(S["m_cb_masked"], 1)
            for c in range(T):
                for u in range(U):
                    dve.wait_ge(S["m_rows"], nth(c, u))
                    rows_ps = PS[u][:, 2 + c % 2, :].rearrange("p (h l) -> p h l", h=NHM)
                    if c == 0:
                        dve.wait_ge(S["m_cum"], nth(0, u))
                    m = ch.mark(nc.vector.tensor_copy(sm[u][:, 7, NHM * c:NHM * (c + 1)], rows_ps[:, :, P - 1]))
                    nc.vector.tensor_tensor(work[u][:, c, :].rearrange("p (h l) -> p h l", h=NHM), rows_ps,
                                            sm[u][:, 2, NHM * c:NHM * (c + 1)].unsqueeze(2).to_broadcast([P, NHM, P]),
                                            ALU.subtract).then_inc(S["m_diff"], 1)
            for u in range(U):
                dve.wait_ge(S["m_diff"], nth(T - 1, u))
                nc.vector.tensor_copy(sm[u][:, 6, :], sm[u][:, 2, :])
                ch.link(nc.vector.tensor_tensor(sm[u][:, 5, :], sm[u][:, 7, :], sm[u][:, 2, :], ALU.subtract))
                nc.vector.tensor_scalar(sm[u][:, 5, :], sm[u][:, 5, :], 0.0, None, ALU.min).then_inc(S["m_ends"], 1)
            for u in range(U):
                nc.vector.tensor_scalar(work[u][:, 0:4, :], work[u][:, 0:4, :], 0.0, None, ALU.min).then_inc(S["m_clamped"], 1)
                dve.wait_ge(S["m_ends_exp"], nth(0, u))
                nc.vector.tensor_tensor(heads(slot(u, 6, 2)), heads(slot(u, 13, 2)),
                                        sm[u][:, 5, :].unsqueeze(2).to_broadcast([P, 16, HDM]), ALU.mult)\
                    .then_inc(S["m_xdd"], 1)
            for u in range(U):
                dve.wait_ge(S["m_exp"], nth(0, u))
                dve.wait_ge(S["m_cb_masked"], nth(0, u))
                decays = slot(u, 0, 4).rearrange("p (c h l) -> p c h l", c=T, h=NHM)
                nc.vector.tensor_tensor(decays, decays, tok(work[u][:, 4, :]).unsqueeze(2).to_broadcast([P, T, NHM, P]),
                                        ALU.mult).then_inc(S["m_decays"], 1)
            for u in range(U):
                y = slot(u, 6, 2)
                dve.wait_ge(S["m_y_off"], nth(0, u))
                ch.link(nc.vector.tensor_tensor(heads(y), PS[u][:, 2:4, :].rearrange("p b (k w) -> p (b k) w", w=HDM),
                                                sm[u][:, 6, :].unsqueeze(2).to_broadcast([P, 16, HDM]), ALU.mult))
                ch.link(nc.vector.tensor_tensor(work[u][:, 6:8, :], work[u][:, 6:8, :], PS[u][:, 0:2, :], ALU.add))
                dve.wait_ge(S["m_skip"], nth(0, u))
                nc.vector.tensor_tensor(y, y, slot(u, 10, 2), ALU.add).then_inc(S["m_y"], 1)
            for u in range(U):
                dve.wait_ge(S["m_z_tanh"], nth(0, u))
                gate = work[u][:, 13:15, :]
                ch.link(nc.vector.scalar_tensor_tensor(out=gate, in0=gate, scalar=1.0, in1=PS[u][:, 0:2, :],
                                                       op0=ALU.add, op1=ALU.mult))
                nc.vector.scalar_tensor_tensor(out=work[u][:, 6:8, :], in0=work[u][:, 6:8, :], scalar=0.5, in1=gate,
                                               op0=ALU.mult, op1=ALU.mult).then_inc(S["m_gated"], 1)
            for u in range(U):
                dve.wait_ge(S["m_square"], nth(0, u))
                nc.vector.tensor_scalar(den[u][:], sm[u][:, 0, 0:T], 1.0 / 256, LN_EPS, ALU.mult, ALU.add)\
                    .then_inc(S["m_mean_sq"], 1)

            def update(u):
                dve.wait_ge(S["m_rstd"], nth(0, u))
                dve.wait_ge(S["m_out"], nth(0, u))
                for t in range(T):
                    ins = nc.vector.scalar_tensor_tensor(out=x[u][:, t, :], in0=PS[u][:, 0, cols(t)], scalar=den2[u][:, t:t + 1],
                                                         in1=x[u][:, t, :], op0=ALU.mult, op1=ALU.add)
                ins.then_inc(S["x"], 1)
            return update

        def mamba_gpsimd(pool, ch):
            rstd_gpsimd(pool, 1)
            for u in range(U):
                pool.wait_ge(S["m_products_bc"], nth(0, u))
                for k in range(3):
                    s = 3 - k
                    ins = nc.gpsimd.tensor_tensor(work[u][:, 2, s:N], work[u][:, 2, s:N], work[u][:, 8 + k, 0:N - s], ALU.add)
                    if k < 2:
                        ch.link(ins)
                ins.then_inc(S["m_conv_bc"], 1)
            for u in range(U):
                pool.wait_ge(S["normed"], nth(1, u))
                nc.gpsimd.tensor_tensor(x[u][:], x[u][:], m_blin[:].unsqueeze(1).to_broadcast([P, T, P]), ALU.add)
            for u in range(U):
                pool.wait_ge(S["m_xdd"], nth(0, u))
                v = slot(u, 10, 2).rearrange("p (c h w) -> p c h w", c=T, h=NHM)
                nc.gpsimd.tensor_tensor(v, v, m_d[:].unsqueeze(1).unsqueeze(3).to_broadcast([P, T, NHM, HDM]), ALU.mult)\
                    .then_inc(S["m_skip"], 1)
                pool.wait_ge(S["m_skip"], nth(0, u))
                m = ch.mark(nc.gpsimd.memset(state(u, 0), 0.0))
                carried = work[u][0:DST, 12, 0:256]
                ch.wait(m)
                pool.wait_ge(S["m_added"], nth(0, u))
                for c in (1, 2):
                    ch.link(nc.gpsimd.tensor_tensor(carried.rearrange("n (h w) -> n h w", h=NHM),
                                                    state(u, c).rearrange("n (h w) -> n h w", h=NHM),
                                                    sm[u][0:DST, 7, NHM * c:NHM * (c + 1)].unsqueeze(2).to_broadcast([DST, NHM, HDM]),
                                                    ALU.mult))
                    ins = nc.gpsimd.tensor_tensor(state(u, c + 1), state(u, c + 1), carried, ALU.add)
                    if c == 1:
                        ch.link(ins)
                ins.then_inc(S["m_scanned"], 1)
            for u in range(U):
                pool.wait_ge(S["m_mean_sq"], nth(0, u))
                nc.gpsimd.tensor_tensor(den2[u][:], den[u][:], minus_half[:], ALU.pow).then_inc(S["m_rstd"], 1)


        def gcn_tensor(pe):
            for u in range(U):
                pe.wait_ge(S["normed"], nth(2, u))
                pe.wait_ge(S[f"adjT_in{u}"], 16)
                for t in range(T):
                    mm = nc.tensor.matmul(PS[u][:, 0, :], xh[u][:, t, :], adjT[u][:, t, :], start=(t == 0), stop=(t == T - 1))
                mm.then_inc(S["gcn_sum"], 1)
            for u in range(U):
                pe.wait_ge(S["gcn_chan"], nth(0, u))
                for t in range(T):
                    nc.tensor.matmul(PS[u][:, 1, cols(t)], ones_h[0:PARTS, :], gcn_b, start=True, stop=False)
                    mm = nc.tensor.matmul(PS[u][:, 1, cols(t)], work[u][:, 0, cols(t)], gcn_w[:], start=False, stop=True)
                mm.then_inc(S["gcn_out"], 1)

        def gcn_scalar(act):
            for u in range(U):
                act.wait_ge(S["gcn_sum"], nth(0, u))
                nc.scalar.activation(work[u][:, 0, :], PS[u][:, 0, :], ACT.Copy).then_inc(S["gcn_chan"], 1)

        def gcn_vector(dve, ch, ready):
            norm_vector(dve, ch, 2, x, xh, ready)

            def update(u):
                dve.wait_ge(S["gcn_out"], nth(0, u))
                nc.vector.tensor_tensor(x[u][:], x[u][:], tok(PS[u][:, 1, :]), ALU.add).then_inc(S["x"], 1)
            return update

        def gcn_gpsimd(pool, ch):
            rstd_gpsimd(pool, 2)

        G1 = E1 // 4

        def not_chosen(u):
            return work[u][0:E1, 9, 0:N // 2].bitcast(BF16)

        def top1_tensor(pe):

            def products(u):
                pe.wait_ge(S["chan"], nth(2, u))
                for t in range(T):
                    mm = nc.tensor.matmul(PS[u][:, 1, E1 * t:E1 * (t + 1)], xT[u][:, cols(t)], e1_router[:], start=True, stop=True)
                mm.then_inc(S["e1_logits"], 1)

            turn_tensor(pe, 2, lambda u: xh[u], lambda u: pe.wait_ge(S["normed"], nth(3, u)), products)
            for g in range(2):
                for u in range(U):
                    nc.tensor.matmul(PS[u][:, 3 * g, :], e1_w1[:, g, :], xT[u][:], start=True, stop=False)
            for u in range(U):
                pe.wait_ge(S["e1_hot"], nth(0, u))
                for t in range(T):
                    mm = nc.tensor.transpose(PS[u][0:E1, 2, cols(t)], oh[u][:, t, :], ident[:])
                mm.then_inc(S["e1_hot_turned"], 1)
            for g in range(G1):
                for u in range(U):
                    if g == 0:
                        pe.wait_ge(S["e1_not_chosen"], nth(0, u))
                    else:
                        if g >= 2:
                            pe.wait_ge(S["e1_hidden"], nth(g - 2, u))
                    b = 3 * (g % 2)
                    if g >= 2:
                        nc.tensor.matmul(PS[u][:, b, :], e1_w1[:, g, :], xT[u][:], start=True, stop=False)
                    nc.tensor.matmul(PS[u][:, b, :], pick[:, g, :], not_chosen(u), start=False, stop=True)\
                        .then_inc(S["e1_up"], 1)
            for u in range(U):
                pe.wait_ge(S["e1_hidden"], nth(G1 - 1, u))
                for t in range(T):
                    nc.tensor.matmul(PS[u][:, 1, cols(t)], work[u][0:E1, 8, cols(t)], e1_b2[:], start=True, stop=False)
                    for g in range(G1):
                        mm = nc.tensor.matmul(PS[u][:, 1, cols(t)], work[u][:, g, cols(t)], e1_w2[:, g, :],
                                              start=False, stop=(g == G1 - 1))
                mm.then_inc(S["e1_out"], 1)

        def top1_scalar(act):
            turn_scalar(act, 2, lambda u: xT[u][:])
            for g in range(G1):
                for u in range(U):
                    act.wait_ge(S["e1_up"], nth(g, u))
                    nc.scalar.activation(work[u][:, g, :], PS[u][:, 3 * (g % 2), :], ACT.Relu, bias=e1_b1[:, g:g + 1])\
                        .then_inc(S["e1_hidden"], 1)

        def top1_vector(dve, ch, ready):
            norm_vector(dve, ch, 3, x, xh, ready)
            for u in range(U):
                dve.wait_ge(S["e1_logits"], nth(0, u))
                ch.link(nc.vector.tensor_tensor(lg[u][:], PS[u][:, 1, 0:T * E1].rearrange("p (t e) -> p t e", t=T),
                                                e1_rb[:].unsqueeze(1).to_broadcast([P, T, E1]), ALU.add))
                top_index(dve, ch, u, E1)
                one_hot(oh[u], u, 0, E1).then_inc(S["e1_hot"], 1)
            for u in range(U):
                dve.wait_ge(S["e1_hot_turned"], nth(0, u))
                nc.vector.tensor_copy(work[u][0:E1, 8, :], PS[u][0:E1, 2, :])
                nc.vector.tensor_scalar(not_chosen(u), PS[u][0:E1, 2, :], 1.0, None, ALU.subtract)\
                    .then_inc(S["e1_not_chosen"], 1)

            def update(u):
                dve.wait_ge(S["e1_out"], nth(0, u))
                nc.vector.scalar_tensor_tensor(out=x[u][:], in0=tok(PS[u][:, 1, :]), scalar=0.0, in1=x[u][:],
                                               op0=ALU.max, op1=ALU.add).then_inc(S["x"], 1)
            return update

        def top1_gpsimd(pool, ch):
            rstd_gpsimd(pool, 3)

        SE = 96

        PADDED = N + 2 * PAD

        def gru_tensor(pe):

            def products(u):
                pe.wait_ge(S["chan"], nth(3, u))
                nc.tensor.matmul(PS[u][:, 1, :], g_c1[:], xT[u][:], start=True, stop=True).then_inc(S["g_conv1"], 1)
                nc.tensor.matmul(PS[u][0:SE, 2, :], g_se[:], xT[u][:], start=True, stop=True).then_inc(S["g_struct"], 1)
                for t in range(T):
                    nc.tensor.matmul(PS[u][:, 3, cols(t)], ones_h[0:PARTS, :], g_msgb, start=True, stop=False)
                    mm = nc.tensor.matmul(PS[u][:, 3, cols(t)], xT[u][:, cols(t)], g_msg[:], start=False, stop=True)
                mm.then_inc(S["g_msg"], 1)

            turn_tensor(pe, 3, lambda u: xh[u], lambda u: pe.wait_ge(S["normed"], nth(4, u)), products)
            for u in range(U):
                for i, (w, part) in enumerate(((g_c2_high, g_high[u]), (g_c2_low, g_high[u]), (g_c2_high, g_low[u]))):
                    pe.wait_ge(S["g_high"], nth(0, u))
                    if i == 2:
                        pe.wait_ge(S["g_low"], nth(0, u))
                    for k in range(TAPS):
                        mm = nc.tensor.matmul(PS[u][:, 0, :], w[:, k, :], part[:, k:k + N],
                                              start=(i == 0 and k == 0), stop=(i == 2 and k == TAPS - 1))
                mm.then_inc(S["g_conv2"], 1)
            for t in range(T):
                for u in range(U):
                    if t == 0:
                        pe.wait_ge(S["g_factors"], nth(0, u))
                    if t >= 2:
                        pe.wait_ge(S["g_near"], nth(t - 2, u))
                    nc.tensor.matmul(PS[u][:, 1 + t % 2, :], work[u][0:SE, 2, cols(t)], work[u][0:SE, 3, :],
                                     start=True, stop=True).then_inc(S["g_dist"], 1)
            for u in range(U):
                pe.wait_ge(S["g_affinity"], nth(T - 1, u))
                pe.wait_ge(S["g_msg_tok"], nth(0, u))
                for t in range(T):
                    mm = nc.tensor.matmul(PS[u][:, 3, :], work[u][:, 4, cols(t)], work[u][:, 6 + t, :],
                                          start=(t == 0), stop=(t == T - 1))
                mm.then_inc(S["g_received"], 1)
            for u in range(U):
                pe.wait_ge(S["g_conv_out"], nth(0, u))
                pe.wait_ge(S["g_received_sb"], nth(0, u))
                for g in range(3):
                    w = slice(P * g, P * (g + 1))
                    nc.tensor.matmul(PS[u][:, g, :], g_ih[:, 0, w], work[u][:, 5, :], start=True, stop=False)
                    nc.tensor.matmul(PS[u][:, g, :], g_ih[:, 1, w], work[u][:, 10, :], start=False, stop=(g == 2))
                    mm = nc.tensor.matmul(PS[u][:, g if g < 2 else 3, :], g_hh[:, w], xT[u][:], start=(g == 2), stop=True)
                mm.then_inc(S["g_gates"], 1)
            for u in range(U):
                pe.wait_ge(S["g_new"], nth(0, u))
                for t in range(T):
                    mm = nc.tensor.transpose(PS[u][:, 0, cols(t)], work[u][:, 1, cols(t)], ident[:])
                mm.then_inc(S["g_new_tok"], 1)

        def gru_scalar(act):
            turn_scalar(act, 3, lambda u: xT[u][:])
            for u in range(U):
                act.wait_ge(S["g_conv1"], nth(0, u))
                nc.scalar.activation(slot(u, 0, 2)[:, PAD:PAD + N], PS[u][:, 1, :], ACT.Relu, bias=g_c[:, 0:1],
                                     scale=g_s[:, 0:1]).then_inc(S["g_hidden"], 1)
                act.wait_ge(S["g_padded"], nth(0, u))
                act.wait_ge(S["g_hidden"], nth(0, u))
                nc.scalar.activation(g_high[u][:], slot(u, 0, 2)[:, 0:PADDED], ACT.Copy).then_inc(S["g_high"], 1)
                act.wait_ge(S["g_struct"], nth(0, u))
                nc.scalar.activation(work[u][0:32, 2, :], PS[u][0:32, 2, :], ACT.Identity, bias=g_seb[0:32, :])
                nc.scalar.activation(work[u][32:64, 2, :], PS[u][32:64, 2, :], ACT.Square, bias=g_seb[32:64, :])
                nc.scalar.activation(work[u][0:32, 3, :], PS[u][0:32, 2, :], ACT.Identity, bias=g_seb2[:], scale=2.0)
                nc.scalar.activation(work[u][64:SE, 3, :], PS[u][64:SE, 2, :], ACT.Square, bias=g_seb[64:SE, :])\
                    .then_inc(S["g_factors"], 1)
            for u in range(U):
                act.wait_ge(S["g_msg"], nth(0, u))
                nc.scalar.activation(work[u][:, 4, :], PS[u][:, 3, :], ACT.Relu).then_inc(S["g_msg_tok"], 1)
            for t in range(T):
                for u in range(U):
                    act.wait_ge(S["g_dist"], nth(t, u))
                    nc.scalar.activation(work[u][:, 6 + t, :], PS[u][:, 1 + t % 2, :], ACT.Exp).then_inc(S["g_near"], 1)
            for u in range(U):
                act.wait_ge(S["g_conv_sum"], nth(0, u))
                nc.scalar.activation(work[u][:, 5, :], work[u][:, 5, :], ACT.Relu, bias=g_c[:, 1:2]).then_inc(S["g_conv_out"], 1)
                act.wait_ge(S["g_received"], nth(0, u))
                nc.scalar.activation(work[u][:, 10, :], PS[u][:, 3, :], ACT.Copy).then_inc(S["g_received_sb"], 1)
            for u in range(U):
                act.wait_ge(S["g_gates"], nth(0, u))
                nc.scalar.activation(work[u][:, 13, :], PS[u][:, 3, :], ACT.Identity, bias=g_half[:, 2:3], scale=0.5)
                nc.scalar.activation(work[u][:, 11, :], PS[u][:, 0, :], ACT.Tanh, bias=g_half[:, 0:1], scale=0.5)\
                    .then_inc(S["g_r"], 1)
                nc.scalar.activation(work[u][:, 12, :], PS[u][:, 1, :], ACT.Tanh, bias=g_half[:, 1:2], scale=0.5)\
                    .then_inc(S["g_z"], 1)
            for u in range(U):
                act.wait_ge(S["g_n_sum"], nth(0, u))
                nc.scalar.activation(work[u][:, 14, :], work[u][:, 13, :], ACT.Tanh, bias=g_bi[:, 2:3]).then_inc(S["g_n"], 1)

        def gru_vector(dve, ch, ready):
            norm_vector(dve, ch, 4, x, xh, ready)
            for u in range(U):
                dve.wait_ge(S["g_high"], nth(0, u))
                nc.vector.tensor_tensor(g_low[u][:], slot(u, 0, 2)[:, 0:PADDED], g_high[u][:].bitcast(F32), ALU.subtract)\
                    .then_inc(S["g_low"], 1)
            for t in range(T):
                for u in range(U):
                    dve.wait_ge(S["g_near"], nth(t, u))
                    nc.vector.tensor_tensor(work[u][:, 6 + t, :], work[u][:, 6 + t, :], adjT[u][:, t, :], ALU.mult)\
                        .then_inc(S["g_affinity"], 1)
            for u in range(U):
                dve.wait_ge(S["g_conv2"], nth(0, u))
                nc.vector.scalar_tensor_tensor(out=work[u][:, 5, :], in0=PS[u][:, 0, :], scalar=g_s[:, 1:2], in1=xT[u][:],
                                               op0=ALU.mult, op1=ALU.add).then_inc(S["g_conv_sum"], 1)
            for u in range(U):
                h_n = work[u][:, 13, :]
                dve.wait_ge(S["g_r"], nth(0, u))
                ch.link(nc.vector.scalar_tensor_tensor(out=h_n, in0=work[u][:, 11, :], scalar=1.0, in1=h_n,
                                                       op0=ALU.add, op1=ALU.mult))
                nc.vector.tensor_tensor(h_n, h_n, PS[u][:, 2, :], ALU.add).then_inc(S["g_n_sum"], 1)
            for u in range(U):
                diff = work[u][:, 0, :]
                dve.wait_ge(S["g_n"], nth(0, u))
                ch.link(nc.vector.tensor_tensor(diff, xT[u][:], work[u][:, 14, :], ALU.subtract))
                dve.wait_ge(S["g_z"], nth(0, u))
                ch.link(nc.vector.scalar_tensor_tensor(out=diff, in0=work[u][:, 12, :], scalar=1.0, in1=diff,
                                                       op0=ALU.add, op1=ALU.mult))
                nc.vector.scalar_tensor_tensor(out=work[u][:, 1, :], in0=diff, scalar=0.5, in1=work[u][:, 14, :],
                                               op0=ALU.mult, op1=ALU.add).then_inc(S["g_new"], 1)

            def update(u):
                dve.wait_ge(S["g_new_tok"], nth(0, u))
                nc.vector.tensor_tensor(x[u][:], x[u][:], tok(PS[u][:, 0, :]), ALU.add).then_inc(S["x"], 1)
            return update

        def gru_gpsimd(pool, ch):
            rstd_gpsimd(pool, 4)
            for u in range(U):
                pool.wait_ge(S["normed"], nth(4, u))
                nc.gpsimd.memset(slot(u, 0, 2)[:, 0:PAD], 0.0)
                ch.link(nc.gpsimd.memset(slot(u, 0, 2)[:, PAD + N:PAD + N + PAD], 0.0))
                ch.link(nc.gpsimd.memset(work[u][64:SE, 2, :], -1.0))
                nc.gpsimd.memset(work[u][32:64, 3, :], -1.0).then_inc(S["g_padded"], 1)
                pool.wait_ge(S["g_padded"], nth(0, u))

        def route_tensor(pe, n):
            for u in range(U):
                pe.wait_ge(S["route_chosen"], nth(0, u))
                for t in range(T):
                    for s in range(t):
                        nc.tensor.matmul(PS[u][:, 1, n * t:n * (t + 1)], ones_h[:], chosen[u][:, s, 0:n],
                                         start=(s == 0), stop=False)
                    nc.tensor.matmul(PS[u][:, 1, n * t:n * (t + 1)], strict[:], chosen[u][:, t, 0:n],
                                     start=(t == 0), stop=True)
                for t in range(T):
                    mm = nc.tensor.matmul(PS[u][:, 2, 0:n], ones_h[:], chosen[u][:, t, 0:n], start=(t == 0), stop=(t == T - 1))
                mm.then_inc(S["route_ranks"], 1)

        def route_scalar(act, n):
            for u in range(U):
                act.wait_ge(S["route_diff"], nth(0, u))
                nc.scalar.activation(wts[u][:], wts[u][:], ACT.Exp).then_inc(S["route_exp"], 1)

        def route_vector(dve, ch, turn, n, logits, extra):
            for u in range(U):
                logits(u)
                top_index(dve, ch, u, n)
                if n < E3:
                    nc.vector.memset(wts[u][:, :, n:E3], 0.0)
                nc.vector.tensor_tensor(wts[u][:, :, 0:n], lg[u][:, :, 0:n], top[u][:, :, 0:1].to_broadcast([P, T, n]),
                                        ALU.subtract)
                nc.vector.tensor_tensor(wts[u][:, :, E3:E3 + 2], top[u][:, :, 0:2], top[u][:, :, 0:1].to_broadcast([P, T, 2]),
                                        ALU.subtract).then_inc(S["route_diff"], 1)
                one_hot(oh[u], u, 0, n)
                ch.link(one_hot(oh2[u], u, 1, n))
                nc.vector.tensor_tensor(chosen[u][:, :, 0:n], oh[u][:, :, 0:n], oh2[u][:, :, 0:n], ALU.add)\
                    .then_inc(S["route_chosen"], 1)
            for u in range(U):
                dve.wait_ge(S["route_exp"], nth(0, u))
                if extra:
                    nc.vector.tensor_reduce(den2[u][:], wts[u][:, :, 0:n], AX.X, ALU.add)
                ch.link(nc.vector.tensor_reduce(den[u][:], wts[u][:, :, E3:E3 + 2], AX.X, ALU.add))
                if extra:
                    ch.link(nc.vector.scalar_tensor_tensor(out=den[u][:], in0=den2[u][:], scalar=extra, in1=den[u][:],
                                                           op0=ALU.mult, op1=ALU.add))
                ch.link(nc.vector.reciprocal(den[u][:], den[u][:]))
                nc.vector.tensor_tensor(weight_of[:, bass.ds(turn * U * T + u * T, T), :], wts[u][:, :, E3:E3 + 2],
                                        den[u][:].unsqueeze(2).to_broadcast([P, T, 2]), ALU.mult)
            for u in range(U):
                dve.wait_ge(S["route_ranks"], nth(0, u))
                if u:
                    dve.wait_ge(S["route_placed"], u)
                row = lg[u][:, :, 0:n]
                ch.link(nc.vector.tensor_tensor(row, PS[u][:, 1, 0:T * n].rearrange("p (t e) -> p t e", t=T),
                                                    place[:, 0:n].unsqueeze(1).to_broadcast([P, T, n]), ALU.add))
                nc.vector.tensor_tensor(place[:, 0:n], place[:, 0:n], PS[u][:, 2, 0:n], ALU.add).then_inc(S["route_placed"], 1)
                nc.vector.tensor_tensor(oh[u][:, :, 0:n], oh[u][:, :, 0:n], row, ALU.mult)
                ch.link(nc.vector.tensor_tensor(oh2[u][:, :, 0:n], oh2[u][:, :, 0:n], row, ALU.mult))
                nc.vector.tensor_reduce(idxf[u][:, :, 0], oh[u][:, :, 0:n], AX.X, ALU.add)
                ch.link(nc.vector.tensor_reduce(idxf[u][:, :, 1], oh2[u][:, :, 0:n], AX.X, ALU.add))
                nc.vector.tensor_copy(sent_to[u][:], idxf[u][:])
                nc.vector.tensor_copy(row_of[:, bass.ds(turn * U * T + u * T, T), :], idxf[u][:])

        def scatter_gpsimd(pool, graphs=range(U)):
            for u in graphs:
                for t in range(T):
                    for k in range(2):
                        nc.gpsimd.indirect_dma_start(
                            out=moe_in, out_offset=bass.IndirectOffsetOnAxis(ap=sent_to[u][:, t, k:k + 1], axis=0),
                            in_=sent[u][:, t, :], in_offset=None).then_inc(S["scattered"], 16)

        def rows_in_set(s, u):
            return (rows, sent_to)[s][u]

        def weights_in_set(s, u):
            return (idxf[u], lg[u])[s][:, :, 0:2]

        def recall_rows(dve, turn, sets=1):
            for g in range(sets * U):
                nc.vector.tensor_copy(rows_in_set(g // U, g % U)[:], row_of[:, bass.ds(turn * sets * U * T + g * T, T), :])\
                    .then_inc(S["rows"], 1)

        def recall_weights(dve, turn, sets=1):
            for g in range(sets * U):
                nc.vector.tensor_copy(weights_in_set(g // U, g % U), weight_of[:, bass.ds(turn * sets * U * T + g * T, T), :])\
                    .then_inc(S["recalled"], 1)

        def gather_gpsimd(pool, n, u, s=0):
            pool.wait_ge(S["rows"], nth(s, u))
            for t in range(T):
                for k in range(2):
                    nc.gpsimd.indirect_dma_start(
                        out=work[u][:, 9 + 2 * s + k, cols(t)], out_offset=None, in_=moe_out[0:P * TILES(n)],
                        in_offset=bass.IndirectOffsetOnAxis(ap=rows_in_set(s, u)[:, t, k:k + 1], axis=0)).then_inc(S[f"gathered{u}"], 16)

        def first_gather(n, sets=1):
            with nc.Block() as block:
                @block.vector
                def _(dve):
                    recall_rows(dve, 0, sets)

                @block.gpsimd
                def _(pool):
                    for g in range(sets * U):
                        gather_gpsimd(pool, n, g % U, g // U)
                    for u in range(U):
                        pool.wait_ge(S[f"gathered{u}"], 16 * 2 * T * sets)
            clear()

        def combine_vector(dve, ch, u, acc, sem, s=0):
            dve.wait_ge(S["recalled"], nth(s, u))
            for k in range(2):
                for t in range(T):
                    ins = nc.vector.scalar_tensor_tensor(out=acc[:, t, :], in0=work[u][:, 9 + 2 * s + k, cols(t)],
                                                         scalar=weights_in_set(s, u)[:, t, k:k + 1], in1=acc[:, t, :],
                                                         op0=ALU.mult, op1=ALU.add)
                    if k == 0:
                        m = ch.mark(ins)
                if k == 0:
                    ch.wait(m)
            ins.then_inc(sem, 1)

        def rms_scalar(act, k, src_ready):
            for u in range(U):
                src_ready(u)
                for t in range(T):
                    ins = nc.scalar.activation(work[u][:, 3, cols(t)], xh[u][:, t, :], ACT.Square,
                                               accum_out=sm[u][:, 0, t:t + 1])
                ins.then_inc(S["a_squares"], 1)

        def rms_vector(dve, k, dst):
            for u in range(U):
                dve.wait_ge(S["a_squares"], nth(k, u))
                nc.vector.tensor_scalar(den[u][:], sm[u][:, 0, 0:T], 1.0 / P, RMS_EPS, ALU.mult, ALU.add)\
                    .then_inc(S["a_mean_sq"], 1)
            for u in range(U):
                dve.wait_ge(S["a_rms"], nth(k, u))
                nc.vector.tensor_tensor(dst(u), xh[u][:], den2[u][:].unsqueeze(2).to_broadcast([P, T, P]),
                                        ALU.mult).then_inc(S["a_normed"], 1)

        def rms_gpsimd(pool, k):
            for u in range(U):
                pool.wait_ge(S["a_mean_sq"], nth(k, u))
                nc.gpsimd.tensor_tensor(den2[u][:], den[u][:], minus_half[:], ALU.pow).then_inc(S["a_rms"], 1)

        LANES = [(g, u) for g in range(NHA // 2) for u in range(U)]

        def by_lane(t, g, u):
            return len(LANES) * t + U * g + u + 1

        def turned_ps(u, g, t):
            return PS[u][:, 2 * g:2 * g + 2, :].rearrange("p b (s n) -> p (b s) n", s=2)[:, 0:t + 1, :]

        def turned_heads(u, g, t):
            return work[u][:, 11:12 + t, 256 * g:256 * (g + 1)]

        def attn_tensor(pe):

            def products(u):
                pe.wait_ge(S["chan"], nth(4, u))
                for i in range(4):
                    mm = nc.tensor.matmul(PS[u][:, i, :], a_qk[:, i, :], work[u][:, 1, :], start=True, stop=True)
                    if i % 2:
                        mm.then_inc(S["a_qk"], 1)

            turn_tensor(pe, 4, lambda u: tok(work[u][:, 0, :]), lambda u: pe.wait_ge(S["a_normed"], nth(0, u)), products)
            for u in range(U):
                pe.wait_ge(S["a_parts"], 2 * u + 2)
                for t in range(T):
                    mm = nc.tensor.matmul(PS[u][:, 0, 64 * t:64 * (t + 1)], work[u][:, 1, cols(t)], a_v[:],
                                          start=True, stop=True)
                mm.then_inc(S["a_v_ps"], 1)
            for t in range(T):
                w = P * (t + 1)
                for g, u in LANES:
                    if t == 0:
                        pe.wait_ge(S["a_rotated"], 2 * u + 2)
                        pe.wait_ge(S["a_v"], nth(0, u))
                    else:
                        pe.wait_ge(S["a_y"], by_lane(t - 1, g, u))
                    for h in (2 * g, 2 * g + 1):
                        r = slice(HDA * h, HDA * (h + 1))
                        nc.tensor.matmul(PS[u][:, h, 0:w], work[u][r, 2, cols(t)], work[u][r, 4, 0:w], start=True, stop=False)
                        mm = nc.tensor.matmul(PS[u][:, h, w - P:w], ident_h[:], causal[:], start=False, stop=True)
                    mm.then_inc(S["a_scores"], 1)
                for g, u in LANES:
                    pe.wait_ge(S["a_p"], by_lane(t, g, u))
                    for s in range(t + 1):
                        for i in range(2):
                            mm = nc.tensor.transpose(PS[u][:, 2 * g + s // 2, cols(2 * (s % 2) + i)],
                                                     work[u][:, 7 + 2 * g + i, cols(s)], ident[:])
                    mm.then_inc(S["a_p_turned"], 1)
                for g, u in LANES:
                    if g == 0:
                        pe.wait_ge(S["a_pT_dve"], nth(t, u))
                    else:
                        pe.wait_ge(S["a_pT_act"], nth(t, u))
                    for i in range(2):
                        for s in range(t + 1):
                            kv = 64 * s + HDA * g
                            mm = nc.tensor.matmul(PS[u][:, 2 * g, HDA * i:HDA * (i + 1)], work[u][:, 11 + s, cols(2 * g + i)],
                                                  work[u][:, 6, kv:kv + HDA], start=(s == 0), stop=(s == t))
                    mm.then_inc(S["a_pv"], 1)

            def products(u):
                pe.wait_ge(S["chan"], nth(5, u))
                for t in range(T):
                    mm = nc.tensor.matmul(PS[u][:, 1, cols(t)], work[u][:, 1, cols(t)], a_o[:], start=True, stop=True)
                mm.then_inc(S["a_out"], 1)

            turn_tensor(pe, 5, lambda u: tok(work[u][:, 5, :]), lambda u: pe.wait_ge(S["a_y"], by_lane(T - 1, 1, u)), products)

            def products(u):
                pe.wait_ge(S["chan"], nth(6, u))
                for t in range(T):
                    mm = nc.tensor.matmul(PS[u][:, 1, E2 * t:E2 * (t + 1)], work[u][:, 1, cols(t)], e2_router[:],
                                          start=True, stop=True)
                mm.then_inc(S["e2_logits"], 1)

            turn_tensor(pe, 6, lambda u: sent[u][:], lambda u: pe.wait_ge(S["a_normed"], nth(1, u)), products)
            route_tensor(pe, E2)

        def attn_scalar(act):
            rms_scalar(act, 0, lambda u: act.wait_ge(S["normed"], nth(5, u)))
            turn_scalar(act, 4, lambda u: work[u][:, 1, :], a_ln1[:])
            for u in range(U):
                act.wait_ge(S["a_v_ps"], nth(0, u))
                nc.scalar.activation(work[u][:, 6, 0:256], PS[u][:, 0, 0:256], ACT.Copy).then_inc(S["a_v"], 1)
            for t in range(T):
                w = P * (t + 1)
                for g, u in LANES:
                    act.wait_ge(S["a_max"], by_lane(t, g, u))
                    for h in (2 * g, 2 * g + 1):
                        ins = nc.scalar.activation(work[u][:, 7 + h, 0:w], PS[u][:, h, 0:w], ACT.Exp, scale=HDA ** -0.5,
                                                   bias=sm[u][:, 1 + t, h:h + 1], accum_out=sm[u][:, 1 + t, 4 + h:5 + h])
                    ins.then_inc(S["a_p"], 1)
                for u in range(U):
                    act.wait_ge(S["a_p_turned"], by_lane(t, 1, u))
                    nc.scalar.activation(turned_heads(u, 1, t), turned_ps(u, 1, t), ACT.Copy).then_inc(S["a_pT_act"], 1)
            turn_scalar(act, 5, lambda u: work[u][:, 1, :])
            rms_scalar(act, 1, lambda u: act.wait_ge(S["a_x"], nth(0, u)))
            turn_scalar(act, 6, lambda u: work[u][:, 1, :], a_ln2[:])
            route_scalar(act, E2)

        def attn_vector(dve, ch, turn, ready):
            norm_vector(dve, ch, 5, x, xh, ready)
            rms_vector(dve, 0, lambda u: tok(work[u][:, 0, :]))
            for u in range(U):
                for half in range(2):
                    dve.wait_ge(S["a_qk"], 2 * u + half + 1)
                    for i in (2 * half, 2 * half + 1):
                        ins = nc.vector.tensor_tensor(work[u][:, 2 + i, :], PS[u][:, i, :], (a_cos, a_sin)[i % 2][:], ALU.mult)
                    ins.then_inc(S["a_parts"], 1)
            for t in range(T):
                w = P * (t + 1)
                for g, u in LANES:
                    pair = slice(2 * g, 2 * g + 2)
                    dve.wait_ge(S["a_scores"], by_lane(t, g, u))
                    ch.link(nc.vector.tensor_reduce(sm[u][:, 5, pair], PS[u][:, pair, 0:w], AX.X, ALU.max))
                    nc.vector.tensor_scalar(sm[u][:, 1 + t, pair], sm[u][:, 5, pair], -HDA ** -0.5, None, ALU.mult)\
                        .then_inc(S["a_max"], 1)
                for u in range(U):
                    dve.wait_ge(S["a_p_turned"], by_lane(t, 0, u))
                    nc.vector.tensor_copy(turned_heads(u, 0, t), turned_ps(u, 0, t)).then_inc(S["a_pT_dve"], 1)
                for g, u in LANES:
                    pair = slice(2 * g, 2 * g + 2)
                    dve.wait_ge(S["a_p"], by_lane(t, g, u))
                    ch.link(nc.vector.reciprocal(sm[u][:, 6, pair], sm[u][:, 1 + t, 4 + 2 * g:6 + 2 * g]))
                    dve.wait_ge(S["a_pv"], by_lane(t, g, u))
                    nc.vector.tensor_tensor(work[u][:, 5, P * t + 64 * g:P * t + 64 * (g + 1)].rearrange("p (h w) -> p h w", h=2),
                                            PS[u][:, 2 * g, 0:64].rearrange("p (h w) -> p h w", h=2),
                                            sm[u][:, 6, pair].unsqueeze(2).to_broadcast([P, 2, HDA]), ALU.mult)\
                        .then_inc(S["a_y"], 1)
            for u in range(U):
                dve.wait_ge(S["a_out"], nth(0, u))
                nc.vector.tensor_tensor(xh[u][:], xh[u][:], tok(PS[u][:, 1, :]), ALU.add).then_inc(S["a_x"], 1)
            dve.wait_ge(S["scattered"], 16 * 2 * T * U)
            rms_vector(dve, 1, lambda u: sent[u][:])

            def e2_logits(u):
                dve.wait_ge(S["e2_logits"], nth(0, u))
                ch.link(nc.vector.tensor_copy(lg[u][:, :, 0:E2], PS[u][:, 1, 0:T * E2].rearrange("p (t e) -> p t e", t=T)))

            route_vector(dve, ch, turn, E2, e2_logits, 1e-9)

        def attn_gpsimd(pool, ch):
            rstd_gpsimd(pool, 5)
            rms_gpsimd(pool, 0)
            for u in range(U):
                for half in range(2):
                    pool.wait_ge(S["a_parts"], 2 * u + half + 1)
                    first, second = work[u][:, 2 + 2 * half, :], work[u][:, 3 + 2 * half, :]
                    nc.gpsimd.tensor_tensor(first, first, second, ALU.add).then_inc(S["a_rotated"], 1)
            for u in range(U):
                pool.wait_ge(S["a_x"], nth(0, u))
                nc.gpsimd.tensor_tensor(x[u][:], x[u][:], xh[u][:], ALU.add).then_inc(S["e2_base"], 1)
            rms_gpsimd(pool, 1)

        def root_tensor(pe):

            def products(u):
                pe.wait_ge(S[f"adjT_in{u}"], 16)
                for t in range(T):
                    mm = nc.tensor.matmul(PS[u][:, 1, :], work[u][:, 0, cols(t)], adjT[u][:, t, :], start=(t == 0), stop=(t == T - 1))
                mm.then_inc(S["r_sum"], 1)

            turn_tensor(pe, 0, lambda u: tok(work[u][:, 0, :]), lambda u: pe.wait_ge(S["r_h"], nth(0, u)), products)
            for u in range(U):
                pe.wait_ge(S["chan"], nth(0, u))
                pe.wait_ge(S["r_sum_sb"], nth(0, u))
                for t in range(T):
                    nc.tensor.matmul(PS[u][:, 2, cols(t)], ones_h[0:PARTS, :], r_b, start=True, stop=False)
                    nc.tensor.matmul(PS[u][:, 2, cols(t)], work[u][:, 2, cols(t)], r_rel[:], start=False, stop=False)
                    mm = nc.tensor.matmul(PS[u][:, 2, cols(t)], work[u][:, 1, cols(t)], r_root[:], start=False, stop=True)
                mm.then_inc(S["r_out"], 1)

        def root_scalar(act):
            turn_scalar(act, 0, lambda u: work[u][:, 1, :])
            for u in range(U):
                act.wait_ge(S["r_sum"], nth(0, u))
                nc.scalar.activation(work[u][:, 2, :], PS[u][:, 1, :], ACT.Copy).then_inc(S["r_sum_sb"], 1)

        def root_vector(dve, ch, turn):
            recall_weights(dve, turn)
            recall_rows(dve, turn + 1)

            def combined(u):
                dve.wait_ge(S[f"x_in{u}"], 16)
                combine_vector(dve, ch, u, x[u], S["combined"])
                dve.wait_ge(S["combined"], nth(0, u))

            norm_vector(dve, ch, 0, x, xh, combined, True)
            h = [tok(work[u][:, 0, :]) for u in range(U)]
            norm_vector(dve, ch, 1, xh, h, lambda u: dve.wait_ge(S["normed"], nth(0, u)), True)
            for u in range(U):
                dve.wait_ge(S["normed"], nth(1, u))
                ch.link(nc.vector.tensor_tensor(h[u], h[u], r_gamma.unsqueeze(1).to_broadcast([P, T, P]), ALU.mult))
                nc.vector.tensor_tensor(h[u], h[u], r_beta.unsqueeze(1).to_broadcast([P, T, P]), ALU.add)\
                    .then_inc(S["r_h"], 1)

            def update(u):
                dve.wait_ge(S["r_out"], nth(0, u))
                dve.wait_ge(S["r_base"], nth(0, u))
                nc.vector.scalar_tensor_tensor(out=x[u][:], in0=tok(PS[u][:, 2, :]), scalar=0.0, in1=x[u][:],
                                               op0=ALU.max, op1=ALU.add).then_inc(S["x"], 1)
            return update

        def root_gpsimd(pool, ch):
            scatter_gpsimd(pool, (0,))
            rstd_gpsimd(pool, 0)
            rstd_gpsimd(pool, 1)
            for u in range(U):
                nc.gpsimd.tensor_tensor(x[u][:], x[u][:], xh[u][:], ALU.add).then_inc(S["r_base"], 1)
            scatter_gpsimd(pool, range(1, U))


        def top2_tensor(pe):

            def products(u):
                pe.wait_ge(S["chan"], nth(1, u))
                for t in range(T):
                    mm = nc.tensor.matmul(PS[u][:, 1, E3 * t:E3 * (t + 1)], xT[u][:, cols(t)], e3_gate[:], start=True, stop=True)
                mm.then_inc(S["e3_logits"], 1)

            turn_tensor(pe, 1, lambda u: sent[u], lambda u: pe.wait_ge(S["normed"], nth(2, u)), products)
            route_tensor(pe, E3)

        def top2_scalar(act):
            turn_scalar(act, 1, lambda u: xT[u][:])
            route_scalar(act, E3)

        def top2_vector(dve, ch, turn, ready):
            dve.wait_ge(S["scattered"], 16 * 2 * T * U)
            norm_vector(dve, ch, 2, x, sent, ready)

            def e3_logits(u):
                dve.wait_ge(S["e3_logits"], nth(0, u))
                ch.link(nc.vector.tensor_tensor(lg[u][:, :, 0:E3], PS[u][:, 1, 0:T * E3].rearrange("p (t e) -> p t e", t=T),
                                                e3_gb[:].unsqueeze(1).to_broadcast([P, T, E3]), ALU.add))

            route_vector(dve, ch, turn, E3, e3_logits, None)

        def top2_gpsimd(pool, ch):
            pool.wait_ge(S["combined"], nth(0, 0))
            gather_gpsimd(pool, E2, 0)
            rstd_gpsimd(pool, 2)
            for u in range(1, U):
                pool.wait_ge(S["combined"], nth(0, u))
                gather_gpsimd(pool, E2, u)

        SETS = 2
        last_x = [[x[u][:] for u in range(U)], [tok(work[u][:, 1, :]) for u in range(U)]]
        last_h = [[xh[u][:] for u in range(U)], [tok(work[u][:, 2, :]) for u in range(U)]]

        def last_vector(dve, ch, turn):
            recall_weights(dve, turn, SETS)
            recall_rows(dve, turn + 1, SETS)
            for s in range(SETS):

                def combined(u):
                    dve.wait_ge(S[f"h_in{U * s + u}"], 16)
                    combine_vector(dve, ch, u, last_h[s][u], S["combined"], s)
                    dve.wait_ge(S["combined"], nth(s, u))

                y = [tok(work[u][:, 3 * s, :]) for u in range(U)]
                norm_vector(dve, ch, s, last_h[s], y, combined, True)
                for u in range(U):
                    out_x = last_x[s][u]
                    dve.wait_ge(S["normed"], nth(s, u))
                    dve.wait_ge(S[f"x_in{U * s + u}"], 16)
                    nc.vector.tensor_tensor(out_x, out_x, e3_beta.unsqueeze(1).to_broadcast([P, T, P]), ALU.add)
                    ch.link(nc.vector.tensor_tensor(y[u], y[u], e3_gamma.unsqueeze(1).to_broadcast([P, T, P]), ALU.mult))
                    nc.vector.tensor_tensor(out_x, out_x, y[u], ALU.add).then_inc(S["x"], 1)

        def last_gpsimd(pool, ch):
            for s in range(SETS):
                rstd_gpsimd(pool, s)
                pool.wait_ge(S["combined"], nth(s, 0))
                gather_gpsimd(pool, E3, 0, s)
            for s in range(SETS):
                for u in range(1, U):
                    pool.wait_ge(S["combined"], nth(s, u))
                    gather_gpsimd(pool, E3, u, s)

        def table_phase(n, jobs):
            grid = slot(0, 0, SLOTS)[0:1, 0:jobs * n].rearrange("p (j e) -> p j e", j=jobs)
            count_j = work[1][0:1, 0, 0:jobs]
            job_e, base, dummy, read = (work[1][0:1, k, 0:jobs] for k in range(1, 5))
            tiles_e, upto, offset, step, ones = (work[1][:, 6, 16 * k:16 * k + n] for k in range(5))
            tiles_i = work[1][:, 7, 0:n].bitcast(I32)
            nodes = 2 * B * T
            row_in, shift = work[1][:, 11, 0:nodes], work[1][:, 12, 0:nodes]
            beyond = slot(0, 5, 4)[:, 0:nodes * n].rearrange("p (r e) -> p r e", r=nodes)
            row_flat = row_of[:, 0:B * T, :].rearrange("p t k -> p (t k)")
            with nc.Block() as block:
                @block.gpsimd
                def _(pool):
                    ch = Chain(pool, S["pool_own"])
                    scatter_gpsimd(pool)
                    nc.gpsimd.memset(work[1][:, 8, 0:P], 0.0)
                    nc.gpsimd.iota(count_j, [[1, jobs]], base=0, channel_multiplier=0,
                                   allow_small_or_imprecise_dtypes=True).then_inc(S["count_j"], 1)
                    ch.link(nc.gpsimd.iota(work[1][:, 9, 0:n], [[0, n]], base=0, channel_multiplier=1,
                                           allow_small_or_imprecise_dtypes=True))
                    ch.link(nc.gpsimd.tensor_tensor(work[1][:, 9, 0:n], work[1][:, 9, 0:n], place[:, 0:n], ALU.add))
                    ch.link(nc.gpsimd.tensor_copy(work[1][:, 10, 0:n].bitcast(I32), work[1][:, 9, 0:n]))
                    nc.gpsimd.dma_start(moe_in[n * REGION:n * REGION + P, :], work[1][:, 8, 0:P]).then_inc(S["scattered"], 16)
                    for e in range(n):
                        nc.gpsimd.indirect_dma_start(
                            out=moe_in, out_offset=bass.IndirectOffsetOnAxis(ap=work[1][:, 10, e:e + 1].bitcast(I32), axis=0),
                            in_=work[1][:, 8, 0:P], in_offset=None).then_inc(S["scattered"], 16)
                    pool.wait_ge(S["scattered"], 16 * (n + 1 + 2 * T * U))

                if n == E3:
                    @block.sync
                    def _(sp):
                        sp.dma_start(e3_w1, d["e3_w1"]).then_inc(S["weights_in"], 16)
                        sp.dma_start(e3_w2, d["e3_w2"]).then_inc(S["weights_in"], 16)
                        sp.wait_ge(S["weights_in"], 16 * 2)

                @block.vector
                def _(dve):
                    ch = Chain(dve, S["dve_own"])
                    tt, ts = nc.vector.tensor_tensor, nc.vector.tensor_scalar
                    first = region_of[:, 0:n]
                    wide = [1, jobs, n]
                    ch.link(tt(tiles_e, place[:, 0:n], first, ALU.subtract))
                    ch.link(ts(tiles_e, tiles_e, float(P - 1), None, ALU.add))
                    ch.link(nc.vector.tensor_copy(tiles_i, tiles_e))
                    ch.link(ts(tiles_i, tiles_i, 7, None, ALU.logical_shift_right))
                    ch.link(nc.vector.tensor_copy(tiles_e, tiles_i))
                    ch.link(nc.vector.memset(ones, 1.0))
                    ch.link(nc.vector.tensor_tensor_scan(upto, ones, tiles_e, 0.0, ALU.mult, ALU.add))
                    ch.link(tt(offset, tiles_e, upto, ALU.subtract))
                    ch.link(nc.vector.scalar_tensor_tensor(out=offset, in0=offset, scalar=float(P), in1=first,
                                                           op0=ALU.mult, op1=ALU.add))
                    nc.vector.tensor_copy(row_in, row_flat)
                    nc.vector.tensor_copy(step[:, 0:1], offset[:, 0:1])
                    ch.link(tt(step[:, 1:n], offset[:, 1:n], offset[:, 0:n - 1], ALU.subtract))
                    by_node = [P, nodes, n]
                    ch.link(tt(beyond, row_in.unsqueeze(2).to_broadcast(by_node), first.unsqueeze(1).to_broadcast(by_node),
                               ALU.is_ge))
                    ch.link(tt(beyond, beyond, step.unsqueeze(1).to_broadcast(by_node), ALU.mult))
                    ch.link(nc.vector.tensor_reduce(shift, beyond, AX.X, ALU.add))
                    ch.link(tt(row_in, row_in, shift, ALU.subtract))
                    nc.vector.tensor_copy(row_flat, row_in)
                    dve.wait_ge(S["count_j"], 1)
                    ch.link(tt(grid, count_j.unsqueeze(2).to_broadcast(wide), upto[0:1].unsqueeze(1).to_broadcast(wide), ALU.is_ge))
                    ch.link(nc.vector.tensor_reduce(job_e, grid, AX.X, ALU.add))
                    ch.link(tt(grid, job_e.unsqueeze(2).to_broadcast(wide), iota32[0:1, 0:n].unsqueeze(1).to_broadcast(wide),
                               ALU.is_equal))
                    ch.link(tt(grid, grid, offset[0:1].unsqueeze(1).to_broadcast(wide), ALU.mult))
                    ch.link(nc.vector.tensor_reduce(base, grid, AX.X, ALU.add))
                    ch.link(nc.vector.scalar_tensor_tensor(out=base, in0=count_j, scalar=float(P), in1=base,
                                                           op0=ALU.mult, op1=ALU.add))
                    ch.link(ts(dummy, job_e, float(n), None, ALU.is_ge))
                    ch.link(ts(read, base, -1.0, float(n * REGION), ALU.mult, ALU.add))
                    ch.link(tt(read, read, dummy, ALU.mult))
                    ch.link(tt(read, read, base, ALU.add))
                    by_turn = [ap.rearrange("p (n j) -> p n j", j=tiles_per_turn(jobs)) for ap in (job_e, read)]
                    nc.vector.tensor_copy(job_table(jobs)[:, 1, :, 0:tiles_per_turn(jobs)], by_turn[1])
                    ch.link(ts(job_e, job_e, float(n - 1), None, ALU.min))
                    nc.vector.tensor_copy(job_table(jobs)[:, 0, :, 0:tiles_per_turn(jobs)], by_turn[0])
            clear()
            with nc.Block() as block:
                @block.vector
                def _(dve):
                    nc.vector.tensor_copy(place[:], region_of[:])
            clear()

        def rows_at(j, first, more):
            s, c = (j // 2) // 4, (j // 2) % 4
            return work[j % 2][:, first + s, cols(c)] if s < 3 else adjT[j % 2][:, more + s - 3, cols(c)]

        def rows_in_at(j):
            return rows_at(j, 0, 0)

        def rows_out_at(j):
            return rows_at(j, 12, 2)

        def experts_phase(n, jobs, hidden, chunks, up, down, finish_x, finish_up, finish_hT, bias):
            group = tiles_per_turn(jobs)
            table = job_table(jobs)

            def loaded(eng, turn, k, j, top):
                m = min(QUAD, group - j)
                row = table[0:1, k, bass.ds(turn, 1), j:j + m].rearrange("p o j -> p (o j)")
                _, values = nc.values_load_multi_w_load_instructions(row, engines=[eng.engine], min_val=0, max_val=top,
                    skip_runtime_bounds_check_because="the table holds experts and rows of the regions")
                return {j + i: v for i, v in enumerate(values)}

            with nc.Fori(0, jobs // group) as turn:
                with nc.Block() as block:
                    @block.sync
                    def _(sp):
                        for j in range(group):
                            if j % QUAD == 0:
                                first_row = loaded(sp, turn, 1, j, n * REGION)
                            sp.dma_start(rows_in_at(j), moe_in[bass.ds(first_row[j], P), :]).then_inc(S[f"rows_in{j}"], 16)

                    @block.tensor
                    def _(pe):
                        expert = {}
                        for s in range(group + 3):
                            j = s
                            if j < group:
                                if j % QUAD == 0:
                                    expert.update(loaded(pe, turn, 0, j, n - 1))
                                pe.wait_ge(S[f"rows_in{j}"], 16)
                                if j >= 2:
                                    pe.wait_ge(S["t_x_chan"], j - 1)
                                nc.tensor.transpose(PS[j % 2][:, 0, 0:P], rows_in_at(j), ident[:]).then_inc(S["t_x"], 1)
                            j = s - 1
                            if 0 <= j < group:
                                pe.wait_ge(S["t_x_chan"], j + 1)
                                if j >= 2:
                                    pe.wait_ge(S["t_hidden"], j - 1)
                                for b, w in enumerate(up):
                                    mm = nc.tensor.matmul(PS[j % 2][:, 1 + b, 0:hidden], work[j % 2][:, 3, cols((j // 2) % 2)],
                                                          w(expert[j]), start=True, stop=True)
                                mm.then_inc(S["t_up"], 1)
                            j = s - 2
                            if 0 <= j < group:
                                pe.wait_ge(S["t_hidden"], j + 1)
                                if j >= 2:
                                    pe.wait_ge(S["t_out_sb"], j - 1)
                                for f, w in enumerate(chunks):
                                    mm = nc.tensor.transpose(PS[j % 2][0:w, 3, cols(f)],
                                                             work[j % 2][:, 8 + (j // 2) % 2, P * f:P * f + w], ident[:])
                                mm.then_inc(S["t_turned"], 1)
                            j = s - 3
                            if 0 <= j < group:
                                pe.wait_ge(S["t_hT"], j + 1)
                                if bias is not None:
                                    nc.tensor.matmul(PS[j % 2][:, 3, 3 * P:4 * P], ones_h[0:PARTS, :], bias(expert[j]), start=True, stop=False)
                                for f, w in enumerate(chunks):
                                    mm = nc.tensor.matmul(PS[j % 2][:, 3, 3 * P:4 * P], work[j % 2][0:w, 10 + (j // 2) % 2, cols(f)],
                                                          down(expert[j], f, w), start=(f == 0 and bias is None),
                                                          stop=(f == len(chunks) - 1))
                                mm.then_inc(S["t_out"], 1)

                    @block.scalar
                    def _(act):
                        expert = {}
                        for s in range(group + 3):
                            if s < group:
                                j = s
                                act.wait_ge(S["t_x"], j + 1)
                                if j >= 4:
                                    act.wait_ge(S["t_up"], j - 3)
                                finish_x(work[j % 2][:, 3, cols((j // 2) % 2)], PS[j % 2][:, 0, 0:P]).then_inc(S["t_x_chan"], 1)
                            j = s - 1
                            if 0 <= j < group:
                                act.wait_ge(S["t_up"], j + 1)
                                finish_up[0](act, j)
                            j = s - 2
                            if 0 <= j < group:
                                act.wait_ge(S["t_turned"], j + 1)
                                if j >= 4:
                                    act.wait_ge(S["t_out"], j - 3)
                                if bias is not None and j % QUAD == 0:
                                    expert.update(loaded(act, turn, 0, j, n - 1))
                                finish_hT(act, expert, j)
                            j = s - 3
                            if 0 <= j < group:
                                act.wait_ge(S["t_out_sb"], j + 1)
                                act.dma_start(moe_out[bass.ds(turn * (group * P) + j * P, P), :], rows_out_at(j))\
                                    .then_inc(S["out_written"], 16)
                        act.wait_ge(S["out_written"], 16 * group)

                    @block.vector
                    def _(dve):
                        ch = Chain(dve, S["dve_own"])
                        for s in range(group + 2):
                            j = s
                            if j < group:
                                finish_up[1](dve, ch, j)
                            j = s - 2
                            if j >= 0:
                                dve.wait_ge(S["t_out"], j + 1)
                                nc.vector.tensor_copy(rows_out_at(j), PS[j % 2][:, 3, 3 * P:4 * P]).then_inc(S["t_out_sb"], 1)
                clear()

        def swiglu_experts():
            def tanh(act, j):
                if j >= 4:
                    act.wait_ge(S["t_hidden"], j - 3)
                nc.scalar.activation(work[j % 2][:, 4 + (j // 2) % 2, 0:HID], PS[j % 2][:, 1, 0:HID], ACT.Tanh, scale=0.5)\
                    .then_inc(S["t_tanh"], 1)

            def silu_up(dve, ch, j):
                v = (j // 2) % 2
                gate = work[j % 2][:, 6 + v, 0:HID]
                dve.wait_ge(S["t_tanh"], j + 1)
                ch.link(nc.vector.scalar_tensor_tensor(out=gate, in0=work[j % 2][:, 4 + v, 0:HID], scalar=1.0,
                                                       in1=PS[j % 2][:, 1, 0:HID], op0=ALU.add, op1=ALU.mult))
                if j >= 4:
                    dve.wait_ge(S["t_turned"], j - 3)
                nc.vector.scalar_tensor_tensor(out=work[j % 2][:, 8 + v, 0:HID], in0=gate, scalar=0.5,
                                               in1=PS[j % 2][:, 2, 0:HID], op0=ALU.mult, op1=ALU.mult)\
                    .then_inc(S["t_hidden"], 1)

            def hT(act, e, j):
                v = (j // 2) % 2
                nc.scalar.activation(work[j % 2][:, 10 + v, 0:2 * P], PS[j % 2][:, 3, 0:2 * P], ACT.Copy)
                nc.scalar.activation(work[j % 2][0:FW[2], 10 + v, 2 * P:3 * P], PS[j % 2][0:FW[2], 3, 2 * P:3 * P], ACT.Copy)\
                    .then_inc(S["t_hT"], 1)

            experts_phase(
                E2, TILES(E2), HID, FW,
                [lambda e: e2_w1[:, bass.ds(e, 1), :].rearrange("c o m -> c (o m)"),
                 lambda e: e2_w3[:, bass.ds(e, 1), :].rearrange("c o m -> c (o m)")],
                lambda e, f, w: e2_w2[0:w, bass.ds(e, 1), f, :].rearrange("m o c -> m (o c)"),
                lambda dst, src: nc.scalar.activation(dst, src, ACT.Copy, scale=a_ln2[:]),
                (tanh, silu_up), hT, None)

        def relu_experts():
            def nothing(act, j):
                pass

            def hidden(dve, ch, j):
                dve.wait_ge(S["t_up"], j + 1)
                if j >= 4:
                    dve.wait_ge(S["t_turned"], j - 3)
                nc.vector.tensor_copy(work[j % 2][:, 8 + (j // 2) % 2, 0:2 * P], PS[j % 2][:, 1, 0:2 * P])\
                    .then_inc(S["t_hidden"], 1)

            def hT(act, e, j):
                for f in range(2):
                    ins = nc.scalar.activation(work[j % 2][:, 10 + (j // 2) % 2, cols(f)], PS[j % 2][:, 3, cols(f)], ACT.Relu,
                                               bias=e3_b1[:, bass.ds(e[j], 1), f])
                ins.then_inc(S["t_hT"], 1)

            experts_phase(
                E3, TILES(E3), 2 * P, [P, P],
                [lambda e: e3_w1[:, bass.ds(e, 1), :, :].rearrange("c o f m -> c (o f m)")],
                lambda e, f, w: e3_w2[:, bass.ds(e, 1), f, :].rearrange("m o c -> m (o c)"),
                lambda dst, src: nc.scalar.activation(dst, src, ACT.Copy),
                (nothing, hidden), hT, lambda e: e3_b2[:, bass.ds(e, 1), :].rearrange("p o c -> p (o c)"))

        engines = {e.engine for e in (nc.tensor, nc.vector, nc.scalar, nc.gpsimd, nc.sync)}

        def clear():
            nc.gpsimd.dma_reset(S.numbers())
            nc.multi_engine_barrier(engines, sems_to_clear=S.numbers())

        def graph(t, turn, u):
            return t[bass.ds(U * turn + u, 1)].rearrange("o (t p) c -> p (o t) c", p=P)

        def broadcast_rows(*pairs):
            with nc.Block() as block:
                @block.sync
                def _(sp):
                    for dst, src in pairs:
                        sp.dma_start(dst, src.partition_broadcast(P)).then_inc(S["weights_in"], 16)
                    sp.wait_ge(S["weights_in"], 16 * len(pairs))

        def first_phase():
            with nc.Block() as block:
                @block.sync
                def _(sp):
                    for u in range(U):
                        sp.dma_start(x[u][:], graph(d["x"], 0, u)).then_inc(S["first_in"], 16)
                        sp.dma_start(adjT[u][:], graph(d["adj"], 0, u)).then_inc(S["first_in"], 16)
                    sp.wait_ge(S["first_in"], 32 * U)
            clear()
            with nc.Fori(0, B // U) as turn:
                with nc.Block() as block:
                    @block.sync
                    def _(sp):
                        for u in range(U):
                            sp.wait_ge(S["gat_max"], by_graph(u, T - 1))
                            sp.dma_start(adjT[u][:], graph(d["adj_t"], turn, u)).then_inc(S[f"adjT_in{u}"], 16)
                        for u in range(U):
                            sp.wait_ge(S["g_affinity"], nth(T - 1, u))
                            sp.dma_start(adjT[u][:], graph(d["adj"], turn + 1, u)).then_inc(S["next_in"], 16)
                        for u in range(U):
                            sp.wait_ge(S["e2_base"], nth(0, u))
                            sp.dma_start(graph(carry_x, turn, u), x[u][:]).then_inc(S[f"stored{u}"], 16)
                        for u in range(U):
                            sp.wait_ge(S[f"stored{u}"], 16)
                            sp.dma_start(x[u][:], graph(d["x"], turn + 1, u)).then_inc(S["next_in"], 16)
                        sp.wait_ge(S["next_in"], 32 * U)

                    @block.tensor
                    def _(pe):
                        gat_tensor(pe)
                        mamba_tensor(pe)
                        gcn_tensor(pe)
                        top1_tensor(pe)
                        gru_tensor(pe)
                        attn_tensor(pe)

                    @block.scalar
                    def _(act):
                        gat_scalar(act)
                        mamba_scalar(act)
                        gcn_scalar(act)
                        top1_scalar(act)
                        gru_scalar(act)
                        attn_scalar(act)

                    @block.vector
                    def _(dve):
                        ch = Chain(dve, S["dve_own"])
                        x_0 = gat_vector(dve, ch)
                        x_1 = mamba_vector(dve, ch, updated(dve, 0, x_0))
                        x_2 = gcn_vector(dve, ch, updated(dve, 1, x_1))
                        x_3 = top1_vector(dve, ch, updated(dve, 2, x_2))
                        x_4 = gru_vector(dve, ch, updated(dve, 3, x_3))
                        attn_vector(dve, ch, turn, updated(dve, 4, x_4))

                    @block.gpsimd
                    def _(pool):
                        ch = Chain(pool, S["pool_own"])
                        gat_gpsimd(pool, ch)
                        mamba_gpsimd(pool, ch)
                        gcn_gpsimd(pool, ch)
                        top1_gpsimd(pool, ch)
                        scatter_gpsimd(pool)
                        gru_gpsimd(pool, ch)
                        attn_gpsimd(pool, ch)
                clear()

        def second_phase():
            broadcast_rows((r_gamma, d["r_gamma"]), (r_beta, d["r_beta"]))
            first_gather(E2)
            with nc.Fori(0, B // U) as turn:
                with nc.Block() as block:
                    @block.sync
                    def _(sp):
                        for u in range(U):
                            sp.dma_start(x[u][:], graph(carry_x, turn, u)).then_inc(S[f"x_in{u}"], 16)
                            sp.dma_start(adjT[u][:], graph(d["adj_t"], turn, u)).then_inc(S[f"adjT_in{u}"], 16)
                        for u in range(U):
                            sp.wait_ge(S[f"x_in{u}"], 16)
                            sp.wait_ge(S["x"], nth(0, u))
                            sp.dma_start(graph(carry_x, turn, u), x[u][:]).then_inc(S["out_written"], 16)
                            sp.wait_ge(S["normed"], nth(2, u))
                            sp.dma_start(graph(carry_h, turn, u), sent[u][:]).then_inc(S["out_written"], 16)
                        sp.wait_ge(S["out_written"], 32 * U)

                    @block.tensor
                    def _(pe):
                        root_tensor(pe)
                        top2_tensor(pe)

                    @block.scalar
                    def _(act):
                        root_scalar(act)
                        top2_scalar(act)

                    @block.vector
                    def _(dve):
                        ch = Chain(dve, S["dve_own"])
                        x_6 = root_vector(dve, ch, turn)
                        top2_vector(dve, ch, turn, updated(dve, 0, x_6))

                    @block.gpsimd
                    def _(pool):
                        ch = Chain(pool, S["pool_own"])
                        root_gpsimd(pool, ch)
                        top2_gpsimd(pool, ch)
                        for u in range(U):
                            pool.wait_ge(S[f"gathered{u}"], 16 * 2 * T)
                clear()

        def last_phase():
            broadcast_rows((e3_gamma, d["e3_gamma"]), (e3_beta, d["e3_beta"]))
            first_gather(E3, SETS)
            with nc.Fori(0, B // (SETS * U)) as turn:
                with nc.Block() as block:
                    @block.sync
                    def _(sp):
                        for g in range(SETS * U):
                            sp.dma_start(last_h[g // U][g % U], graph(carry_h, SETS * turn, g)).then_inc(S[f"h_in{g}"], 16)
                            sp.dma_start(last_x[g // U][g % U], graph(carry_x, SETS * turn, g)).then_inc(S[f"x_in{g}"], 16)
                        for g in range(SETS * U):
                            sp.wait_ge(S["x"], g + 1)
                            sp.dma_start(graph(out, SETS * turn, g), last_x[g // U][g % U]).then_inc(S["out_written"], 16)
                        sp.wait_ge(S["out_written"], 16 * SETS * U)

                    @block.vector
                    def _(dve):
                        last_vector(dve, Chain(dve, S["dve_own"]), turn)

                    @block.gpsimd
                    def _(pool):
                        last_gpsimd(pool, None)
                        for u in range(U):
                            pool.wait_ge(S[f"gathered{u}"], 16 * 2 * T * SETS)
                clear()

        clear()
        S.release()
        for phase in (first_phase, lambda: table_phase(E2, TILES(E2)), swiglu_experts, second_phase,
                      lambda: table_phase(E3, TILES(E3)), relu_experts, last_phase):
            phase()
            S.release()


def kernel(**inputs):
    import numpy as np
    import concourse.bacc as bacc
    from concourse.bass_utils import run_bass_kernel_spmd

    g = {k: np.asarray(v) for k, v in inputs.items()}

    def experts_out(w):
        return w.transpose(2, 0, 1)

    def rows(w):
        return w.reshape(-1, P, *w.shape[1:]).swapaxes(0, 1)

    head = np.arange(HDA)
    swap = (head + HDA // 2) % HDA
    q_cols = np.arange(NHA * HDA)
    q_swap = (q_cols // HDA) * HDA + swap[q_cols % HDA]
    k_cols = (q_cols // HDA // 2) * HDA + q_cols % HDA
    k_swap = (q_cols // HDA // 2) * HDA + swap[q_cols % HDA]
    wq, wk = g["L2_ffn_wq"], g["L2_ffn_wk"]
    a_qk = np.concatenate([wq[q_cols].T, wq[q_swap].T, wk[k_cols].T, wk[k_swap].T], axis=1).reshape(P, 4, P)

    inv_freq = 1.0 / 10000.0 ** (np.arange(0, HDA, 2, dtype=np.float32) / HDA)
    freqs = np.outer(np.arange(N, dtype=np.float32), inv_freq)
    emb = np.concatenate([freqs, freqs], axis=-1)
    sign = np.where(head < HDA // 2, -1.0, 1.0).astype(np.float32)
    a_cos = np.tile(np.cos(emb).T, (NHA, 1)).astype(np.float32)
    a_sin = np.tile((np.sin(emb) * sign).T, (NHA, 1)).astype(np.float32)

    def padded(a):
        return np.concatenate([a, np.zeros((U, *a.shape[1:]), a.dtype)])

    arrays = {
        "x": padded(g["x"]), "adj": padded(g["adj"]), "adj_t": g["adj"].transpose(0, 2, 1),
        "gat_w": g["L0_gnn_W"], "gat_wt": g["L0_gnn_W"].T, "gat_a": g["L0_gnn_a"].reshape(2, P).T,
        "m_in": g["L0_ffn_W_in"], "m_conv_w": rows(g["L0_ffn_conv_w"]), "m_conv_b": rows(g["L0_ffn_conv_b"]),
        "m_dt_bias": g["L0_ffn_dt_bias"], "m_a_log": g["L0_ffn_A_log"], "m_d": g["L0_ffn_D"],
        "m_norm_w": rows(g["L0_ffn_norm_w"]), "m_out_t": g["L0_ffn_W_out"].T, "m_lin": g["L0_ffn_W_lin"],
        "m_b_lin": g["L0_ffn_b_lin"],
        "gcn_w": g["L1_gnn_weight"], "gcn_b": g["L1_gnn_bias"],
        "e1_router_t": g["L1_ffn_router_w"].T, "e1_rb": g["L1_ffn_router_b"],
        "e1_w1": g["L1_ffn_W1"].transpose(1, 0, 2).reshape(P, 8, P), "e1_b1": rows(g["L1_ffn_b1"].reshape(-1)),
        "e1_w2": rows(g["L1_ffn_W2"].reshape(-1, P)), "e1_b2": g["L1_ffn_b2"],
        "g_se_t": g["L2_gnn_w_se"].T, "g_se_b": g["L2_gnn_b_se"][:, None],
        "g_c1_t": g["L2_gnn_conv1_w"][:, :, 0].T, "g_c2_t": g["L2_gnn_conv2_w"].transpose(1, 2, 0),
        "g_msg_t": g["L2_gnn_w_msg"].T, "g_msg_b": g["L2_gnn_b_msg"],
        "g_ih_t": rows(g["L2_gnn_w_ih"].T), "g_hh_t": g["L2_gnn_w_hh"].T,
        "g_b_ih": rows(g["L2_gnn_b_ih"]), "g_b_hh": rows(g["L2_gnn_b_hh"]),
        "a_ln1": g["L2_ffn_ln1_w"][:, None], "a_ln2": g["L2_ffn_ln2_w"][:, None], "a_qk": a_qk,
        "a_v_t": g["L2_ffn_wv"].T, "a_o_t": g["L2_ffn_wo"].T, "a_cos": a_cos, "a_sin": a_sin,
        "e2_router_t": g["L2_ffn_router_w"].T, "e2_w1_t": experts_out(g["L2_ffn_w1"]),
        "e2_w3_t": experts_out(g["L2_ffn_w3"]), "e2_w2_t": experts_out(g["L2_ffn_w2"]),
        "r_rel": g["L3_gnn_W_rel"], "r_root": g["L3_gnn_W_root"], "r_b": g["L3_gnn_b_rel"],
        "r_gamma": g["L3_gnn_ln_gamma"], "r_beta": g["L3_gnn_ln_beta"],
        "e3_gate": g["L3_ffn_gate_w"], "e3_gb": g["L3_ffn_gate_b"], "e3_w1": g["L3_ffn_w1"].transpose(1, 0, 2).reshape(P, E3, 2, P),
        "e3_b1": g["L3_ffn_b1"].reshape(E3, 2, P).transpose(2, 0, 1),
        "e3_w2": g["L3_ffn_w2"].reshape(E3, 2, P, P).transpose(2, 0, 1, 3), "e3_b2": g["L3_ffn_b2"],
        "e3_gamma": g["L3_ffn_gamma"], "e3_beta": g["L3_ffn_beta"],
    }
    arrays["g_bn"] = np.stack([g[f"L2_gnn_bn{n}_{k}"] for n in (1, 2) for k in "gbmv"], axis=1)

    nc = bacc.Bacc("TRN2", target_bir_lowering=False, num_devices=1)
    feed, d = {}, {}
    for name, a in arrays.items():
        a = np.ascontiguousarray(a)
        feed[f"in_{name}_dram"] = a
        d[name] = nc.dram_tensor(f"in_{name}_dram", a.shape, mybir.dt.from_np(a.dtype), kind="ExternalInput").ap()
    out = nc.dram_tensor("out_0_dram", g["x"].shape, F32, kind="ExternalOutput").ap()
    build_network(nc, d, out)
    return run_bass_kernel_spmd(nc, [feed], core_ids=[0]).results[0]["out_0_dram"]
```
